# Optimizing a Trainium2 kernel written in Bass

```python
import numpy as np
import jax
import jax.numpy as jnp

def _softmax(x, axis=-1):
    return jax.nn.softmax(x, axis=axis)

def _gelu(x):
    return jax.nn.gelu(x, approximate=True)

def _silu(x):
    return jax.nn.silu(x)

def _sigmoid(x):
    return jax.nn.sigmoid(x)

def _layernorm(x, axis=-1, eps=1e-05):
    m = jnp.mean(x, axis=axis, keepdims=True)
    v = jnp.var(x, axis=axis, keepdims=True)
    return (x - m) / jnp.sqrt(v + eps)

def _scatter_add(tgt, idx, src, axis=0):
    return tgt.at[idx].add(src)

def _segment_sum(src, seg, n):
    return jax.ops.segment_sum(src, seg, n)
kernel_name = 'mk_gnn_ffn_d1_gnn_r8_d0979a'

def setup_inputs(seed: int=0):
    np.random.seed(seed)
    _w = jnp.asarray

    def _rec_inputs():
        import jax
        import jax.numpy as jnp
        _gk = jax.random.key(seed)
        x = -8.776e-05 + 1 * jax.random.normal(jax.random.fold_in(_gk, 1), (1250, 512), jnp.float32)
        _s = jax.random.randint(jax.random.fold_in(_gk, 2), (20000,), 0, 1250, jnp.int32)
        _d = jax.random.randint(jax.random.fold_in(_gk, 3), (20000,), 0, 1250, jnp.int32)
        _loop = jnp.arange(1250, dtype=jnp.int32)
        src = jnp.concatenate([_s, _d, _loop])
        dst = jnp.concatenate([_d, _s, _loop])
        _o = jnp.argsort(dst, stable=True)
        src = src[_o]
        dst = dst[_o]
        return (x, src, dst)
    x, src, dst = _rec_inputs()

    def _L0_gnn_setup():
        import jax, jax.numpy as jnp
        import numpy as np
        N_NODES = 1250
        D_IN = 512
        D_HID = 512
        D_OUT = 512
        N_EDGES = 20000

        def sage_conv(x, edge_index, W_l, b_l, W_r):
            src, dst = (edge_index[0], edge_index[1])
            msgs = x[src]
            agg = jax.ops.segment_sum(msgs, dst, num_segments=x.shape[0])
            cnt = jax.ops.segment_sum(jnp.ones((msgs.shape[0],), x.dtype), dst, num_segments=x.shape[0])
            agg = agg / jnp.maximum(cnt, 1.0)[:, None]
            return agg @ W_l.T + b_l + x @ W_r.T
        key = jax.random.key(seed)
        ks = jax.random.split(key, 8)
        s = lambda d: 1.0 / np.sqrt(d)
        x = jax.random.normal(ks[0], (N_NODES, D_IN), dtype=jnp.float32)
        edge_index = jax.random.randint(ks[1], (2, N_EDGES), 0, N_NODES, dtype=jnp.int64)
        W1_l = jax.random.uniform(ks[2], (D_HID, D_IN), jnp.float32, -s(D_IN), s(D_IN))
        b1 = jax.random.uniform(ks[3], (D_HID,), jnp.float32, -s(D_IN), s(D_IN))
        W1_r = jax.random.uniform(ks[4], (D_HID, D_IN), jnp.float32, -s(D_IN), s(D_IN))
        W2_l = jax.random.uniform(ks[5], (D_OUT, D_HID), jnp.float32, -s(D_HID), s(D_HID))
        b2 = jax.random.uniform(ks[6], (D_OUT,), jnp.float32, -s(D_HID), s(D_HID))
        W2_r = jax.random.uniform(ks[7], (D_OUT, D_HID), jnp.float32, -s(D_HID), s(D_HID))
        return {'x': x, 'edge_index': edge_index, 'W1_l': W1_l, 'b1': b1, 'W1_r': W1_r, 'W2_l': W2_l, 'b2': b2, 'W2_r': W2_r}
    _L0_gnn_all = _L0_gnn_setup()
    _L0_gnn_in = {k: v for k, v in _L0_gnn_all.items() if k in ('W1_l', 'b1', 'W1_r', 'W2_l', 'b2', 'W2_r')}
    del _L0_gnn_all

    def _L0_ffn_setup():
        import jax, jax.numpy as jnp
        import numpy as np
        D = 512
        H = 8
        K = 4
        HD = D // H

        def _ln(x, w, b, eps=1e-05):
            m = x.mean(-1, keepdims=True)
            v = ((x - m) ** 2).mean(-1, keepdims=True)
            return (x - m) / jnp.sqrt(v + eps) * w + b

        def _spatial_experts(xn, idx, in_w, in_b, out_w, out_b):
            W = in_w[idx]
            qkv = jnp.einsum('btd,bed->bte', xn, W) + in_b[idx][:, None, :]
            q, k, v = jnp.split(qkv, 3, axis=-1)
            B, T, _ = xn.shape
            q = q.reshape(B, T, H, HD) * HD ** (-0.5)
            k = k.reshape(B, T, H, HD)
            v = v.reshape(B, T, H, HD)
            att = jax.nn.softmax(jnp.einsum('bthd,bshd->bhts', q, k), axis=-1)
            o = jnp.einsum('bhts,bshd->bthd', att, v).reshape(B, T, D)
            return jnp.einsum('btd,bod->bto', o, out_w[idx]) + out_b[idx][:, None, :]

        def _temporal_experts(xt, idx, qw, qb, kw, kb, vw, vb, pw, pb):
            B, T, _ = xt.shape
            q = (jnp.einsum('btd,bod->bto', xt, qw[idx]) + qb[idx][:, None, :]).reshape(B, T, H, HD)
            k = (jnp.einsum('btd,bod->bto', xt, kw[idx]) + kb[idx][:, None, :]).reshape(B, T, H, HD)
            v = (jnp.einsum('btd,bod->bto', xt, vw[idx]) + vb[idx][:, None, :]).reshape(B, T, H, HD)
            logits = jnp.einsum('bthd,bshd->bhts', q, k) * HD ** (-0.5)
            causal = jnp.tril(jnp.ones((T, T), dtype=bool))
            logits = jnp.where(causal, logits, -jnp.inf)
            att = jax.nn.softmax(logits, axis=-1)
            o = jnp.einsum('bhts,bshd->bthd', att, v).reshape(B, T, D)
            o = jnp.einsum('btd,bod->bto', o, pw[idx]) + pb[idx][:, None, :]
            return xt + o

        def _cross_mha(q_in, kv_in, in_w, in_b, out_w, out_b):
            B, T, _ = q_in.shape
            S = kv_in.shape[1]
            Wq, Wk, Wv = (in_w[:D], in_w[D:2 * D], in_w[2 * D:])
            bq, bk, bv = (in_b[:D], in_b[D:2 * D], in_b[2 * D:])
            q = (q_in @ Wq.T + bq).reshape(B, T, H, HD) * HD ** (-0.5)
            k = (kv_in @ Wk.T + bk).reshape(B, S, H, HD)
            v = (kv_in @ Wv.T + bv).reshape(B, S, H, HD)
            att = jax.nn.softmax(jnp.einsum('bthd,bshd->bhts', q, k), axis=-1)
            o = jnp.einsum('bhts,bshd->bthd', att, v).reshape(B, T, D)
            return o @ out_w.T + out_b
        key = jax.random.key(seed)
        ks = iter(jax.random.split(key, 40))
        B, T = (256, 64)
        p = lambda *shape: jax.random.normal(next(ks), shape, dtype=jnp.float32) * 0.02
        inp = {'x': jax.random.normal(next(ks), (B, T, D), dtype=jnp.float32), 'router_w1': p(128, D), 'router_b1': jnp.zeros((128,), jnp.float32), 'router_w2': p(2 * K, 128), 'router_b2': jnp.zeros((2 * K,), jnp.float32), 'norm_s_w': jnp.ones((D,), jnp.float32), 'norm_s_b': jnp.zeros((D,), jnp.float32), 'norm_t_w': jnp.ones((D,), jnp.float32), 'norm_t_b': jnp.zeros((D,), jnp.float32), 'sp_in_w': p(K, 3 * D, D), 'sp_in_b': jnp.zeros((K, 3 * D), jnp.float32), 'sp_out_w': p(K, D, D), 'sp_out_b': jnp.zeros((K, D), jnp.float32), 'tq_w': p(K, D, D), 'tq_b': jnp.zeros((K, D), jnp.float32), 'tk_w': p(K, D, D), 'tk_b': jnp.zeros((K, D), jnp.float32), 'tv_w': p(K, D, D), 'tv_b': jnp.zeros((K, D), jnp.float32), 'tp_w': p(K, D, D), 'tp_b': jnp.zeros((K, D), jnp.float32), 'cross_in_w': p(3 * D, D), 'cross_in_b': jnp.zeros((3 * D,), jnp.float32), 'cross_out_w': p(D, D), 'cross_out_b': jnp.zeros((D,), jnp.float32), 'norm_mlp_w': jnp.ones((D,), jnp.float32), 'norm_mlp_b': jnp.zeros((D,), jnp.float32), 'mlp_w1': p(4 * D, D), 'mlp_b1': jnp.zeros((4 * D,), jnp.float32), 'mlp_w2': p(D, 4 * D), 'mlp_b2': jnp.zeros((D,), jnp.float32)}
        return inp
    _L0_ffn_all = _L0_ffn_setup()
    _L0_ffn_in = {k: v for k, v in _L0_ffn_all.items() if k in ('router_w1', 'router_b1', 'router_w2', 'router_b2', 'norm_s_w', 'norm_s_b', 'norm_t_w', 'norm_t_b', 'sp_in_w', 'sp_in_b', 'sp_out_w', 'sp_out_b', 'tq_w', 'tq_b', 'tk_w', 'tk_b', 'tv_w', 'tv_b', 'tp_w', 'tp_b', 'cross_in_w', 'cross_in_b', 'cross_out_w', 'cross_out_b', 'norm_mlp_w', 'norm_mlp_b', 'mlp_w1', 'mlp_b1', 'mlp_w2', 'mlp_b2')}
    del _L0_ffn_all
    return {'x': x, 'src': src, 'dst': dst, 'L0_gnn_W1_l': _L0_gnn_in['W1_l'], 'L0_gnn_b1': _L0_gnn_in['b1'], 'L0_gnn_W1_r': _L0_gnn_in['W1_r'], 'L0_gnn_W2_l': _L0_gnn_in['W2_l'], 'L0_gnn_b2': _L0_gnn_in['b2'], 'L0_gnn_W2_r': _L0_gnn_in['W2_r'], 'L0_ffn_router_w1': _L0_ffn_in['router_w1'], 'L0_ffn_router_b1': _L0_ffn_in['router_b1'], 'L0_ffn_router_w2': _L0_ffn_in['router_w2'], 'L0_ffn_router_b2': _L0_ffn_in['router_b2'], 'L0_ffn_norm_s_w': _L0_ffn_in['norm_s_w'], 'L0_ffn_norm_s_b': _L0_ffn_in['norm_s_b'], 'L0_ffn_norm_t_w': _L0_ffn_in['norm_t_w'], 'L0_ffn_norm_t_b': _L0_ffn_in['norm_t_b'], 'L0_ffn_sp_in_w': _L0_ffn_in['sp_in_w'], 'L0_ffn_sp_in_b': _L0_ffn_in['sp_in_b'], 'L0_ffn_sp_out_w': _L0_ffn_in['sp_out_w'], 'L0_ffn_sp_out_b': _L0_ffn_in['sp_out_b'], 'L0_ffn_tq_w': _L0_ffn_in['tq_w'], 'L0_ffn_tq_b': _L0_ffn_in['tq_b'], 'L0_ffn_tk_w': _L0_ffn_in['tk_w'], 'L0_ffn_tk_b': _L0_ffn_in['tk_b'], 'L0_ffn_tv_w': _L0_ffn_in['tv_w'], 'L0_ffn_tv_b': _L0_ffn_in['tv_b'], 'L0_ffn_tp_w': _L0_ffn_in['tp_w'], 'L0_ffn_tp_b': _L0_ffn_in['tp_b'], 'L0_ffn_cross_in_w': _L0_ffn_in['cross_in_w'], 'L0_ffn_cross_in_b': _L0_ffn_in['cross_in_b'], 'L0_ffn_cross_out_w': _L0_ffn_in['cross_out_w'], 'L0_ffn_cross_out_b': _L0_ffn_in['cross_out_b'], 'L0_ffn_norm_mlp_w': _L0_ffn_in['norm_mlp_w'], 'L0_ffn_norm_mlp_b': _L0_ffn_in['norm_mlp_b'], 'L0_ffn_mlp_w1': _L0_ffn_in['mlp_w1'], 'L0_ffn_mlp_b1': _L0_ffn_in['mlp_b1'], 'L0_ffn_mlp_w2': _L0_ffn_in['mlp_w2'], 'L0_ffn_mlp_b2': _L0_ffn_in['mlp_b2']}

def reference(x, src, dst, L0_gnn_W1_l, L0_gnn_b1, L0_gnn_W1_r, L0_gnn_W2_l, L0_gnn_b2, L0_gnn_W2_r, L0_ffn_router_w1, L0_ffn_router_b1, L0_ffn_router_w2, L0_ffn_router_b2, L0_ffn_norm_s_w, L0_ffn_norm_s_b, L0_ffn_norm_t_w, L0_ffn_norm_t_b, L0_ffn_sp_in_w, L0_ffn_sp_in_b, L0_ffn_sp_out_w, L0_ffn_sp_out_b, L0_ffn_tq_w, L0_ffn_tq_b, L0_ffn_tk_w, L0_ffn_tk_b, L0_ffn_tv_w, L0_ffn_tv_b, L0_ffn_tp_w, L0_ffn_tp_b, L0_ffn_cross_in_w, L0_ffn_cross_in_b, L0_ffn_cross_out_w, L0_ffn_cross_out_b, L0_ffn_norm_mlp_w, L0_ffn_norm_mlp_b, L0_ffn_mlp_w1, L0_ffn_mlp_b1, L0_ffn_mlp_w2, L0_ffn_mlp_b2):
    import jax
    import jax.numpy as jnp

    def _L0_gnn_ref(x, edge_index, W1_l, b1, W1_r, W2_l, b2, W2_r):
        import jax, jax.numpy as jnp
        import numpy as np
        N_NODES = 1250
        D_IN = 512
        D_HID = 512
        D_OUT = 512
        N_EDGES = 20000

        def sage_conv(x, edge_index, W_l, b_l, W_r):
            src, dst = (edge_index[0], edge_index[1])
            msgs = x[src]
            agg = jax.ops.segment_sum(msgs, dst, num_segments=x.shape[0])
            cnt = jax.ops.segment_sum(jnp.ones((msgs.shape[0],), x.dtype), dst, num_segments=x.shape[0])
            agg = agg / jnp.maximum(cnt, 1.0)[:, None]
            return agg @ W_l.T + b_l + x @ W_r.T
        h = jax.nn.relu(sage_conv(x, edge_index, W1_l, b1, W1_r))
        return sage_conv(h, edge_index, W2_l, b2, W2_r)

    def _L0_ffn_ref(x, router_w1, router_b1, router_w2, router_b2, norm_s_w, norm_s_b, norm_t_w, norm_t_b, sp_in_w, sp_in_b, sp_out_w, sp_out_b, tq_w, tq_b, tk_w, tk_b, tv_w, tv_b, tp_w, tp_b, cross_in_w, cross_in_b, cross_out_w, cross_out_b, norm_mlp_w, norm_mlp_b, mlp_w1, mlp_b1, mlp_w2, mlp_b2):
        import jax, jax.numpy as jnp
        import numpy as np
        D = 512
        H = 8
        K = 4
        HD = D // H

        def _ln(x, w, b, eps=1e-05):
            m = x.mean(-1, keepdims=True)
            v = ((x - m) ** 2).mean(-1, keepdims=True)
            return (x - m) / jnp.sqrt(v + eps) * w + b

        def _spatial_experts(xn, idx, in_w, in_b, out_w, out_b):
            W = in_w[idx]
            qkv = jnp.einsum('btd,bed->bte', xn, W) + in_b[idx][:, None, :]
            q, k, v = jnp.split(qkv, 3, axis=-1)
            B, T, _ = xn.shape
            q = q.reshape(B, T, H, HD) * HD ** (-0.5)
            k = k.reshape(B, T, H, HD)
            v = v.reshape(B, T, H, HD)
            att = jax.nn.softmax(jnp.einsum('bthd,bshd->bhts', q, k), axis=-1)
            o = jnp.einsum('bhts,bshd->bthd', att, v).reshape(B, T, D)
            return jnp.einsum('btd,bod->bto', o, out_w[idx]) + out_b[idx][:, None, :]

        def _temporal_experts(xt, idx, qw, qb, kw, kb, vw, vb, pw, pb):
            B, T, _ = xt.shape
            q = (jnp.einsum('btd,bod->bto', xt, qw[idx]) + qb[idx][:, None, :]).reshape(B, T, H, HD)
            k = (jnp.einsum('btd,bod->bto', xt, kw[idx]) + kb[idx][:, None, :]).reshape(B, T, H, HD)
            v = (jnp.einsum('btd,bod->bto', xt, vw[idx]) + vb[idx][:, None, :]).reshape(B, T, H, HD)
            logits = jnp.einsum('bthd,bshd->bhts', q, k) * HD ** (-0.5)
            causal = jnp.tril(jnp.ones((T, T), dtype=bool))
            logits = jnp.where(causal, logits, -jnp.inf)
            att = jax.nn.softmax(logits, axis=-1)
            o = jnp.einsum('bhts,bshd->bthd', att, v).reshape(B, T, D)
            o = jnp.einsum('btd,bod->bto', o, pw[idx]) + pb[idx][:, None, :]
            return xt + o

        def _cross_mha(q_in, kv_in, in_w, in_b, out_w, out_b):
            B, T, _ = q_in.shape
            S = kv_in.shape[1]
            Wq, Wk, Wv = (in_w[:D], in_w[D:2 * D], in_w[2 * D:])
            bq, bk, bv = (in_b[:D], in_b[D:2 * D], in_b[2 * D:])
            q = (q_in @ Wq.T + bq).reshape(B, T, H, HD) * HD ** (-0.5)
            k = (kv_in @ Wk.T + bk).reshape(B, S, H, HD)
            v = (kv_in @ Wv.T + bv).reshape(B, S, H, HD)
            att = jax.nn.softmax(jnp.einsum('bthd,bshd->bhts', q, k), axis=-1)
            o = jnp.einsum('bhts,bshd->bthd', att, v).reshape(B, T, D)
            return o @ out_w.T + out_b
        pooled = x.mean(axis=1)
        h = jax.nn.gelu(pooled @ router_w1.T + router_b1, approximate=False)
        route = jax.nn.softmax(h @ router_w2.T + router_b2, axis=-1)
        idx_s = jnp.argmax(route[:, :K], axis=-1)
        idx_t = jnp.argmax(route[:, K:], axis=-1)
        xn = _ln(x, norm_s_w, norm_s_b)
        spatial_out = _spatial_experts(xn, idx_s, sp_in_w, sp_in_b, sp_out_w, sp_out_b)
        xt = _ln(x, norm_t_w, norm_t_b)
        temporal_out = _temporal_experts(xt, idx_t, tq_w, tq_b, tk_w, tk_b, tv_w, tv_b, tp_w, tp_b)
        fused = _cross_mha(spatial_out, temporal_out, cross_in_w, cross_in_b, cross_out_w, cross_out_b)
        x = x + fused
        h2 = _ln(x, norm_mlp_w, norm_mlp_b)
        x = x + (jax.nn.gelu(h2 @ mlp_w1.T + mlp_b1, approximate=False) @ mlp_w2.T + mlp_b2)
        return x
    edge_index = jnp.stack([src, dst])
    x = x + _L0_gnn_ref(_layernorm(x, axis=-1), edge_index, L0_gnn_W1_l, L0_gnn_b1, L0_gnn_W1_r, L0_gnn_W2_l, L0_gnn_b2, L0_gnn_W2_r)
    x = x + _L0_ffn_ref(_layernorm(x, axis=-1)[None], L0_ffn_router_w1, L0_ffn_router_b1, L0_ffn_router_w2, L0_ffn_router_b2, L0_ffn_norm_s_w, L0_ffn_norm_s_b, L0_ffn_norm_t_w, L0_ffn_norm_t_b, L0_ffn_sp_in_w, L0_ffn_sp_in_b, L0_ffn_sp_out_w, L0_ffn_sp_out_b, L0_ffn_tq_w, L0_ffn_tq_b, L0_ffn_tk_w, L0_ffn_tk_b, L0_ffn_tv_w, L0_ffn_tv_b, L0_ffn_tp_w, L0_ffn_tp_b, L0_ffn_cross_in_w, L0_ffn_cross_in_b, L0_ffn_cross_out_w, L0_ffn_cross_out_b, L0_ffn_norm_mlp_w, L0_ffn_norm_mlp_b, L0_ffn_mlp_w1, L0_ffn_mlp_b1, L0_ffn_mlp_w2, L0_ffn_mlp_b2)[0]
    return x

_drawn_inputs = setup_inputs


def setup_inputs(seed=0):
    import zlib

    import numpy as np

    out = dict(_drawn_inputs(seed))
    spreads = {'L0_ffn_router_b1': (0.0, 0.1),
     'L0_ffn_router_b2': (0.0, 0.46),
     'L0_ffn_norm_s_w': (1.0, 0.6),
     'L0_ffn_norm_s_b': (0.0, 0.8),
     'L0_ffn_norm_t_w': (1.0, 0.6),
     'L0_ffn_norm_t_b': (0.0, 0.764),
     'L0_ffn_sp_in_b': (0.0, 0.8),
     'L0_ffn_sp_out_b': (0.0, 0.8),
     'L0_ffn_tq_b': (0.0, 0.8),
     'L0_ffn_tk_b': (0.0, 2.0),
     'L0_ffn_tv_b': (0.0, 0.8),
     'L0_ffn_tp_b': (0.0, 0.786),
     'L0_ffn_cross_in_b': (0.0, 0.357),
     'L0_ffn_cross_out_b': (0.0, 0.377),
     'L0_ffn_norm_mlp_w': (1.0, 0.6),
     'L0_ffn_norm_mlp_b': (0.0, 0.658),
     'L0_ffn_mlp_b1': (0.0, 0.295),
     'L0_ffn_mlp_b2': (0.0, 0.371)}
    factors = {'L0_gnn_b1': 4.895,
     'L0_ffn_router_w1': 4.81,
     'L0_ffn_router_w2': 4.81,
     'L0_ffn_sp_in_w': 8.0,
     'L0_ffn_sp_out_w': 8.0,
     'L0_ffn_tq_w': 8.0,
     'L0_ffn_tk_w': 8.0,
     'L0_ffn_tv_w': 8.0,
     'L0_ffn_tp_w': 8.0}
    for name, (base, spread) in spreads.items():
        noise = np.random.default_rng([zlib.crc32(name.encode()), seed]).standard_normal(out[name].shape)
        drawn = base * np.exp(spread * noise) if base else spread * noise
        out[name] = jnp.asarray(drawn.astype(out[name].dtype))
    for name, factor in factors.items():
        out[name] = (out[name] * factor).astype(out[name].dtype)
    return out
```

```python
from collections import namedtuple
from contextlib import ExitStack

import concourse.bass as bass
from concourse import mybir

F32 = mybir.dt.float32
F32R = mybir.dt.float32r
BF16 = mybir.dt.bfloat16
I32 = mybir.dt.int32
ALU = mybir.AluOpType
ACT = mybir.ActivationFunctionType
AX = mybir.AxisListType
ds = bass.ds

T, D, H, HD, NEXP = 1250, 512, 8, 64, 4
P = 125
NT = T // P
KC = D // 128
E = 41250
EC = E // P
EQ, EJ = 110, 3
WD = 25
NW = T // WD
WK = WD * NT
EPS = 1e-5
SCALE = float(HD) ** -0.5
BANK = 512
CHUNKS = [(0, 512), (512, 512), (1024, 226)]
EG = 4
EP = -(-EC // EG) * EG
RING = 2
SEG = 5
HG = NT // 2
NQ = 4

ORDER = ["g1l", "g1r", "g2l", "g2r", "qs", "ks", "vs", "us", "qc", "qt", "kt", "vt", "ut", "kc", "vc", "uc"]
UNIT = {n: 4 * i for i, n in enumerate(ORDER)}
UNIT["mlp"] = 4 * len(ORDER)
G0, S0 = 0, 16
T0 = S0 + 16 * NEXP
C0 = T0 + 16 * NEXP
M0 = C0 + 16
ROWB = dict(g1=0, g2=1, vs=2, vt=2 + NEXP, vc=2 + 2 * NEXP, uc=3 + 2 * NEXP, m2=4 + 2 * NEXP)


def Sems(make, prefix, names):
    names = names.split()
    return namedtuple(prefix, names)(*[make(f"{prefix}_{n}") for n in names])


class Chain:

    def __init__(self, eng, sem, base=0):
        self.eng, self.sem, self.base, self.n = eng, sem, base, 0

    def __call__(self, ins):
        self.n += 1
        ins.then_inc(self.sem, 1)
        self.eng.wait_ge(self.sem, self.base + self.n)


class Attn:

    def __init__(self, turn, causal):
        self.turn, self.causal = turn, causal
        self.blocks = [i + 1 if causal else NT for i in range(NT)] * 2
        self.banks = [(b + 3) // 4 for b in self.blocks]
        self.cols = [P * b for b in self.blocks]
        self.cum = [sum(self.banks[:n]) for n in range(2 * NT + 1)]
        self.total = self.cum[-1]
        full, half = 6 * NT, 2 * sum((i + 4) // 4 for i in range(NT))
        self.tiles0 = 2 * NT * (H // 2 + 1) * turn
        self.groups0 = 2 * HG * (H // 2 + 1) * turn
        self.banks0 = (H // 2 + 1) * (0, full, full + half)[turn]
        self.cuts0 = 7 * H * turn
        self.qin0 = 32 * H * turn
        self.links = 4 * HG + (2 * NT if causal else 0)
        self.links0 = H // 2 * (0, 4 * HG, 8 * HG + 2 * NT)[turn]

    def tile(self, hp, n):
        return self.tiles0 + 2 * NT * (hp + 1) + n + 1

    def bank(self, hp, n, b):
        return self.banks0 + self.total * (hp + 1 + n // (2 * NT)) + self.cum[n % (2 * NT)] + b + 1

    def group(self, hp, g):
        return self.groups0 + 2 * HG * (hp + 1) + g + 1


def gnn_ffn_program(nc, x, src, dst, weights, qkv_bias, out_bias, row_bias, ln_cols, mlp_b1,
                    router_w1, router_w2, router_b1, router_b2, out):
    with ExitStack() as ctx:
        def sb(name, shape, dt=F32):
            return ctx.enter_context(nc.sbuf_tensor(name, shape, dt))

        def sem(name):
            return ctx.enter_context(nc.semaphore(name))

        F = sb("F", [128, 22620])
        R = sb("R", [128, 22740], F32R)
        w_raw = sb("w_raw", [128, 2, 512])
        w_hi = sb("w_hi", [128, 4, 512], F32R)
        w_lo = sb("w_lo", [128, 4, 512], F32R)
        TB = sb("TB", [128, 3, 512])
        brow = sb("brow", [128, 512])
        ident = sb("ident", [128, 128])
        ones = sb("ones", [128, HD])
        ones_r = sb("ones_r", [128, 2], F32R)
        bcol = sb("bcol", [128, 12])
        bcol_q = sb("bcol_q", [128, 4])
        ocol = sb("ocol", [128, 4])
        lncol = sb("lncol", [128, 6, 4])
        b1col = sb("b1col", [128, 16])
        stats = sb("stats", [128, 2, 6])
        mv = sb("mv", [128, 2, 2])
        sd = sb("sd", [128, 2, 2])
        mr1 = sb("mr1", [128, NT, 2])
        rcnt = sb("rcnt", [128, NT, 1])
        cntm = sb("cntm", [128, 2])
        ngm = sb("ngm", [128, 2])
        rs = sb("rs", [128, 4])
        rr = sb("rr", [128, 2])
        rt = sb("rt", [128, 48])
        eps_t = sb("eps_t", [128, 1])
        zero = sb("zero", [128, 1])
        idx_i = sb("idx_i", [1, 2], I32)
        win = sb("win", [1, 2 * NW], I32)
        ps = ctx.enter_context(nc.psum_tensor("ps", [128, 8, BANK], F32))

        def flat(a):
            return ps[:, 3 * a:3 * a + 3, :].rearrange("p a b -> p (a b)")

        def rows(a):
            return a.rearrange("p (i f) -> p i f", i=NT)

        def cols(a):
            return a.rearrange("p (k t) -> p k t", k=KC)

        AT = F[:, 0:12500].rearrange("p (h d) -> p h d", h=NT)
        RW = rows(F[:, 12500:17620])
        ZT = cols(F[:, 17620:22620])
        e_base = 12500

        def eview(off, n, parts=P):
            return F[0:parts, e_base + off:e_base + off + n]
        s_i = eview(0, 375, EQ).bitcast(I32)
        d_i = eview(375, 375, EQ).bitcast(I32)
        s_f = eview(750, 375, EQ)
        d_f = eview(1125, 375, EQ)
        h_f = eview(1500, 375, EQ)
        l_f = eview(0, 375, EQ)
        k_f = eview(375, 375, EQ)
        mm2 = eview(1875, 6, EQ)
        loT = eview(1882, EP)
        keyT = eview(2214, EP)
        wcol = eview(2546, 8, NW)
        woff = eview(2554, NW)
        iota_b = eview(2604, 128).bitcast(BF16)
        zero_b = eview(2732, 125).bitcast(BF16)
        oh_key = eview(2858, RING * EG * 125).bitcast(BF16).rearrange("p (r g c) -> p r g c", r=RING, g=EG)
        oh_lo = eview(3858, RING * EG * 64).bitcast(BF16).rearrange("p (r g c) -> p r g c", r=RING, g=EG)
        dbc = eview(2858, 2 * EC, NW)
        msk = eview(3518, EC, NW)
        cid = eview(4370, EP, NW)
        QK = F[:, 0:10000].rearrange("p (j m t) -> p j m t", j=2, m=KC)
        V = rows(F[:, 10000:15120])
        XR = cols(F[:, 10000:15000])
        PB = F[:, 15120:17620].rearrange("p (b t) -> p b t", b=2)
        ACC = rows(F[:, 0:5120])
        w1r = F[:, 15120:15632]
        w2r = F[:, 15632:15640]
        prow = F[0:1, 15700:16212]
        diag = TB[:, 0, 0:250].rearrange("p (s t) -> p s t", s=2)
        comb = TB[0:HD, 1, 0:252]
        mask = TB[0:P, 0, 256:256 + P]

        X0 = (cols(R[:, 0:5000]), cols(R[:, 5000:10000]))
        X1 = (cols(R[:, 10000:15000]), cols(R[:, 15000:20000]))
        Y = (rows(R[:, 10000:15120]), rows(R[:, 15120:20240]))
        AS = [[R[0:P, 20240 + 1250 * p + 625 * h:20240 + 1250 * p + 625 * h + 625]
               .rearrange("p (c d) -> p c d", c=5) for h in range(2)] for p in range(2)]
        HB = 10080
        QSH = [R[:, HB:HB + 1250], R[:, HB + 1250:HB + 2500]]
        QSL = [R[:, HB + 2500:HB + 3750], R[:, HB + 3750:HB + 5000]]
        KS = [R[:, HB + 5000:HB + 6250], R[:, HB + 6250:HB + 7500]]
        VS = [R[0:P, HB + 7500 + 1280 * b:HB + 8780 + 1280 * b].rearrange("p (c n) -> p c n", c=NT) for b in range(2)]
        KT = R[:, HB + 10060:HB + 10060 + 1250]
        PT = [R[0:P, 5040 * p:5040 * p + 5040]
              .rearrange("p (g c s t) -> p g c s t", g=2, c=NT, s=2) for p in range(2)]

        mm_d = nc.dram_tensor("mm_d", [2, EC], F32, kind="Internal").ap()
        x1_d = nc.dram_tensor("x1_d", [NT, P, D], F32, kind="Internal").ap()
        zt_d = nc.dram_tensor("zt_d", [128, KC, T], F32, kind="Internal").ap()
        xt_d = nc.dram_tensor("xt_d", [128, KC, T], F32, kind="Internal").ap()
        qc_d = nc.dram_tensor("qc_d", [128, KC, T], F32, kind="Internal").ap()

        const_ok, small_in, w_split, w_used = (sem(n) for n in ("const_ok", "small_in", "w_split", "w_used"))
        w_in = [sem("w_in0"), sem("w_in1")]
        ln_names = "src0 src1 var std nrm tr ev lk"
        ln0, ln2, ln3 = (Sems(sem, n, ln_names) for n in ("lnx", "lnz", "lnm"))
        ln1 = Sems(sem, "h", "nrm tr ev lk")
        sp = {n: Sems(sem, "cut_" + n, names) for n, names in
              dict(x="hi lo", h="hi lo", s="val hi lo", os="hi lo", t="val hi lo st0 st1", ot="hi lo", oc="hi lo",
                   m="val hi lo").items()}
        pj = {n: Sems(sem, "prod_" + n, names) for n, names in
              dict(g="ps a v", qk="a", v="ps v", u="a v t", uc="ps v", m1="a v t", m2="ps a v").items()}
        A = Sems(sem, "att", "qin0 qin1 cut scores negmax exp tr hi lo pv diag bc bot post lk")
        KS_, KT_, KC_ = Attn(0, False), Attn(1, True), Attn(2, False)
        ag = [Sems(sem, f"agg{n}", "hi lo pe cnt dv") for n in range(2)]
        e = Sems(sem, "edge", "in_ lk tr mm mmd mmi w win ev")
        oh_ready, oh_used, at_ready, at_free = (sem(n) for n in ("oh_ready", "oh_used", "at_ready", "at_free"))
        r = Sems(sem, "router", "in_ sums row tr col h he l i lk")
        bcol_in = [sem(f"bcol_in{i}") for i in range(4)]
        ocol_in = [sem(f"ocol_in{i}") for i in range(2)]
        row_in, row_free, xr_in, qc_st, qc_in, zt_in, x1_st, fin, out_st, biasq, pad_ok, mask_ok, ysum, zt_st, held = (
            sem(n) for n in ("row_in", "row_free", "xr_in", "qc_st", "qc_in", "zt_in", "x1_st", "fin", "out_st",
                             "biasq", "pad_ok", "mask_ok", "ysum", "zt_st", "held"))

        block = ctx.enter_context(nc.Block())

        @block.sync
        def _(eng):
            def load_units(unit, count, dram):
                for j in range(count):
                    if not isinstance(unit, int) or unit + j >= 2:
                        eng.wait_ge(w_split, 2 * (unit + j) - 2)
                    eng.dma_start(w_raw[:, j % 2, :], weights[ds(dram + j, 1), :, :].rearrange("a p c -> p (a c)")
                                  ).then_inc(w_in[j % 2], 16)

            def load_row(n, row):
                if n:
                    eng.wait_ge(row_free, n)
                eng.dma_start(brow[0:P, :], row_bias[ds(row, 1), :].to_broadcast([P, D])).then_inc(row_in, 16)

            def load_tiles(L, source):
                with eng.Fori(0, NT // 2) as i2:
                    for b in range(2):
                        eng.wait_ge(L.tr, 2 * i2 + b + 1)
                        eng.dma_start(TB[0:P, b, :], source[ds(2 * i2 + b, 1), :, :].rearrange("a p f -> p (a f)")
                                      ).then_inc((L.src0, L.src1)[b], 16)

            def load_heads(K):
                with eng.Fori(0, H // 2) as hp:
                    for b in range(2):
                        eng.wait_ge(A.scores, K.tile(hp, NT * (b - 1) - 1))
                        for half in range(2):
                            for j, t in ((0, QSL), (1, KS)):
                                eng.dma_start(t[b][64 * half:64 * half + 64, :].bitcast(F32),
                                              QK[64 * b:64 * b + 64, j, ds(hp, 1), :].rearrange("p a t -> p (a t)")
                                              ).then_inc((A.qin0, A.qin1)[b], 16)

            eng.dma_start(s_i, src.rearrange("(q r) -> q r", q=EQ)).then_inc(e.in_, 16)
            eng.dma_start(d_i, dst.rearrange("(q r) -> q r", q=EQ)).then_inc(e.in_, 16)
            load_tiles(ln0, x)
            eng.dma_start(lncol[:], ln_cols).then_inc(small_in, 16)
            eng.dma_start(b1col[:], mlp_b1).then_inc(small_in, 16)
            eng.dma_start(rt[:, 0:1], router_b1).then_inc(small_in, 16)
            eng.dma_start(rt[0:1, 8:16], router_b2).then_inc(small_in, 16)
            eng.wait_ge(e.mm, 2)
            eng.dma_start(mm_d.rearrange("m (q j) -> q m j", j=EJ), mm2.rearrange("q (m j) -> q m j", m=2)
                          ).then_inc(e.mmd, 16)
            eng.wait_ge(e.mmd, 16)
            eng.dma_start(dbc, mm_d.rearrange("m c -> (m c)").unsqueeze(0).to_broadcast([NW, 2 * EC])
                          ).then_inc(e.mmi, 16)
            eng.wait_ge(e.w, 2)
            eng.dma_start(win[:, :].rearrange("a (w c) -> a w c", c=2), wcol[:, 6:8].bitcast(I32)).then_inc(e.win, 16)
            load_row(0, ROWB["g1"])
            load_units(0, 16, G0)
            load_row(1, ROWB["g2"])
            load_tiles(ln2, x)
            with eng.Fori(0, NT) as i:
                eng.wait_ge(ysum, i + 1)
                eng.dma_start(x1_d[ds(i, 1), :, :].rearrange("a p f -> p (a f)"),
                              RW[0:P, ds(i, 1), :].rearrange("p a f -> p (a f)")).then_inc(x1_st, 16)
            eng.wait_ge(x1_st, 16 * NT)
            eng.dma_start(w1r, router_w1).then_inc(r.in_, 16)
            eng.dma_start(w2r, router_w2).then_inc(r.in_, 16)
            eng.wait_ge(r.i, 2)
            e_s = eng.value_load(idx_i[0:1, 0:1], min_val=0, max_val=NEXP - 1)
            e_t = eng.value_load(idx_i[0:1, 1:2], min_val=0, max_val=NEXP - 1)
            eng.dma_start(bcol[:], qkv_bias[ds(e_s, 1), :, :].rearrange("a p c -> p (a c)")).then_inc(bcol_in[0], 16)
            eng.dma_start(ocol[:], out_bias[ds(e_s, 1), :, :].rearrange("a p c -> p (a c)")).then_inc(ocol_in[0], 16)
            load_row(2, e_s + ROWB["vs"])
            load_units(UNIT["qs"], 4, e_s * 16 + S0)
            eng.dma_start(zt_d, ZT).then_inc(zt_st, 16)
            load_units(UNIT["ks"], 8, e_s * 16 + (S0 + 4))
            eng.wait_ge(pj["qk"].a, 8)
            eng.wait_ge(zt_st, 16)
            load_heads(KS_)
            load_units(UNIT["us"], 4, e_s * 16 + (S0 + 12))
            load_units(UNIT["qc"], 4, C0)
            eng.dma_start(bcol[:], qkv_bias[2 * NEXP, :, :]).then_inc(bcol_in[1], 16)
            load_row(3, e_t + ROWB["vt"])
            eng.wait_ge(sp["os"].lo, KC)
            eng.wait_ge(zt_st, 16)
            eng.dma_start(ZT, zt_d).then_inc(zt_in, 16)
            eng.wait_ge(pj["u"].v, 4)
            eng.dma_start(ocol[:], out_bias[ds(e_t + NEXP, 1), :, :].rearrange("a p c -> p (a c)")
                          ).then_inc(ocol_in[1], 16)
            load_units(UNIT["qt"], 4, e_t * 16 + T0)
            eng.wait_ge(pj["qk"].a, 12)
            eng.dma_start(qc_d, QK[:, 0, :, :]).then_inc(qc_st, 16)
            eng.dma_start(bcol[:], qkv_bias[ds(e_t + NEXP, 1), :, :].rearrange("a p c -> p (a c)")
                          ).then_inc(bcol_in[2], 16)
            for k in range(KC):
                eng.wait_ge(sp["t"].val, k + 1)
                eng.dma_start(xt_d[:, k, :], PB[:, k % 2, :]).then_inc((sp["t"].st0, sp["t"].st1)[k % 2], 16)
            load_units(UNIT["kt"], 8, e_t * 16 + (T0 + 4))
            eng.wait_ge(pj["qk"].a, 20)
            load_heads(KT_)
            load_units(UNIT["ut"], 4, e_t * 16 + (T0 + 12))
            eng.wait_ge(A.cut, 14 * H)
            eng.wait_ge(sp["t"].st0, 32)
            eng.wait_ge(sp["t"].st1, 32)
            eng.dma_start(XR, xt_d).then_inc(xr_in, 16)
            eng.dma_start(bcol[:], qkv_bias[2 * NEXP, :, :]).then_inc(bcol_in[3], 16)
            load_row(4, ROWB["vc"])
            eng.wait_ge(qc_st, 16)
            eng.dma_start(QK[:, 0, :, :], qc_d).then_inc(qc_in, 16)
            load_units(UNIT["kc"], 8, C0 + 4)
            eng.wait_ge(pj["qk"].a, 24)
            eng.wait_ge(qc_in, 16)
            load_heads(KC_)
            load_row(5, ROWB["uc"])
            load_units(UNIT["uc"], 4, C0 + 12)
            eng.wait_ge(sp["oc"].lo, KC)
            load_tiles(ln3, x1_d)
            load_row(6, ROWB["m2"])
            with eng.Fori(0, NQ) as q:
                load_units(q * 8 + UNIT["mlp"], 4, q * 4 + M0)
                load_units(q * 8 + (UNIT["mlp"] + 4), 4, q * 4 + (M0 + 16))
            for i in range(NT):
                eng.wait_ge(fin, i + 1)
                eng.dma_start(out[i, :, :], ACC[0:P, i, :]).then_inc(out_st, 16)
            eng.wait_ge(out_st, 16 * NT)

        @block.gpsimd
        def _(eng):
            eng.memset(ident[:], 0.0).then_inc(const_ok, 1)
            eng.memset(ones[:], 1.0).then_inc(const_ok, 1)
            eng.memset(ones_r[:].bitcast(F32), 1.0).then_inc(const_ok, 1)
            eng.memset(eps_t[:], EPS).then_inc(const_ok, 1)
            eng.memset(zero[:], 0.0).then_inc(const_ok, 1)
            eng.wait_ge(const_ok, 1)
            eng.affine_select(out=ident[:], in_=ident[:], compare_op=ALU.not_equal, fill=1.0, base=0,
                              pattern=[[-1, 128]], channel_multiplier=1).then_inc(const_ok, 1)
            for t, step, count, per_partition in ((iota_b[:, 0:250], 1, 250, 0), (woff, WK, NW, 0), (cid, 1, EP // EG, 0),
                                                  (wcol[:, 0:1], 1, 1, WD), (rt[0:1, 16:20], -1, 4, 0)):
                eng.iota(t, pattern=[[step, count]] + ([[0, EG]] if t is cid else []), base=4 if step < 0 else 0, channel_multiplier=per_partition,
                         allow_small_or_imprecise_dtypes=True).then_inc(const_ok, 1)
            eng.memset(zero_b, 0.0).then_inc(const_ok, 1)
            eng.memset(loT[:, EC:EP], 0.0).then_inc(const_ok, 1)
            eng.memset(keyT[:, EC:EP], -1.0).then_inc(const_ok, 1)

            def hi_part(to, a):
                return eng.tensor_tensor(to, a, zero[0:to.shape[0], :].to_broadcast(list(to.shape)), ALU.add)

            def cut_unit(u, s):
                if isinstance(u, int):
                    eng.wait_ge(w_in[s % 2], 16 * (u // 2 + 1))
                    if u >= 4:
                        eng.wait_ge(w_used, u - 3)
                else:
                    eng.wait_ge(w_in[s % 2], (u - s % 2) * 8 + 16)
                    eng.sem_inc(held, 1)
                    eng.wait_ge(w_used, u - 3)
                    eng.sem_inc(held, 1)
                hi_part(w_hi[:, s, :], w_raw[:, s % 2, :]).then_inc(w_split, 1)
                eng.wait_ge(w_split, 2 * u + 1)
                eng.tensor_tensor(w_lo[:, s, :], w_raw[:, s % 2, :], w_hi[:, s, :].bitcast(F32), ALU.subtract
                                  ).then_inc(w_split, 1)

            def cut_units(unit, end):
                for u in range(unit, end):
                    cut_unit(u, u % 4)

            def cut_heads(K):
                eng.sem_inc(A.scores, 2 * NT)
                with eng.Fori(0, H // 2) as hp:
                    for b in range(2):
                        n0 = K.cuts0 + 14 * hp + 7 * b
                        eng.wait_ge((A.qin0, A.qin1)[b], K.qin0 + 64 * hp + 64)
                        eng.sem_inc(held, 1)
                        hi_part(QSH[b], QSL[b].bitcast(F32)).then_inc(A.cut, 1)
                        eng.wait_ge(A.cut, n0 + 1)
                        eng.sem_inc(held, 1)
                        eng.tensor_tensor(KT[64:128, :], KS[b][64:128, :].bitcast(F32),
                                          zero[64:128, :].to_broadcast([64, T]), ALU.add).then_inc(A.cut, 1)
                        eng.wait_ge(A.cut, n0 + 2)
                        eng.sem_inc(held, 1)
                        hi_part(KS[b][0:64, :], KS[b][0:64, :].bitcast(F32)).then_inc(A.cut, 1)
                        eng.wait_ge(A.cut, n0 + 3)
                        eng.tensor_tensor(QSL[b], QSL[b].bitcast(F32), QSH[b].bitcast(F32), ALU.subtract
                                          ).then_inc(A.cut, 1)
                        eng.wait_ge(A.cut, n0 + 4)
                        eng.tensor_tensor(KS[b][64:128, :], KS[b][64:128, :].bitcast(F32), KT[64:128, :].bitcast(F32),
                                          ALU.subtract).then_inc(A.cut, 1)
                        eng.wait_ge(A.cut, n0 + 5)
                        eng.wait_ge(A.pv, K.group(hp, HG * (b - 1) - 1))
                        eng.sem_inc(held, 1)
                        eng.wait_ge(pj["v"].v, NT * (K.turn + 1))
                        vh = V[0:P, :, ds(128 * hp + 64 * b, 64)]
                        eng.tensor_copy(VS[b][:, :, 0:64], vh).then_inc(A.cut, 1)
                        eng.wait_ge(A.cut, n0 + 6)
                        eng.sem_inc(held, 1)
                        eng.tensor_tensor(VS[b][:, :, 64:128], vh, VS[b][:, :, 0:64].bitcast(F32), ALU.subtract
                                          ).then_inc(A.cut, 1)

            cut_units(0, UNIT["us"])
            cut_heads(KS_)
            cut_units(UNIT["us"], UNIT["ut"])
            eng.memset(mask, 0.0).then_inc(mask_ok, 1)
            eng.wait_ge(mask_ok, 1)
            eng.affine_select(out=mask, in_=mask, compare_op=ALU.is_ge, fill=-1e30, base=0,
                              pattern=[[-1, P]], channel_multiplier=1).then_inc(mask_ok, 1)
            cut_heads(KT_)
            cut_units(UNIT["ut"], UNIT["uc"])
            cut_heads(KC_)
            cut_units(UNIT["uc"], UNIT["mlp"])
            with eng.Fori(0, 2 * NQ) as q:
                for s in range(4):
                    cut_unit(q * 4 + (UNIT["mlp"] + s), s)

        @block.tensor
        def _(eng):
            def three(to, ah, al, bh, bl, first, last):
                eng.matmul(to, ah, bh, start=first, stop=False)
                eng.matmul(to, al, bh, start=False, stop=False)
                return eng.matmul(to, ah, bl, start=False, stop=last)

            def turn(L, b, i2):
                eng.wait_ge(L.nrm, 2 * i2 + b + 1)
                eng.wait_ge(L.ev, 2 * i2 + b + 1)
                t = 2 if L is ln2 else b
                for k in range(KC):
                    ins = eng.transpose(ps[:, 6 + b, P * k:P * k + P], TB[0:P, t, 128 * k:128 * k + 128],
                                        ident[0:P, 0:P])
                ins.then_inc(L.tr, 1)

            def product_cols(J, unit, X, free, n0=0, k_ready=None, k0=0, last=None):
                for m in range(4):
                    eng.wait_ge(w_split, 2 * (unit + m) + 2)
                    if not isinstance(n0, int) or n0 + m >= 2:
                        eng.wait_ge(free, n0 + m - 1)
                    if last is not None and m < 2:
                        eng.wait_ge(last[0], last[1] - 1 + m)
                    for c, (lo, n) in enumerate(CHUNKS):
                        for k in range(KC):
                            if m == 0 and c == 0 and k_ready is not None:
                                eng.wait_ge(k_ready, k0 + k + 1)
                            wk = slice(128 * k, 128 * k + 128)
                            ins = three(flat(m % 2)[:, lo:lo + n], w_hi[:, m, wk], w_lo[:, m, wk],
                                        X[0][:, k, lo:lo + n], X[1][:, k, lo:lo + n], k == 0, k == KC - 1)
                    ins.then_inc(w_used, 1)

            def product_tile(J, i, unit, X, free, n0=0):
                if not isinstance(n0, int) or n0 + i >= 2:
                    eng.wait_ge(free, n0 + i - 1)
                tk = slice(P * i, P * i + P)
                for k in range(KC):
                    ins = three(ps[0:P, 6 + i % 2, :], X[0][:, k, tk], X[1][:, k, tk],
                                w_hi[:, k, :], w_lo[:, k, :], k == 0, k == KC - 1)
                ins.then_inc(J.ps, 1)

            def product_rows(J, unit, X, free, n0=0, ready=None):
                eng.wait_ge(w_split, 2 * (unit + 3) + 2)
                if ready is not None:
                    eng.wait_ge(ready, KC)
                for i in range(NT):
                    product_tile(J, i, unit, X, free, n0)
                eng.wait_ge(J.ps, n0 + NT)
                eng.sem_inc(w_used, 4)

            pair = eng.alloc_register("pair")

            def adjacency(first_w2, end_w2):
                with eng.Fori(first_w2, end_w2) as w2:
                    for j in range(2):
                        w = 2 * w2 + j
                        acc = ps[:, j, 0:WK]
                        first = eng.value_load(win[0:1, ds(2 * w, 1)], min_val=0, max_val=EP // EG - 1)
                        end = eng.value_load(win[0:1, ds(2 * w + 1, 1)], min_val=1, max_val=EP // EG)
                        eng.wait_ge(at_free, w + 1)
                        eng.matmul(acc, zero_b[:, 0:128], zero_b[:, 0:WK], start=True, stop=False)
                        with eng.Fori(first, end):
                            now = eng.snap(pair)
                            slot = eng.snap(now & (RING - 1))
                            eng.wait_ge(oh_ready, now * 2 + 2)
                            for g in range(EG):
                                ins = eng.matmul(acc, oh_lo[:, ds(slot, 1), g, :].rearrange("p a c -> p (a c)"),
                                                 oh_key[:, ds(slot, 1), g, :].rearrange("p a c -> p (a c)"),
                                                 start=False, stop=False)
                            ins.then_inc(oh_used, 1)
                            eng.reg_add(pair, pair, 1)
                        eng.matmul(acc, zero_b[:, 0:128], zero_b[:, 0:WK], start=False, stop=True).then_inc(at_ready, 1)

            def aggregate(layer):
                L, A = (ln1, ln2)[layer], ag[layer]
                with eng.Fori(0, NT // 2) as i2:
                    for b in range(2):
                        i = 2 * i2 + b
                        eng.wait_ge(A.dv, i + 1)
                        for h in range(2):
                            eng.wait_ge(A.lo, 2 * i + h + 1)
                            for c in range(5):
                                k = 5 * h + c
                                ins = three(ps[0:P, b, :], AS[0][h][:, c, :], AS[1][h][:, c, :],
                                            Y[0][0:P, k, :], Y[1][0:P, k, :], k == 0, k == NT - 1)
                                if layer == 0:
                                    eng.matmul(ps[0:P, 2 + b, 0:2], AS[0][h][:, c, :], ones_r[0:P, :],
                                               start=(k == 0), stop=False)
                                    ins = eng.matmul(ps[0:P, 2 + b, 0:2], AS[1][h][:, c, :], ones_r[0:P, :],
                                                     start=False, stop=(k == NT - 1))
                            ins.then_inc(A.pe, 1)
                    for b in range(2):
                        if layer == 1:
                            eng.wait_ge(ysum, 2 * i2 + b + 1)
                            eng.matmul(ps[0:1, 4, :], ones[0:P, 0:1], TB[0:P, b, :], start=False, stop=False
                                       ).then_inc(r.sums, 1)
                        turn(L, b, i2)

            def scores(K, hp, n):
                b, i = n // NT % 2, n % NT
                nxt = n // (2 * NT)
                if i == 0:
                    eng.wait_ge(A.cut, K.cuts0 + 14 * (hp + nxt) + 7 * b + 5)
                for c, (lo, w) in enumerate(CHUNKS):
                    if lo >= K.cols[i]:
                        continue
                    w = min(w, K.cols[i] - lo)
                    w += w % 2
                    before = min(c, K.banks[(n - 2) % NT] - 1)
                    eng.wait_ge(A.lo, K.bank(hp, n - 2, before))
                    to = flat(n % 2)[0:P, lo:lo + w]
                    eng.matmul(to, QSH[b][:, P * i:P * i + P], KS[b][:, lo:lo + w], start=True, stop=False)
                    ins = eng.matmul(to, QSL[b][:, P * i:P * i + P], KS[b][:, lo:lo + w], start=False, stop=True)
                ins.then_inc(A.scores, 1)

            def turn_probs(K, hp, n):
                eng.wait_ge(A.exp, K.tile(hp, n))
                for bank in range(K.banks[n]):
                    for q in range(min(4, K.blocks[n] - 4 * bank)):
                        c = 4 * bank + q
                        ins = eng.transpose(ps[0:P, 3 * (n % 2) + bank, P * q:P * q + P],
                                            PB[0:P, n % 2, P * c:P * c + P], ident[0:P, 0:P])
                    ins.then_inc(A.tr, 1)

            def values(K, hp, g):
                b, gh = g // HG, g % HG
                eng.wait_ge(A.lo, K.bank(hp, 2 * g + 1, K.banks[2 * g + 1] - 1))
                eng.wait_ge(A.post, K.group(hp, g - 1))
                if gh == 0:
                    eng.wait_ge(A.cut, K.cuts0 + 14 * hp + 7 * b + 7)
                for c in range(K.blocks[2 * g + 1]):
                    s = 1 if c >= K.blocks[2 * g] else 0
                    for p in range(2):
                        rhs = PT[p][:, g % 2, c, s:2, :].rearrange("p s t -> p (s t)")
                        ins = eng.matmul(ps[:, 6, 126 * s:252], VS[b][:, c, :], rhs, start=(c == 0 and p == 0),
                                         stop=(c == K.blocks[2 * g + 1] - 1 and p == 1))
                ins.then_inc(A.pv, 1)
                eng.wait_ge(A.diag, K.group(hp, g))
                for s in range(2):
                    ins = eng.matmul(ps[0:HD, 7, P * s:P * s + P], ones[0:P, :], diag[0:P, s, :], start=True, stop=True)
                ins.then_inc(A.bc, 1)

            def attend(K):
                scores(K, 0, 0)

                def body(hp, last):
                    for n in range(2 * NT):
                        if not (last and n == 2 * NT - 1):
                            scores(K, hp, n + 1)
                        turn_probs(K, hp, n)
                        if n % 2 == 0 and n >= 2:
                            values(K, hp, n // 2 - 1)
                    values(K, hp, 2 * HG - 1)
                with eng.Fori(0, H // 2 - 1) as hp:
                    body(hp, False)
                body(H // 2 - 1, True)

            eng.wait_ge(const_ok, 6)
            eng.wait_ge(e.mm, 1)
            for bank, t in ((4, l_f), (5, k_f)):
                for j in range(EJ):
                    ins = eng.transpose(ps[0:P, bank, EQ * j:EQ * j + EQ], t[:, P * j:P * j + P], ident[0:EQ, 0:EQ])
            ins.then_inc(e.tr, 1)
            with eng.Fori(0, NT // 2) as i2:
                for b in range(2):
                    turn(ln0, b, i2)
            eng.wait_ge(const_ok, 14)
            eng.wait_ge(e.win, 16)
            eng.reg_mov(pair, 0)
            for seg in range(SEG):
                adjacency(NW // 2 // SEG * seg, NW // 2 // SEG * (seg + 1))
                if seg == 0:
                    eng.wait_ge(w_split, 2 * (UNIT["g1l"] + 3) + 2)
                    eng.wait_ge(sp["x"].lo, KC)
                for i in range(NT // SEG * seg, NT // SEG * (seg + 1)):
                    product_tile(pj["g"], i, UNIT["g1l"], X0, pj["g"].v)
            eng.wait_ge(pj["g"].ps, NT)
            eng.sem_inc(w_used, 4)
            product_rows(pj["g"], UNIT["g1r"], X0, pj["g"].v, n0=NT)
            aggregate(0)
            product_rows(pj["g"], UNIT["g2l"], X0, pj["g"].v, n0=2 * NT, ready=sp["h"].lo)
            product_rows(pj["g"], UNIT["g2r"], X0, pj["g"].v, n0=3 * NT)
            eng.wait_ge(e.ev, 2)
            eng.matmul(ps[0:1, 4, :], ident[0:1, 1:2], brow[0:1, :], start=True, stop=False)
            aggregate(1)
            eng.matmul(ps[0:1, 4, :], ident[0:1, 1:2], brow[0:1, :], start=False, stop=True).then_inc(r.tr, 1)
            eng.wait_ge(r.row, 1)
            for k in range(KC):
                ins = eng.matmul(ps[:, 5, k:k + 1], prow[:, 128 * k:128 * k + 128], ones[0:1, 0:1], start=True, stop=True)
            ins.then_inc(r.tr, 1)
            eng.wait_ge(r.in_, 32)
            eng.wait_ge(r.col, 1)
            for k in range(KC):
                ins = eng.matmul(ps[:, 5, 8:9], w1r[:, 128 * k:128 * k + 128], rt[:, 1 + k:2 + k],
                                 start=(k == 0), stop=(k == KC - 1))
            ins.then_inc(r.h, 1)
            eng.wait_ge(r.he, 1)
            eng.matmul(ps[0:1, 5, 16:24], rt[:, 5:6], w2r, start=True, stop=True).then_inc(r.l, 1)

            product_cols(pj["qk"], UNIT["qs"], X0, pj["qk"].a, n0=0, k_ready=sp["s"].lo)
            product_cols(pj["qk"], UNIT["ks"], X0, pj["qk"].a, n0=4)
            product_rows(pj["v"], UNIT["vs"], X0, pj["v"].v, n0=0 * NT)
            attend(KS_)
            product_cols(pj["u"], UNIT["us"], X1, pj["u"].v, k_ready=sp["os"].lo)
            product_cols(pj["qk"], UNIT["qc"], X0, pj["qk"].a, n0=8, k_ready=pj["u"].t,
                         last=(pj["u"].v, 4))
            product_cols(pj["qk"], UNIT["qt"], X0, pj["qk"].a, n0=12, k_ready=sp["t"].lo)
            product_cols(pj["qk"], UNIT["kt"], X0, pj["qk"].a, n0=16)
            product_rows(pj["v"], UNIT["vt"], X0, pj["v"].v, n0=1 * NT)
            attend(KT_)
            product_cols(pj["u"], UNIT["ut"], X1, pj["u"].v, n0=4, k_ready=sp["ot"].lo)
            product_cols(pj["qk"], UNIT["kc"], X0, pj["qk"].a, n0=20, k_ready=pj["u"].t, k0=4,
                         last=(pj["u"].v, 8))
            product_rows(pj["v"], UNIT["vc"], X0, pj["v"].v, n0=2 * NT)
            attend(KC_)
            eng.wait_ge(w_split, 2 * (UNIT["uc"] + 3) + 2)
            eng.wait_ge(sp["oc"].lo, KC)
            for i in range(NT + 2):
                if i < NT:
                    product_tile(pj["uc"], i, UNIT["uc"], X1, pj["uc"].v)
                if i >= 2:
                    j = i - 2
                    eng.wait_ge(ln3.nrm, j + 1)
                    eng.wait_ge(ln3.ev, j + 1)
                    for k in range(KC):
                        ins = eng.transpose(ps[:, 4 + j % 2, P * k:P * k + P], TB[0:P, j % 2, 128 * k:128 * k + 128],
                                            ident[0:P, 0:P])
                    ins.then_inc(ln3.tr, 1)
            eng.wait_ge(pj["uc"].ps, NT)
            eng.sem_inc(w_used, 4)

            def mlp(q):
                u = 8 * q + UNIT["mlp"]
                product_cols(pj["m1"], u, X0, pj["m1"].a, n0=4 * q, k_ready=sp["m"].lo if isinstance(q, int) else None)
                eng.wait_ge(w_split, 2 * (u + 7) + 2)
                eng.wait_ge(pj["m1"].t, 4 * q + 4)
                for i in range(NT):
                    product_tile(pj["m2"], i, u, X1, pj["m2"].v, n0=NT * q)
                eng.wait_ge(pj["m2"].ps, NT * q + NT)
                eng.sem_inc(w_used, 4)
            mlp(0)
            with eng.Fori(1, NQ) as q:
                mlp(q)

        @block.scalar
        def _(eng):
            eng.wait_ge(const_ok, 5)

            def prime(sem_, n):
                eng.sem_inc(sem_, n)

            def deviation(L, b, i2, per=1):
                eng.wait_ge(L.var, per * (2 * i2 + b) + 1)
                eng.activation(sd[0:P, b, 0:1], mv[0:P, b, 1:2], ACT.Sqrt, bias=eps_t[0:P, :]).then_inc(L.std, 1)

            def cols_out(L, b, i2, func=ACT.Copy):
                eng.wait_ge(L.tr, 2 * i2 + b + 3)
                eng.activation(ZT[:, :, ds((2 * i2 + b) * P, P)],
                               ps[:, 6 + b, 0:KC * P].rearrange("p (k t) -> p k t", k=KC), func).then_inc(L.ev, 1)

            def cut_hi(S, get, X, affine):
                for k in range(KC):
                    if affine:
                        eng.wait_ge(S.val, k + 1)
                    eng.activation(X[0][:, k, :], get(k), ACT.Copy).then_inc(S.hi, 1)

            def bias_cols(J, unit, dst_, bias, scale, n0=0):
                for m in range(4):
                    eng.wait_ge(w_used, unit + m + 1)
                    eng.activation(dst_[:, m, :], flat(m % 2)[:, 0:T], ACT.Identity, bias=bias[:, m:m + 1],
                                   scale=scale).then_inc(J.a, 1)

            def attend(K):
                eng.sem_inc(A.exp, 2 * NT)
                eng.sem_inc(A.hi, K.total)
                eng.sem_inc(A.bot, 2 * HG)

                def exponentials(hp, n):
                    eng.wait_ge(A.negmax, K.tile(hp, n))
                    eng.wait_ge(A.tr, K.bank(hp, n - 2, K.banks[(n - 2) % (2 * NT)] - 1))
                    w = K.cols[n % (2 * NT)]
                    eng.activation(PB[0:P, n % 2, 0:w], flat(n % 2)[0:P, 0:w], ACT.Exp, bias=ngm[0:P, n % 2:n % 2 + 1],
                                   accum_out=rs[0:P, n % 4:n % 4 + 1]).then_inc(A.exp, 1)

                def probs_hi(hp, n):
                    g = n // 2
                    eng.wait_ge(A.pv, K.group(hp, g - 2))
                    for bank in range(K.banks[n]):
                        nb = min(4, K.blocks[n] - 4 * bank)
                        eng.wait_ge(A.tr, K.bank(hp, n, bank))
                        eng.activation(PT[0][:, g % 2, 4 * bank:4 * bank + nb, n % 2, 0:P],
                                       ps[0:P, 3 * (n % 2) + bank, 0:P * nb].rearrange("p (c t) -> p c t", c=nb),
                                       ACT.Copy).then_inc(A.hi, 1)

                def bottom(hp, g):
                    eng.wait_ge(A.pv, K.group(hp, g))
                    eng.wait_ge(A.post, K.group(hp, g - 1))
                    eng.activation(comb, ps[64:128, 6, 0:252], ACT.Copy).then_inc(A.bot, 1)

                def body(hp, last):
                    for n in range(2 * NT):
                        probs_hi(hp, n)
                        if not (last and n == 2 * NT - 1):
                            exponentials(hp, n + 1)
                        if n % 2 == 0 and n >= 2:
                            bottom(hp, n // 2 - 1)
                    bottom(hp, 2 * HG - 1)
                exponentials(0, 0)
                with eng.Fori(0, H // 2 - 1) as hp:
                    body(hp, False)
                body(H // 2 - 1, True)

            eng.wait_ge(e.tr, 1)
            for bank, t in ((4, loT), (5, keyT)):
                eng.activation(t[:, 0:EC].rearrange("p (q j) -> p j q", j=EJ),
                               ps[0:P, bank, 0:EC].rearrange("p (j q) -> p j q", j=EJ), ACT.Copy).then_inc(e.ev, 1)
            with eng.Fori(0, NT // 2) as i2:
                for b in range(2):
                    deviation(ln0, b, i2)
                for b in range(2):
                    cols_out(ln0, b, i2)
            eng.wait_ge(ln0.ev, NT + 2)
            cut_hi(sp["x"], lambda k: ZT[:, k, :], X0, False)
            def rows_hi(J, n0, first_i=0, end_i=NT):
                for i in range(first_i, end_i):
                    eng.wait_ge(J.ps, n0 + i + 1)
                    eng.activation(Y[0][0:P, i, :], ps[0:P, 6 + i % 2, :], ACT.Copy).then_inc(J.a, 1)

            def aggregate(layer):
                A, L = ag[layer], (ln1, ln2)[layer]
                with eng.Fori(0, NT // 2) as i2:
                    for b in range(2):
                        for h in range(2):
                            i = 2 * i2 + b
                            eng.wait_ge(A.pe, 2 * i + h + 1)
                            eng.activation(AS[0][h], AT[0:P, 5 * h:5 * h + 5, ds(i * P, P)], ACT.Copy).then_inc(A.hi, 1)
                    if layer:
                        for b in range(2):
                            deviation(L, b, i2, 2)
                            eng.wait_ge(L.var, 2 * (2 * i2 + b) + 2)
                            eng.activation(sd[0:P, b, 0:1], mv[0:P, b, 1:2], ACT.Sqrt, bias=eps_t[0:P, :]
                                           ).then_inc(L.std, 1)
                            cols_out(L, b, i2)
                    else:
                        for b in range(2):
                            cols_out(L, b, i2, ACT.Relu)
            for seg in range(SEG):
                with eng.Fori(NW // 2 // SEG * seg, NW // 2 // SEG * (seg + 1)) as w2:
                    for j in range(2):
                        w = 2 * w2 + j
                        eng.wait_ge(at_ready, w + 1)
                        eng.activation(AT[0:P, :, ds(w * WD, WD)],
                                       ps[0:P, j, 0:WK].rearrange("p (d h) -> p h d", h=NT), ACT.Copy
                                       ).then_inc(at_free, 1)
                rows_hi(pj["g"], 0, NT // SEG * seg, NT // SEG * (seg + 1))
            aggregate(0)
            eng.wait_ge(ln1.ev, NT + 2)
            cut_hi(sp["h"], lambda k: ZT[:, k, :], X0, False)
            rows_hi(pj["g"], 2 * NT)
            aggregate(1)
            eng.wait_ge(r.tr, 1)
            eng.wait_ge(x1_st, 16 * NT)
            eng.activation(prow, ps[0:1, 4, :], ACT.Copy, scale=1.0 / T).then_inc(r.row, 1)
            eng.wait_ge(r.tr, 2)
            eng.activation(rt[:, 1:5], ps[:, 5, 0:4], ACT.Copy).then_inc(r.col, 1)
            eng.wait_ge(small_in, 64)
            eng.wait_ge(r.h, 1)
            eng.activation(rt[:, 5:6], ps[:, 5, 8:9], ACT.Gelu, bias=rt[:, 0:1]).then_inc(r.he, 1)

            cut_hi(sp["s"], lambda k: PB[:, k % 2, :], X0, True)
            eng.wait_ge(biasq, 1)
            bias_cols(pj["qk"], UNIT["qs"], QK[:, 0], bcol_q, SCALE)
            bias_cols(pj["qk"], UNIT["ks"], QK[:, 1], bcol[:, 4:8], 1.0)
            attend(KS_)

            def cut_out(S, K):
                eng.wait_ge(A.post, K.group(H // 2 - 1, 2 * HG - 1))
                cut_hi(S, lambda k: ZT[:, k, :], X1, False)

            def out_hi(J, n0):
                for m in range(4):
                    eng.wait_ge(J.v, n0 + m + 1)
                    eng.activation(X0[0][:, m, :], PB[:, m % 2, :], ACT.Copy).then_inc(J.a, 1)
            cut_out(sp["os"], KS_)
            out_hi(pj["u"], 0)
            eng.wait_ge(biasq, 2)
            bias_cols(pj["qk"], UNIT["qc"], QK[:, 0], bcol_q, SCALE)
            cut_hi(sp["t"], lambda k: PB[:, k % 2, :], X0, True)
            eng.wait_ge(biasq, 3)
            eng.wait_ge(qc_st, 16)
            bias_cols(pj["qk"], UNIT["qt"], QK[:, 0], bcol_q, SCALE)
            bias_cols(pj["qk"], UNIT["kt"], QK[:, 1], bcol[:, 4:8], 1.0)
            attend(KT_)
            cut_out(sp["ot"], KT_)
            out_hi(pj["u"], 4)
            eng.wait_ge(bcol_in[3], 16)
            bias_cols(pj["qk"], UNIT["kc"], QK[:, 1], bcol[:, 4:8], 1.0)
            attend(KC_)
            cut_out(sp["oc"], KC_)
            for i in range(NT + 2):
                if i < NT:
                    eng.wait_ge(ln3.var, i + 1)
                    eng.activation(sd[0:P, i % 2, 0:1], mv[0:P, i % 2, 1:2], ACT.Sqrt, bias=eps_t[0:P, :]
                                   ).then_inc(ln3.std, 1)
                if i >= 2:
                    j = i - 2
                    eng.wait_ge(ln3.tr, j + 3)
                    eng.activation(ZT[:, :, P * j:P * j + P],
                                   ps[:, 4 + j % 2, 0:KC * P].rearrange("p (k t) -> p k t", k=KC), ACT.Copy
                                   ).then_inc(ln3.ev, 1)
            cut_hi(sp["m"], lambda k: PB[:, k % 2, :], X0, True)

            def mlp(q):
                for m in range(4):
                    eng.wait_ge(w_used, 8 * q + (UNIT["mlp"] + m + 1))
                    if not isinstance(q, int) or 4 * q + m >= 2:
                        eng.wait_ge(pj["m1"].t, 4 * q + m - 1)
                    b1 = b1col[:, m:m + 1] if isinstance(q, int) else b1col[:, ds(4 * q + m, 1)]
                    eng.activation(PB[:, m % 2, :], flat(m % 2)[:, 0:T], ACT.Gelu, bias=b1).then_inc(pj["m1"].a, 1)
            mlp(0)
            with eng.Fori(1, NQ) as q:
                mlp(q)

        @block.vector
        def _(eng):
            for s, n in ((ln0.tr, 2), (ln0.ev, 2), (ln1.tr, 2), (ln1.ev, 2), (ln2.tr, 2), (ln2.ev, 2), (ln3.tr, 2),
                         (ln3.ev, 2), (at_free, 2), (ag[0].pe, 2), (ag[0].dv, 2), (ag[1].pe, 2), (ag[1].dv, 2),
                         (oh_used, RING)):
                eng.sem_inc(s, n)

            link = Chain(eng, e.lk)
            eng.wait_ge(e.in_, 32)
            eng.tensor_copy(s_f, s_i).then_inc(e.lk, 1)
            eng.tensor_copy(d_f, d_i).then_inc(e.lk, 1)
            link.n = 2
            eng.wait_ge(e.lk, 2)
            link(eng.tensor_scalar(h_f, s_f, float(P), None, ALU.is_ge))
            for j in range(2, NT):
                link(eng.scalar_tensor_tensor(out=h_f, in0=s_f, scalar=float(P * j), in1=h_f, op0=ALU.is_ge, op1=ALU.add))
            link(eng.scalar_tensor_tensor(out=l_f, in0=h_f, scalar=-float(P), in1=s_f, op0=ALU.mult, op1=ALU.add))
            eng.scalar_tensor_tensor(out=k_f, in0=d_f, scalar=float(NT), in1=h_f, op0=ALU.mult, op1=ALU.add
                                     ).then_inc(e.mm, 1)
            d3 = d_f.rearrange("q (j p) -> q j p", j=EJ)
            link(eng.tensor_reduce(out=mm2[:, 0:3], in_=d3, op=ALU.min, axis=AX.X))
            eng.tensor_reduce(out=mm2[:, 3:6], in_=d3, op=ALU.max, axis=AX.X).then_inc(e.mm, 1)

            def stat(L, b, i2, source, c, buf=None):
                eng.sem_inc(held, 1)
                c(eng.bn_stats(stats[0:P, b, :], source))
                eng.sem_inc(held, 1)
                eng.bn_aggr(mv[0:P, b, :], stats[0:P, b, :]).then_inc(L.var, 1)

            with eng.Fori(0, NT // 2) as i2:
                c = Chain(eng, ln0.lk, 4 * i2)
                for b in range(2):
                    eng.wait_ge((ln0.src0, ln0.src1)[b], 16 * i2 + 16)
                    stat(ln0, b, i2, TB[0:P, b, :], c)
                for b in range(2):
                    eng.wait_ge(ln0.std, 2 * i2 + b + 1)
                    c(eng.reciprocal(sd[0:P, b, 1:2], sd[0:P, b, 0:1]))
                    eng.tensor_scalar(TB[0:P, b, :], TB[0:P, b, :], mv[0:P, b, 0:1], sd[0:P, b, 1:2],
                                      ALU.subtract, ALU.mult).then_inc(ln0.nrm, 1)

            eng.wait_ge(const_ok, 14)
            eng.wait_ge(e.mmi, 16)
            link(eng.tensor_scalar(wcol[:, 1:2], wcol[:, 0:1], float(WD - 1), None, ALU.add))
            link(eng.tensor_scalar(msk, dbc[:, EC:2 * EC], wcol[:, 0:1], None, ALU.is_ge))
            link(eng.scalar_tensor_tensor(out=msk, in0=dbc[:, 0:EC], scalar=wcol[:, 1:2], in1=msk,
                                          op0=ALU.is_le, op1=ALU.mult))
            link(eng.scalar_tensor_tensor(out=dbc[:, 0:EC], in0=cid[:, 0:EC], scalar=1.0, in1=msk, op0=ALU.add, op1=ALU.mult))
            link(eng.tensor_reduce(out=wcol[:, 2:3], in_=dbc[:, 0:EC], op=ALU.max, axis=AX.X))
            link(eng.scalar_tensor_tensor(out=dbc[:, 0:EC], in0=msk, scalar=-1000.0, in1=cid[:, 0:EC], op0=ALU.mult, op1=ALU.add))
            link(eng.tensor_reduce(out=wcol[:, 4:5], in_=dbc[:, 0:EC], op=ALU.min, axis=AX.X))
            link(eng.tensor_scalar(wcol[:, 3:4], wcol[:, 2:3], 1.0, None, ALU.max))
            link(eng.tensor_scalar(wcol[:, 5:6], wcol[:, 3:4], -1.0, None, ALU.add))
            eng.tensor_scalar(wcol[:, 6:7].bitcast(I32), wcol[:, 4:5], 1000.0, wcol[:, 5:6], ALU.add, ALU.min
                              ).then_inc(e.w, 1)
            eng.tensor_copy(wcol[:, 7:8].bitcast(I32), wcol[:, 3:4]).then_inc(e.w, 1)

            def cut_lo(S, get, X):
                for k in range(KC):
                    eng.wait_ge(S.hi, k + 1)
                    eng.tensor_tensor(X[1][:, k, :], get(k), X[0][:, k, :].bitcast(F32), ALU.subtract).then_inc(S.lo, 1)

            def cut_affine(S, w, b, X, stored=False):
                for k in range(KC):
                    if k >= 2 and stored:
                        eng.wait_ge((S.st0, S.st1)[k % 2], 16)
                    if k >= 2:
                        eng.wait_ge(S.lo, k - 1)
                    eng.tensor_scalar(PB[:, k % 2, :], ZT[:, k, :], lncol[:, w, k:k + 1], lncol[:, b, k:k + 1],
                                      ALU.mult, ALU.add).then_inc(S.val, 1)
                    if k:
                        lo_affine(S, X, k - 1)
                lo_affine(S, X, KC - 1)

            def lo_affine(S, X, k):
                eng.wait_ge(S.hi, k + 1)
                eng.tensor_tensor(X[1][:, k, :], PB[:, k % 2, :], X[0][:, k, :].bitcast(F32), ALU.subtract
                                  ).then_inc(S.lo, 1)

            eng.wait_ge(ln0.ev, NT + 2)
            cut_lo(sp["x"], lambda k: ZT[:, k, :], X0)

            eng.wait_ge(e.win, 16)
            eng.wait_ge(e.ev, 2)
            def rows_lo(J, a0, first_i=0, end_i=NT):
                for i in range(first_i, end_i):
                    eng.wait_ge(J.a, a0 + i + 1)
                    eng.tensor_tensor(Y[1][0:P, i, :], ps[0:P, 6 + i % 2, :], Y[0][0:P, i, :].bitcast(F32), ALU.subtract
                                      ).then_inc(J.v, 1)

            def rows_bias(J, dst_, n0, row):
                eng.wait_ge(row_in, 16 * row)
                for i in range(NT):
                    eng.wait_ge(J.ps, n0 + i + 1)
                    eng.tensor_tensor(dst_[0:P, i, :], ps[0:P, 6 + i % 2, :], brow[0:P, :], ALU.add).then_inc(J.v, 1)
                eng.wait_ge(J.v, n0 + NT)
                eng.sem_inc(row_free, 1)

            def aggregate(layer):
                A, L = ag[layer], (ln1, ln2)[layer]
                with eng.Fori(0, NT // 2) as i2:
                    c = Chain(eng, L.lk, (16 if layer else 4) * i2)
                    for b in range(2):
                        for h in range(2):
                            i = 2 * i2 + b
                            eng.wait_ge(A.hi, 2 * i + h + 1)
                            eng.tensor_tensor(AS[1][h], AT[0:P, 5 * h:5 * h + 5, ds(i * P, P)], AS[0][h].bitcast(F32),
                                              ALU.subtract).then_inc(A.lo, 1)
                    for b in range(2):
                        i = 2 * i2 + b
                        rc = rcnt[0:P, ds(i, 1), :].rearrange("p a c -> p (a c)")
                        rw = RW[0:P, ds(i, 1), :].rearrange("p a f -> p (a f)")
                        eng.wait_ge(A.pe, 2 * i + 4)
                        if layer == 0:
                            c(eng.tensor_scalar(cntm[0:P, b:b + 1], ps[0:P, 2 + b, 0:1], 1.0, None, ALU.max))
                            c(eng.reciprocal(rc, cntm[0:P, b:b + 1]))
                            eng.wait_ge(L.tr, i + 1)
                            eng.scalar_tensor_tensor(out=TB[0:P, b, :], in0=ps[0:P, b, :], scalar=rc, in1=rw,
                                                     op0=ALU.mult, op1=ALU.add).then_inc(L.nrm, 1)
                            eng.wait_ge(L.nrm, i + 1)
                            eng.sem_inc(A.dv, 1)
                            continue
                        c(eng.scalar_tensor_tensor(out=rw, in0=ps[0:P, b, :], scalar=rc, in1=rw, op0=ALU.mult, op1=ALU.add))
                        eng.sem_inc(A.dv, 1)
                        eng.wait_ge((L.src0, L.src1)[b], 16 * i2 + 16)
                        c(eng.tensor_tensor(rw, rw, TB[0:P, b, :], ALU.add))
                        stat(L, b, i2, rw, c)
                        eng.wait_ge(L.std, 2 * i + 1)
                        c(eng.reciprocal(sd[0:P, b, 1:2], sd[0:P, b, 0:1]))
                        m1 = mr1[0:P, ds(i, 1), :].rearrange("p a c -> p (a c)")
                        eng.tensor_copy(m1[:, 0:1], mv[0:P, b, 0:1]).then_inc(L.lk, 1)
                        eng.tensor_copy(m1[:, 1:2], sd[0:P, b, 1:2]).then_inc(L.lk, 1)
                        eng.tensor_scalar(TB[0:P, b, :], rw, mv[0:P, b, 0:1], sd[0:P, b, 1:2],
                                          ALU.subtract, ALU.mult).then_inc(ysum, 1)
                        c.n += 2
                        eng.wait_ge(ysum, i + 1)
                        stat(L, b, i2, TB[0:P, b, :], c)
                        eng.wait_ge(L.std, 2 * i + 2)
                        c(eng.reciprocal(sd[0:P, b, 1:2], sd[0:P, b, 0:1]))
                        eng.wait_ge(L.tr, i + 2)
                        eng.tensor_scalar(TB[0:P, 2, :], TB[0:P, b, :], mv[0:P, b, 0:1], sd[0:P, b, 1:2],
                                          ALU.subtract, ALU.mult).then_inc(L.nrm, 1)

            pair = eng.alloc_register("pair")
            eng.reg_mov(pair, 0)
            for seg in range(SEG):
                with eng.Fori(NW // SEG * seg, NW // SEG * (seg + 1)) as w:
                    first = eng.value_load(win[0:1, ds(2 * w, 1)], min_val=0, max_val=EP // EG - 1)
                    end = eng.value_load(win[0:1, ds(2 * w + 1, 1)], min_val=1, max_val=EP // EG)
                    with eng.Fori(first, end) as c:
                        now = eng.snap(pair)
                        slot = eng.snap(now & (RING - 1))
                        eng.wait_ge(oh_used, now + 1)
                        eng.tensor_tensor(oh_lo[:, ds(slot, 1), :, :].rearrange("p a g c -> p (a g) c"),
                                          iota_b[:, 0:128].unsqueeze(1).to_broadcast([P, EG, 128]),
                                          loT[:, ds(c * EG, EG)].unsqueeze(2).to_broadcast([P, EG, 128]),
                                          ALU.is_equal).then_inc(oh_ready, 1)
                        eng.scalar_tensor_tensor(out=oh_key[:, ds(slot, 1), :, :].rearrange("p a g c -> p (a g) c"),
                                                 in0=iota_b[:, 0:WK].unsqueeze(1).to_broadcast([P, EG, WK]),
                                                 scalar=woff[:, ds(w, 1)],
                                                 in1=keyT[:, ds(c * EG, EG)].unsqueeze(2).to_broadcast([P, EG, WK]),
                                                 op0=ALU.add, op1=ALU.is_equal).then_inc(oh_ready, 1)
                        eng.reg_add(pair, pair, 1)
                if seg:
                    rows_lo(pj["g"], 0, NT // SEG * (seg - 1), NT // SEG * seg)
            rows_lo(pj["g"], 0, NT - NT // SEG, NT)
            rows_bias(pj["g"], RW, NT, 1)
            aggregate(0)
            eng.wait_ge(ln1.ev, NT + 2)
            cut_lo(sp["h"], lambda k: ZT[:, k, :], X0)
            rows_lo(pj["g"], NT)
            rows_bias(pj["g"], RW, 3 * NT, 2)
            aggregate(1)

            eng.wait_ge(r.l, 1)
            link = Chain(eng, r.lk)
            link(eng.tensor_tensor(rt[0:1, 24:32], ps[0:1, 5, 16:24], rt[0:1, 8:16], ALU.add))
            for j in range(2):
                lg = rt[0:1, 24 + 4 * j:28 + 4 * j]
                link(eng.tensor_reduce(out=rt[0:1, 32:33], in_=lg, op=ALU.max, axis=AX.X))
                link(eng.scalar_tensor_tensor(out=rt[0:1, 36:40], in0=lg, scalar=rt[0:1, 32:33], in1=rt[0:1, 16:20],
                                              op0=ALU.is_equal, op1=ALU.mult))
                link(eng.tensor_reduce(out=rt[0:1, 33:34], in_=rt[0:1, 36:40], op=ALU.max, axis=AX.X))
                eng.tensor_scalar(idx_i[0:1, j:j + 1], rt[0:1, 33:34], -1.0, 4.0, ALU.mult, ALU.add).then_inc(r.i, 1)

            def scaled_bias(n, came):
                eng.wait_ge(came, 16)
                eng.tensor_scalar(bcol_q[:], bcol[:, 0:4], SCALE, None, ALU.mult).then_inc(biasq, 1)

            def attend(K):
                eng.sem_inc(A.negmax, 2 * NT)
                eng.sem_inc(A.lo, K.total)
                eng.sem_inc(A.tr, K.total)
                eng.sem_inc(A.pv, 2 * HG)
                eng.sem_inc(A.diag, 2 * HG)
                eng.sem_inc(A.bc, 2 * HG)
                eng.sem_inc(A.post, 2 * HG)
                if K.causal:
                    eng.wait_ge(mask_ok, 2)

                def greatest(c, n):
                    eng.wait_ge(A.scores, K.tile(c.hp, n))
                    i = n % NT
                    if K.causal:
                        block_ = flat(n % 2)[0:P, P * i:P * i + P]
                        c(eng.tensor_tensor(block_, block_, mask, ALU.add))
                    eng.tensor_reduce(out=ngm[0:P, n % 2:n % 2 + 1], in_=flat(n % 2)[0:P, 0:K.cols[i]], op=ALU.max,
                                      axis=AX.X, negate=True).then_inc(A.negmax, 1)

                def probs_lo(hp, n):
                    g = n // 2
                    for bank in range(K.banks[n]):
                        nb = min(4, K.blocks[n] - 4 * bank)
                        blk = (slice(None), g % 2, slice(4 * bank, 4 * bank + nb), n % 2, slice(0, P))
                        eng.wait_ge(A.hi, K.bank(hp, n, bank))
                        eng.tensor_tensor(PT[1][blk],
                                          ps[0:P, 3 * (n % 2) + bank, 0:P * nb].rearrange("p (c t) -> p c t", c=nb),
                                          PT[0][blk].bitcast(F32), ALU.subtract).then_inc(A.lo, 1)

                def inverse(c, hp, g):
                    eng.wait_ge(A.exp, K.tile(hp, 2 * g + 1))
                    k = 2 * g % 4
                    c(eng.reciprocal(rr[0:P, :], rs[0:P, k:k + 2]))
                    for s in range(2):
                        ins = eng.tensor_scalar(diag[0:P, s, :], ident[0:P, 0:P], rr[0:P, s:s + 1], None, ALU.mult)
                    ins.then_inc(A.diag, 1)

                def output(c, hp, g):
                    b, gh = g // HG, g % HG
                    eng.wait_ge(A.bot, K.group(hp, g))
                    c(eng.tensor_tensor(comb, ps[0:HD, 6, 0:252], comb, ALU.add))
                    eng.wait_ge(A.bc, K.group(hp, g))
                    o = ZT[64 * b:64 * b + 64, ds(hp, 1), 2 * P * gh:2 * P * gh + 2 * P].rearrange("p a (s t) -> p (a s) t", s=2)
                    eng.tensor_tensor(o, ps[0:HD, 7, 0:2 * P].rearrange("p (s t) -> p s t", s=2),
                                      comb.rearrange("p (s t) -> p s t", s=2)[:, :, 0:P], ALU.mult).then_inc(A.post, 1)

                def body(hp, last):
                    c = Chain(eng, A.lk, K.links0 + int(K.causal) + K.links * hp)
                    c.hp = hp
                    for n in range(2 * NT):
                        if not (last and n == 2 * NT - 1):
                            greatest(c, n + 1)
                        probs_lo(hp, n)
                        if n % 2 == 0 and n >= 2:
                            output(c, hp, n // 2 - 1)
                        if n % 2 == 1:
                            inverse(c, hp, n // 2)
                    output(c, hp, 2 * HG - 1)
                    assert last or c.n == K.links
                c0 = Chain(eng, A.lk, K.links0)
                c0.hp = 0
                greatest(c0, 0)
                with eng.Fori(0, H // 2 - 1) as hp:
                    body(hp, False)
                body(H // 2 - 1, True)

            def clear_pads():
                for p in range(2):
                    for s in range(2):
                        ins = eng.memset(PT[p][:, :, :, s, P:P + 1].rearrange("p g c t -> p g (c t)").bitcast(F32), 0.0)
                        ins.then_inc(pad_ok, 1)

            def out_val(J, unit, n0, residual=False):
                for m in range(4):
                    eng.wait_ge(w_used, unit + m + 1)
                    if residual:
                        ins = eng.scalar_tensor_tensor(out=PB[:, m % 2, :], in0=flat(m % 2)[:, 0:T],
                                                       scalar=ocol[:, m:m + 1], in1=XR[:, m, :], op0=ALU.add, op1=ALU.add)
                    else:
                        ins = eng.tensor_scalar(PB[:, m % 2, :], flat(m % 2)[:, 0:T], ocol[:, m:m + 1], None, ALU.add)
                    ins.then_inc(J.v, 1)
                    eng.wait_ge(J.a, n0 + m + 1)
                    eng.tensor_tensor(X0[1][:, m, :], PB[:, m % 2, :], X0[0][:, m, :].bitcast(F32), ALU.subtract
                                      ).then_inc(J.t, 1)

            eng.wait_ge(small_in, 64)
            eng.wait_ge(r.h, 1)
            cut_affine(sp["s"], 0, 1, X0)
            scaled_bias(1, bcol_in[0])
            rows_bias(pj["v"], V, 0 * NT, 3)
            clear_pads()
            attend(KS_)
            cut_lo(sp["os"], lambda k: ZT[:, k, :], X1)
            eng.wait_ge(ocol_in[0], 16)
            out_val(pj["u"], UNIT["us"], 0)
            scaled_bias(2, bcol_in[1])
            eng.wait_ge(zt_in, 16)
            eng.wait_ge(pj["u"].t, 4)
            cut_affine(sp["t"], 2, 3, X0, stored=True)
            scaled_bias(3, bcol_in[2])
            rows_bias(pj["v"], V, 1 * NT, 4)
            clear_pads()
            attend(KT_)
            cut_lo(sp["ot"], lambda k: ZT[:, k, :], X1)
            eng.wait_ge(ocol_in[1], 16)
            eng.wait_ge(xr_in, 16)
            out_val(pj["u"], UNIT["ut"], 4, residual=True)
            rows_bias(pj["v"], V, 2 * NT, 5)
            clear_pads()
            attend(KC_)
            cut_lo(sp["oc"], lambda k: ZT[:, k, :], X1)
            eng.wait_ge(row_in, 16 * 6)
            J = pj["uc"]
            c = Chain(eng, ln3.lk)
            for i in range(NT):
                b = i % 2
                y = PB[0:P, b, 0:D]
                eng.wait_ge((ln3.src0, ln3.src1)[b], 16 * (i // 2 + 1))
                c(eng.tensor_scalar(y, TB[0:P, b, :], mr1[0:P, i, 0:1], mr1[0:P, i, 1:2], ALU.subtract, ALU.mult))
                c(eng.tensor_tensor(y, y, brow[0:P, :], ALU.add))
                eng.wait_ge(J.ps, i + 1)
                eng.tensor_tensor(y, ps[0:P, 6 + b, :], y, ALU.add).then_inc(J.v, 1)
                eng.wait_ge(J.v, i + 1)
                c(eng.tensor_tensor(ACC[0:P, i, :], y, TB[0:P, b, :], ALU.add))
                stat(ln3, b, 0, y, c)
                eng.wait_ge(ln3.std, i + 1)
                c(eng.reciprocal(sd[0:P, b, 1:2], sd[0:P, b, 0:1]))
                eng.tensor_scalar(TB[0:P, b, :], y, mv[0:P, b, 0:1], sd[0:P, b, 1:2], ALU.subtract, ALU.mult
                                  ).then_inc(ln3.nrm, 1)
            eng.sem_inc(row_free, 1)
            eng.wait_ge(ln3.ev, NT + 2)
            cut_affine(sp["m"], 4, 5, X0)
            eng.wait_ge(row_in, 16 * 7)
            for i in range(NT):
                eng.tensor_tensor(ACC[0:P, i, :], ACC[0:P, i, :], brow[0:P, :], ALU.add).then_inc(pj["m2"].a, 1)
            eng.wait_ge(pj["m2"].a, NT)

            def mlp(q):
                J1, J2 = pj["m1"], pj["m2"]
                for m in range(4):
                    eng.wait_ge(J1.a, 4 * q + m + 1)
                    if m == 0 and not isinstance(q, int):
                        eng.wait_ge(J2.ps, NT * q)
                    eng.tensor_scalar(X1[0][:, m, :], PB[:, m % 2, :], 1.0, None, ALU.mult).then_inc(J1.v, 1)
                    eng.wait_ge(J1.v, 4 * q + m + 1)
                    eng.tensor_tensor(X1[1][:, m, :], PB[:, m % 2, :], X1[0][:, m, :].bitcast(F32), ALU.subtract
                                      ).then_inc(J1.t, 1)
                for i in range(NT):
                    eng.wait_ge(J2.ps, NT * q + i + 1)
                    ins = eng.tensor_tensor(ACC[0:P, i, :], ps[0:P, 6 + i % 2, :], ACC[0:P, i, :], ALU.add)
                    ins.then_inc(J2.v, 1)
            mlp(0)
            with eng.Fori(1, NQ - 1) as q:
                mlp(q)
            J1, J2 = pj["m1"], pj["m2"]
            q = NQ - 1
            eng.wait_ge(J2.ps, NT * q)
            for m in range(4):
                eng.wait_ge(J1.a, 4 * q + m + 1)
                eng.tensor_scalar(X1[0][:, m, :], PB[:, m % 2, :], 1.0, None, ALU.mult).then_inc(J1.v, 1)
                eng.wait_ge(J1.v, 4 * q + m + 1)
                eng.tensor_tensor(X1[1][:, m, :], PB[:, m % 2, :], X1[0][:, m, :].bitcast(F32), ALU.subtract
                                  ).then_inc(J1.t, 1)
            eng.wait_ge(J2.v, NT * q)
            for i in range(NT):
                eng.wait_ge(J2.ps, NT * q + i + 1)
                eng.tensor_tensor(ACC[0:P, i, :], ps[0:P, 6 + i % 2, :], ACC[0:P, i, :], ALU.add).then_inc(fin, 1)
                eng.wait_ge(fin, i + 1)
                eng.sem_inc(J2.v, 1)


def kernel(**inputs):
    import numpy as np
    import concourse.bacc as bacc
    from concourse.bass_utils import run_bass_kernel_spmd

    a = {k: np.asarray(v) for k, v in inputs.items()}
    f = {k[7:]: v for k, v in a.items() if k.startswith("L0_ffn_")}

    def by_rows(w):
        return w.T.reshape(-1, 128, w.shape[0]).reshape(-1, 128, 512)

    def by_blocks(w):
        return w.reshape(-1, 128, KC, 128).transpose(0, 3, 2, 1).reshape(-1, 128, 512)

    def by_cols(b):
        return b.reshape(-1, 128).T

    units = [by_rows(a[n]) for n in ("L0_gnn_W1_l", "L0_gnn_W1_r", "L0_gnn_W2_l", "L0_gnn_W2_r")]
    for n in range(NEXP):
        w = f["sp_in_w"][n]
        units += [by_blocks(w[0:D]), by_blocks(w[D:2 * D]), by_rows(w[2 * D:]), by_blocks(f["sp_out_w"][n])]
    for n in range(NEXP):
        units += [by_blocks(f["tq_w"][n]), by_blocks(f["tk_w"][n]), by_rows(f["tv_w"][n]), by_blocks(f["tp_w"][n])]
    w = f["cross_in_w"]
    units += [by_blocks(w[0:D]), by_blocks(w[D:2 * D]), by_rows(w[2 * D:]), by_rows(f["cross_out_w"])]
    units += [by_blocks(f["mlp_w1"]), by_rows(f["mlp_w2"])]
    qkv = [by_cols(f["sp_in_b"][n]) for n in range(NEXP)]
    qkv += [by_cols(np.concatenate([f["tq_b"][n], f["tk_b"][n], f["tv_b"][n]])) for n in range(NEXP)]
    qkv += [by_cols(f["cross_in_b"])]
    outs = [by_cols(f["sp_out_b"][n]) for n in range(NEXP)] + [by_cols(f["tp_b"][n]) for n in range(NEXP)]
    row_bias = [a["L0_gnn_b1"], a["L0_gnn_b2"]] + [f["sp_in_b"][n][2 * D:] for n in range(NEXP)]
    row_bias += [f["tv_b"][n] for n in range(NEXP)] + [f["cross_in_b"][2 * D:], f["cross_out_b"], f["mlp_b2"]]
    data = {
        "x": a["x"].reshape(NT, P, D),
        "src": a["src"],
        "dst": a["dst"],
        "weights": np.concatenate(units),
        "qkv_bias": np.stack(qkv),
        "out_bias": np.stack(outs),
        "row_bias": np.stack(row_bias),
        "ln_cols": np.stack([by_cols(f[n]) for n in ("norm_s_w", "norm_s_b", "norm_t_w", "norm_t_b",
                                                     "norm_mlp_w", "norm_mlp_b")], axis=1),
        "mlp_b1": by_cols(f["mlp_b1"]),
        "router_w1": f["router_w1"].T.reshape(KC, 128, 128).transpose(1, 0, 2).reshape(128, D),
        "router_w2": f["router_w2"].T,
        "router_b1": f["router_b1"].reshape(128, 1),
        "router_b2": f["router_b2"].reshape(1, 2 * NEXP),
    }
    nc = bacc.Bacc("TRN2", target_bir_lowering=False, num_devices=1)
    arrays, args = {}, []
    for name, v in data.items():
        v = np.ascontiguousarray(v)
        arrays[f"in_{name}"] = v
        args.append(nc.dram_tensor(f"in_{name}", v.shape, mybir.dt.from_np(v.dtype), kind="ExternalInput").ap())
    out = nc.dram_tensor("out_x", (NT, P, D), F32, kind="ExternalOutput").ap()
    gnn_ffn_program(nc, *args, out)
    got = run_bass_kernel_spmd(nc, [arrays], core_ids=[0])
    return got.results[0]["out_x"].reshape(T, D)
```

```python
from collections import namedtuple
from contextlib import ExitStack

import concourse.bass as bass
from concourse import mybir

F32 = mybir.dt.float32
F32R = mybir.dt.float32r
BF16 = mybir.dt.bfloat16
I32 = mybir.dt.int32
ALU = mybir.AluOpType
ACT = mybir.ActivationFunctionType
AX = mybir.AxisListType
ds = bass.ds

T, D, H, HD, NEXP = 1250, 512, 8, 64, 4
P = 125
NT = T // P
KC = D // 128
E = 41250
EC = E // P
EQ, EJ = 110, 3
WD = 25
NW = T // WD
WK = WD * NT
EPS = 1e-5
SCALE = float(HD) ** -0.5
BANK = 512
CHUNKS = [(0, 512), (512, 512), (1024, 226)]
EG = 4
EP = -(-EC // EG) * EG
RING = 2
SEG = 5
HG = NT // 2
NQ = 4

ORDER = ["g1l", "g1r", "g2l", "g2r", "qs", "ks", "vs", "us", "qc", "qt", "kt", "vt", "ut", "kc", "vc", "uc"]
UNIT = {n: 4 * i for i, n in enumerate(ORDER)}
UNIT["mlp"] = 4 * len(ORDER)
G0, S0 = 0, 16
T0 = S0 + 16 * NEXP
C0 = T0 + 16 * NEXP
M0 = C0 + 16
ROWB = dict(g1=0, g2=1, vs=2, vt=2 + NEXP, vc=2 + 2 * NEXP, uc=3 + 2 * NEXP, m2=4 + 2 * NEXP)


def Sems(make, prefix, names):
    names = names.split()
    return namedtuple(prefix, names)(*[make(f"{prefix}_{n}") for n in names])


class Chain:

    def __init__(self, eng, sem, base=0):
        self.eng, self.sem, self.base, self.n = eng, sem, base, 0

    def __call__(self, ins):
        self.n += 1
        ins.then_inc(self.sem, 1)
        self.eng.wait_ge(self.sem, self.base + self.n)


class Attn:

    def __init__(self, turn, causal):
        self.turn, self.causal = turn, causal
        self.blocks = [i + 1 if causal else NT for i in range(NT)] * 2
        self.banks = [(b + 3) // 4 for b in self.blocks]
        self.cols = [P * b for b in self.blocks]
        self.parts = [1 + (c > BANK) for c in self.cols]
        self.cum = [sum(self.banks[:n]) for n in range(2 * NT + 1)]
        self.cum_parts = [sum(self.parts[:n]) for n in range(2 * NT + 1)]
        self.total = self.cum[-1]
        self.total_parts = self.cum_parts[-1]
        full, half = 6 * NT, 2 * sum((i + 4) // 4 for i in range(NT))
        self.tiles0 = 2 * NT * (H // 2 + 1) * turn
        self.groups0 = 2 * HG * (H // 2 + 1) * turn
        self.banks0 = (H // 2 + 1) * (0, full, full + half)[turn]
        full, half = 4 * NT, 2 * sum(1 + (P * (i + 1) > BANK) for i in range(NT))
        self.parts0 = (H // 2 + 1) * (0, full, full + half)[turn]
        self.cuts0 = 7 * H * turn
        self.qin0 = 32 * H * turn
        full, half = 6 * HG, 4 * HG + 2 * sum(P * (2 * g + 1) > BANK for g in range(HG)) + 2 * NT
        self.links = half if causal else full
        self.links0 = H // 2 * (0, full, full + half)[turn]

    def tile(self, hp, n):
        return self.tiles0 + 2 * NT * (hp + 1) + n + 1

    def bank(self, hp, n, b):
        return self.banks0 + self.total * (hp + 1 + n // (2 * NT)) + self.cum[n % (2 * NT)] + b + 1

    def part(self, hp, n, p):
        return (self.parts0 + self.total_parts * (hp + 1 + n // (2 * NT)) + self.cum_parts[n % (2 * NT)] + p + 1)

    def group(self, hp, g):
        return self.groups0 + 2 * HG * (hp + 1) + g + 1


def gnn_ffn_program(nc, x, src, dst, weights, qkv_bias, out_bias, row_bias, ln_cols, mlp_b1,
                    router_w1, router_w2, router_b1, router_b2, out):
    with ExitStack() as ctx:
        def sb(name, shape, dt=F32):
            return ctx.enter_context(nc.sbuf_tensor(name, shape, dt))

        def sem(name):
            return ctx.enter_context(nc.semaphore(name))

        F = sb("F", [128, 22620])
        R = sb("R", [128, 22740], F32R)
        w_raw = sb("w_raw", [128, 2, 512])
        w_hi = sb("w_hi", [128, 4, 512], F32R)
        w_lo = sb("w_lo", [128, 4, 512], F32R)
        TB = sb("TB", [128, 3, 512])
        brow = sb("brow", [128, 512])
        ident = sb("ident", [128, 128])
        ones = sb("ones", [128, HD])
        ones_r = sb("ones_r", [128, 2], F32R)
        bcol = sb("bcol", [128, 12])
        bcol_q = sb("bcol_q", [128, 4])
        ocol = sb("ocol", [128, 4])
        lncol = sb("lncol", [128, 6, 4])
        b1col = sb("b1col", [128, 16])
        stats = sb("stats", [128, 2, 6])
        mv = sb("mv", [128, 2, 2])
        sd = sb("sd", [128, 2, 2])
        mr1 = sb("mr1", [128, NT, 2])
        rcnt = sb("rcnt", [128, NT, 1])
        cntm = sb("cntm", [128, 2])
        ngm = sb("ngm", [128, 2])
        rs = sb("rs", [128, 2, 4])
        rr = sb("rr", [128, 2])
        rt = sb("rt", [128, 48])
        eps_t = sb("eps_t", [128, 1])
        zero = sb("zero", [128, 1])
        idx_i = sb("idx_i", [1, 2], I32)
        win = sb("win", [1, 2 * NW], I32)
        wide = sb("wide", [1, NW + 1])
        many = sb("many", [1, 1], I32)
        ps = ctx.enter_context(nc.psum_tensor("ps", [128, 8, BANK], F32))

        def flat(a):
            return ps[:, 3 * a:3 * a + 3, :].rearrange("p a b -> p (a b)")

        def rows(a):
            return a.rearrange("p (i f) -> p i f", i=NT)

        def cols(a):
            return a.rearrange("p (k t) -> p k t", k=KC)

        AT = F[:, 0:12500].rearrange("p (h d) -> p h d", h=NT)
        RW = rows(F[:, 12500:17620])
        ZT = cols(F[:, 17620:22620])
        e_base = 12500

        def eview(off, n, parts=P):
            return F[0:parts, e_base + off:e_base + off + n]
        s_i = eview(0, 375, EQ).bitcast(I32)
        d_i = eview(375, 375, EQ).bitcast(I32)
        s_f = eview(750, 375, EQ)
        d_f = eview(1125, 375, EQ)
        h_f = eview(1500, 375, EQ)
        l_f = eview(0, 375, EQ)
        k_f = eview(375, 375, EQ)
        mm2 = eview(1875, 6, EQ)
        loT = eview(1882, EP)
        keyT = eview(2214, EP)
        wcol = eview(2546, 8, NW)
        woff = eview(2554, NW)
        iota_b = eview(2604, 128).bitcast(BF16)
        zero_b = eview(2732, 125).bitcast(BF16)
        oh_key = eview(2858, RING * EG * 125).bitcast(BF16).rearrange("p (r g c) -> p r g c", r=RING, g=EG)
        oh_lo = eview(3858, RING * EG * 64).bitcast(BF16).rearrange("p (r g c) -> p r g c", r=RING, g=EG)
        dbc = eview(2858, 2 * EC, NW)
        msk = eview(3518, EC, NW)
        cid = eview(4370, EP, NW)
        QK = F[:, 0:10000].rearrange("p (j m t) -> p j m t", j=2, m=KC)
        V = rows(F[:, 10000:15120])
        XR = cols(F[:, 10000:15000])
        PB = F[:, 15120:17620].rearrange("p (b t) -> p b t", b=2)
        ACC = rows(F[:, 0:5120])
        w1r = F[:, 15120:15632]
        w2r = F[:, 15632:15640]
        prow = F[0:1, 15700:16212]
        diag = TB[:, 0, 0:250].rearrange("p (s t) -> p s t", s=2)
        comb = TB[0:HD, 1, 0:252]
        mask = TB[0:P, 0, 256:256 + P]

        X0 = (cols(R[:, 0:5000]), cols(R[:, 5000:10000]))
        X1 = (cols(R[:, 10000:15000]), cols(R[:, 15000:20000]))
        Y = (rows(R[:, 10000:15120]), rows(R[:, 15120:20240]))
        AS = [[R[0:P, 20240 + 1250 * p + 625 * h:20240 + 1250 * p + 625 * h + 625]
               .rearrange("p (c d) -> p c d", c=5) for h in range(2)] for p in range(2)]
        HB = 10080
        QSH = [R[:, HB:HB + 1250], R[:, HB + 1250:HB + 2500]]
        QSL = [R[:, HB + 2500:HB + 3750], R[:, HB + 3750:HB + 5000]]
        KS = [R[:, HB + 5000:HB + 6250], R[:, HB + 6250:HB + 7500]]
        VS = [R[0:P, HB + 7500 + 1280 * b:HB + 8780 + 1280 * b].rearrange("p (c n) -> p c n", c=NT) for b in range(2)]
        KT = R[:, HB + 10060:HB + 10060 + 1250]
        PT = [R[0:P, 5040 * p:5040 * p + 5040]
              .rearrange("p (g c s t) -> p g c s t", g=2, c=NT, s=2) for p in range(2)]

        mm_d = nc.dram_tensor("mm_d", [2, EC], F32, kind="Internal").ap()
        x1_d = nc.dram_tensor("x1_d", [NT, P, D], F32, kind="Internal").ap()
        zt_d = nc.dram_tensor("zt_d", [128, KC, T], F32, kind="Internal").ap()
        xt_d = nc.dram_tensor("xt_d", [128, KC, T], F32, kind="Internal").ap()
        qc_d = nc.dram_tensor("qc_d", [128, KC, T], F32, kind="Internal").ap()

        const_ok, small_in, w_split, w_used = (sem(n) for n in ("const_ok", "small_in", "w_split", "w_used"))
        w_in = [sem("w_in0"), sem("w_in1")]
        ln_names = "src0 src1 var std nrm tr ev lk"
        ln0, ln2, ln3 = (Sems(sem, n, ln_names) for n in ("lnx", "lnz", "lnm"))
        ln1 = Sems(sem, "h", "nrm tr ev lk")
        sp = {n: Sems(sem, "cut_" + n, names) for n, names in
              dict(x="hi lo", h="hi lo", s="val hi lo", os="hi lo", t="val hi lo st0 st1", ot="hi lo", oc="hi lo",
                   m="val hi lo").items()}
        pj = {n: Sems(sem, "prod_" + n, names) for n, names in
              dict(g="ps a v", qk="a", v="ps v", u="a v t", uc="ps v", m1="a v t", m2="ps a v").items()}
        A = Sems(sem, "att", "qin0 qin1 cut scores negmax exp tr hi lo pv diag bc bot post lk")
        KS_, KT_, KC_ = Attn(0, False), Attn(1, True), Attn(2, False)
        ag = [Sems(sem, f"agg{n}", "hi lo pe cnt dv") for n in range(2)]
        e = Sems(sem, "edge", "in_ lk tr mm mmd mmi w win ev many")
        oh_ready, oh_used, at_ready, at_free = (sem(n) for n in ("oh_ready", "oh_used", "at_ready", "at_free"))
        r = Sems(sem, "router", "in_ sums row tr col h he l i lk")
        bcol_in = [sem(f"bcol_in{i}") for i in range(4)]
        ocol_in = [sem(f"ocol_in{i}") for i in range(2)]
        row_in, row_free, xr_in, qc_st, qc_in, zt_in, x1_st, fin, out_st, biasq, pad_ok, mask_ok, ysum, zt_st, held = (
            sem(n) for n in ("row_in", "row_free", "xr_in", "qc_st", "qc_in", "zt_in", "x1_st", "fin", "out_st",
                             "biasq", "pad_ok", "mask_ok", "ysum", "zt_st", "held"))

        block = ctx.enter_context(nc.Block())

        @block.sync
        def _(eng):
            def load_units(unit, count, dram):
                for j in range(count):
                    if not isinstance(unit, int) or unit + j >= 2:
                        eng.wait_ge(w_split, 2 * (unit + j) - 2)
                    eng.dma_start(w_raw[:, j % 2, :], weights[ds(dram + j, 1), :, :].rearrange("a p c -> p (a c)")
                                  ).then_inc(w_in[j % 2], 16)

            def load_row(n, row):
                if n:
                    eng.wait_ge(row_free, n)
                eng.dma_start(brow[0:P, :], row_bias[ds(row, 1), :].to_broadcast([P, D])).then_inc(row_in, 16)

            def load_tiles(L, source):
                with eng.Fori(0, NT // 2) as i2:
                    for b in range(2):
                        eng.wait_ge(L.tr, 2 * i2 + b + 1)
                        eng.dma_start(TB[0:P, b, :], source[ds(2 * i2 + b, 1), :, :].rearrange("a p f -> p (a f)")
                                      ).then_inc((L.src0, L.src1)[b], 16)

            def load_heads(K):
                with eng.Fori(0, H // 2) as hp:
                    for b in range(2):
                        eng.wait_ge(A.scores, K.tile(hp, NT * (b - 1) - 1))
                        for half in range(2):
                            for j, t in ((0, QSL), (1, KS)):
                                eng.dma_start(t[b][64 * half:64 * half + 64, :].bitcast(F32),
                                              QK[64 * b:64 * b + 64, j, ds(hp, 1), :].rearrange("p a t -> p (a t)")
                                              ).then_inc((A.qin0, A.qin1)[b], 16)

            eng.dma_start(s_i, src.rearrange("(q r) -> q r", q=EQ)).then_inc(e.in_, 16)
            eng.dma_start(d_i, dst.rearrange("(q r) -> q r", q=EQ)).then_inc(e.in_, 16)
            load_tiles(ln0, x)
            eng.dma_start(lncol[:], ln_cols).then_inc(small_in, 16)
            eng.dma_start(b1col[:], mlp_b1).then_inc(small_in, 16)
            eng.dma_start(rt[:, 0:1], router_b1).then_inc(small_in, 16)
            eng.dma_start(rt[0:1, 8:16], router_b2).then_inc(small_in, 16)
            eng.wait_ge(e.mm, 2)
            eng.dma_start(mm_d.rearrange("m (q j) -> q m j", j=EJ), mm2.rearrange("q (m j) -> q m j", m=2)
                          ).then_inc(e.mmd, 16)
            eng.wait_ge(e.mmd, 16)
            eng.dma_start(dbc, mm_d.rearrange("m c -> (m c)").unsqueeze(0).to_broadcast([NW, 2 * EC])
                          ).then_inc(e.mmi, 16)
            eng.wait_ge(e.w, 2)
            eng.dma_start(win[:, :].rearrange("a (w c) -> a w c", c=2), wcol[:, 6:8].bitcast(I32)).then_inc(e.win, 16)
            load_row(0, ROWB["g1"])
            load_units(0, 16, G0)
            load_row(1, ROWB["g2"])
            load_tiles(ln2, x)
            with eng.Fori(0, NT) as i:
                eng.wait_ge(ysum, i + 1)
                eng.dma_start(x1_d[ds(i, 1), :, :].rearrange("a p f -> p (a f)"),
                              RW[0:P, ds(i, 1), :].rearrange("p a f -> p (a f)")).then_inc(x1_st, 16)
            eng.wait_ge(x1_st, 16 * NT)
            eng.dma_start(w1r, router_w1).then_inc(r.in_, 16)
            eng.dma_start(w2r, router_w2).then_inc(r.in_, 16)
            eng.wait_ge(r.i, 2)
            e_s = eng.value_load(idx_i[0:1, 0:1], min_val=0, max_val=NEXP - 1)
            e_t = eng.value_load(idx_i[0:1, 1:2], min_val=0, max_val=NEXP - 1)
            eng.dma_start(bcol[:], qkv_bias[ds(e_s, 1), :, :].rearrange("a p c -> p (a c)")).then_inc(bcol_in[0], 16)
            eng.dma_start(ocol[:], out_bias[ds(e_s, 1), :, :].rearrange("a p c -> p (a c)")).then_inc(ocol_in[0], 16)
            load_row(2, e_s + ROWB["vs"])
            load_units(UNIT["qs"], 4, e_s * 16 + S0)
            eng.dma_start(zt_d, ZT).then_inc(zt_st, 16)
            load_units(UNIT["ks"], 8, e_s * 16 + (S0 + 4))
            eng.wait_ge(pj["qk"].a, 8)
            eng.wait_ge(zt_st, 16)
            load_heads(KS_)
            load_units(UNIT["us"], 4, e_s * 16 + (S0 + 12))
            load_units(UNIT["qc"], 4, C0)
            eng.dma_start(bcol[:], qkv_bias[2 * NEXP, :, :]).then_inc(bcol_in[1], 16)
            load_row(3, e_t + ROWB["vt"])
            eng.wait_ge(sp["os"].lo, KC)
            eng.wait_ge(zt_st, 16)
            eng.dma_start(ZT, zt_d).then_inc(zt_in, 16)
            eng.wait_ge(pj["u"].v, 4)
            eng.dma_start(ocol[:], out_bias[ds(e_t + NEXP, 1), :, :].rearrange("a p c -> p (a c)")
                          ).then_inc(ocol_in[1], 16)
            load_units(UNIT["qt"], 4, e_t * 16 + T0)
            for m in range(4):
                eng.wait_ge(pj["qk"].a, 9 + m)
                eng.dma_start(qc_d[:, m, :], QK[:, 0, m, :]).then_inc(qc_st, 16)
            eng.dma_start(bcol[:], qkv_bias[ds(e_t + NEXP, 1), :, :].rearrange("a p c -> p (a c)")
                          ).then_inc(bcol_in[2], 16)
            for k in range(KC):
                eng.wait_ge(sp["t"].val, k + 1)
                eng.dma_start(xt_d[:, k, :], PB[:, k % 2, :]).then_inc((sp["t"].st0, sp["t"].st1)[k % 2], 16)
            load_units(UNIT["kt"], 8, e_t * 16 + (T0 + 4))
            eng.wait_ge(pj["qk"].a, 20)
            load_heads(KT_)
            load_units(UNIT["ut"], 4, e_t * 16 + (T0 + 12))
            eng.wait_ge(A.cut, 14 * H)
            eng.wait_ge(sp["t"].st0, 32)
            eng.wait_ge(sp["t"].st1, 32)
            eng.dma_start(XR, xt_d).then_inc(xr_in, 16)
            eng.dma_start(bcol[:], qkv_bias[2 * NEXP, :, :]).then_inc(bcol_in[3], 16)
            load_row(4, ROWB["vc"])
            eng.wait_ge(qc_st, 16 * 4)
            eng.dma_start(QK[:, 0, :, :], qc_d).then_inc(qc_in, 16)
            load_units(UNIT["kc"], 8, C0 + 4)
            eng.wait_ge(pj["qk"].a, 24)
            eng.wait_ge(qc_in, 16)
            load_heads(KC_)
            load_row(5, ROWB["uc"])
            load_units(UNIT["uc"], 4, C0 + 12)
            eng.wait_ge(sp["oc"].lo, KC)
            load_tiles(ln3, x1_d)
            load_row(6, ROWB["m2"])
            with eng.Fori(0, NQ) as q:
                load_units(q * 8 + UNIT["mlp"], 4, q * 4 + M0)
                load_units(q * 8 + (UNIT["mlp"] + 4), 4, q * 4 + (M0 + 16))
            for i in range(NT):
                eng.wait_ge(fin, i + 1)
                eng.dma_start(out[i, :, :], ACC[0:P, i, :]).then_inc(out_st, 16)
            eng.wait_ge(out_st, 16 * NT)

        @block.gpsimd
        def _(eng):
            eng.memset(ident[:], 0.0).then_inc(const_ok, 1)
            eng.memset(ones[:], 1.0).then_inc(const_ok, 1)
            eng.memset(ones_r[:].bitcast(F32), 1.0).then_inc(const_ok, 1)
            eng.memset(eps_t[:], EPS).then_inc(const_ok, 1)
            eng.memset(zero[:], 0.0).then_inc(const_ok, 1)
            eng.wait_ge(const_ok, 1)
            eng.affine_select(out=ident[:], in_=ident[:], compare_op=ALU.not_equal, fill=1.0, base=0,
                              pattern=[[-1, 128]], channel_multiplier=1).then_inc(const_ok, 1)
            for t, step, count, per_partition in ((iota_b[:, 0:250], 1, 250, 0), (woff, WK, NW, 0), (cid, 1, EP // EG, 0),
                                                  (wcol[:, 0:1], 1, 1, WD), (rt[0:1, 16:20], -1, 4, 0)):
                eng.iota(t, pattern=[[step, count]] + ([[0, EG]] if t is cid else []), base=4 if step < 0 else 0, channel_multiplier=per_partition,
                         allow_small_or_imprecise_dtypes=True).then_inc(const_ok, 1)
            eng.memset(zero_b, 0.0).then_inc(const_ok, 1)
            eng.memset(loT[:, EC:EP], 0.0).then_inc(const_ok, 1)
            eng.memset(keyT[:, EC:EP], -1.0).then_inc(const_ok, 1)

            def hi_part(to, a):
                return eng.tensor_tensor(to, a, zero[0:to.shape[0], :].to_broadcast(list(to.shape)), ALU.add)

            def cut_unit(u, s):
                if isinstance(u, int):
                    eng.wait_ge(w_in[s % 2], 16 * (u // 2 + 1))
                    if u >= 4:
                        eng.wait_ge(w_used, u - 3)
                else:
                    eng.wait_ge(w_in[s % 2], (u - s % 2) * 8 + 16)
                    eng.sem_inc(held, 1)
                    eng.wait_ge(w_used, u - 3)
                    eng.sem_inc(held, 1)
                hi_part(w_hi[:, s, :], w_raw[:, s % 2, :]).then_inc(w_split, 1)
                eng.wait_ge(w_split, 2 * u + 1)
                eng.tensor_tensor(w_lo[:, s, :], w_raw[:, s % 2, :], w_hi[:, s, :].bitcast(F32), ALU.subtract
                                  ).then_inc(w_split, 1)

            def cut_units(unit, end):
                for u in range(unit, end):
                    cut_unit(u, u % 4)

            def cut_heads(K):
                eng.sem_inc(A.scores, 2 * NT)
                with eng.Fori(0, H // 2) as hp:
                    for b in range(2):
                        n0 = K.cuts0 + 14 * hp + 7 * b
                        eng.wait_ge((A.qin0, A.qin1)[b], K.qin0 + 64 * hp + 64)
                        eng.sem_inc(held, 1)
                        hi_part(QSH[b], QSL[b].bitcast(F32)).then_inc(A.cut, 1)
                        eng.wait_ge(A.cut, n0 + 1)
                        eng.sem_inc(held, 1)
                        eng.tensor_tensor(KT[64:128, :], KS[b][64:128, :].bitcast(F32),
                                          zero[64:128, :].to_broadcast([64, T]), ALU.add).then_inc(A.cut, 1)
                        eng.wait_ge(A.cut, n0 + 2)
                        eng.sem_inc(held, 1)
                        hi_part(KS[b][0:64, :], KS[b][0:64, :].bitcast(F32)).then_inc(A.cut, 1)
                        eng.wait_ge(A.cut, n0 + 3)
                        eng.tensor_tensor(QSL[b], QSL[b].bitcast(F32), QSH[b].bitcast(F32), ALU.subtract
                                          ).then_inc(A.cut, 1)
                        eng.wait_ge(A.cut, n0 + 4)
                        eng.tensor_tensor(KS[b][64:128, :], KS[b][64:128, :].bitcast(F32), KT[64:128, :].bitcast(F32),
                                          ALU.subtract).then_inc(A.cut, 1)
                        eng.wait_ge(A.cut, n0 + 5)
                        eng.wait_ge(A.pv, K.group(hp, HG * (b - 1) - 1))
                        eng.sem_inc(held, 1)
                        eng.wait_ge(pj["v"].v, NT * (K.turn + 1))
                        vh = V[0:P, :, ds(128 * hp + 64 * b, 64)]
                        eng.tensor_copy(VS[b][:, :, 0:64], vh).then_inc(A.cut, 1)
                        eng.wait_ge(A.cut, n0 + 6)
                        eng.sem_inc(held, 1)
                        eng.tensor_tensor(VS[b][:, :, 64:128], vh, VS[b][:, :, 0:64].bitcast(F32), ALU.subtract
                                          ).then_inc(A.cut, 1)

            cut_units(0, UNIT["us"])
            cut_heads(KS_)
            cut_units(UNIT["us"], UNIT["ut"])
            eng.memset(mask, 0.0).then_inc(mask_ok, 1)
            eng.wait_ge(mask_ok, 1)
            eng.affine_select(out=mask, in_=mask, compare_op=ALU.is_ge, fill=-1e30, base=0,
                              pattern=[[-1, P]], channel_multiplier=1).then_inc(mask_ok, 1)
            cut_heads(KT_)
            cut_units(UNIT["ut"], UNIT["uc"])
            cut_heads(KC_)
            cut_units(UNIT["uc"], UNIT["mlp"])
            with eng.Fori(0, 2 * NQ) as q:
                for s in range(4):
                    cut_unit(q * 4 + (UNIT["mlp"] + s), s)

        @block.tensor
        def _(eng):
            def three(to, ah, al, bh, bl, first, last):
                eng.matmul(to, ah, bh, start=first, stop=False)
                eng.matmul(to, al, bh, start=False, stop=False)
                return eng.matmul(to, ah, bl, start=False, stop=last)

            def turn(L, b, i):
                eng.wait_ge(L.nrm, i + 1)
                eng.wait_ge(L.ev, i + 1)
                t = 2 if L is ln2 else b
                for k in range(KC):
                    ins = eng.transpose(ps[:, 6 + b, P * k:P * k + P], TB[0:P, t, 128 * k:128 * k + 128],
                                        ident[0:P, 0:P])
                ins.then_inc(L.tr, 1)

            def product_cols(J, unit, X, free, n0=0, k_ready=None, k0=0, last=None):
                for m in range(4):
                    eng.wait_ge(w_split, 2 * (unit + m) + 2)
                    if not isinstance(n0, int) or n0 + m >= 2:
                        eng.wait_ge(free, n0 + m - 1)
                    if last is not None and m < 2:
                        eng.wait_ge(last[0], last[1] - 1 + m)
                    for c, (lo, n) in enumerate(CHUNKS):
                        for k in range(KC):
                            if m == 0 and c == 0 and k_ready is not None:
                                eng.wait_ge(k_ready, k0 + k + 1)
                            wk = slice(128 * k, 128 * k + 128)
                            ins = three(flat(m % 2)[:, lo:lo + n], w_hi[:, m, wk], w_lo[:, m, wk],
                                        X[0][:, k, lo:lo + n], X[1][:, k, lo:lo + n], k == 0, k == KC - 1)
                    ins.then_inc(w_used, 1)

            def product_tile(J, i, unit, X, free, n0=0):
                if not isinstance(n0, int) or n0 + i >= 2:
                    eng.wait_ge(free, n0 + i - 1)
                tk = slice(P * i, P * i + P)
                for k in range(KC):
                    ins = three(ps[0:P, 6 + i % 2, :], X[0][:, k, tk], X[1][:, k, tk],
                                w_hi[:, k, :], w_lo[:, k, :], k == 0, k == KC - 1)
                ins.then_inc(J.ps, 1)

            def product_rows(J, unit, X, free, n0=0, ready=None):
                eng.wait_ge(w_split, 2 * (unit + 3) + 2)
                if ready is not None:
                    eng.wait_ge(ready, KC)
                for i in range(NT):
                    product_tile(J, i, unit, X, free, n0)
                eng.wait_ge(J.ps, n0 + NT)
                eng.sem_inc(w_used, 4)

            pair = eng.alloc_register("pair")

            def adjacency(first_w2, end_w2):
                with eng.Fori(first_w2, end_w2) as w2:
                    for j in range(2):
                        w = 2 * w2 + j
                        acc = ps[:, j, 0:WK]
                        first = eng.value_load(win[0:1, ds(2 * w, 1)], min_val=0, max_val=EP // EG - 1)
                        end = eng.value_load(win[0:1, ds(2 * w + 1, 1)], min_val=1, max_val=EP // EG)
                        eng.wait_ge(at_free, w + 1)
                        eng.matmul(acc, zero_b[:, 0:128], zero_b[:, 0:WK], start=True, stop=False)
                        with eng.Fori(first, end):
                            now = eng.snap(pair)
                            slot = eng.snap(now & (RING - 1))
                            eng.wait_ge(oh_ready, now * 2 + 2)
                            for g in range(EG):
                                ins = eng.matmul(acc, oh_lo[:, ds(slot, 1), g, :].rearrange("p a c -> p (a c)"),
                                                 oh_key[:, ds(slot, 1), g, :].rearrange("p a c -> p (a c)"),
                                                 start=False, stop=False)
                            ins.then_inc(oh_used, 1)
                            eng.reg_add(pair, pair, 1)
                        eng.matmul(acc, zero_b[:, 0:128], zero_b[:, 0:WK], start=False, stop=True).then_inc(at_ready, 1)

            def aggregate(layer, nlo):
                L, A = (ln1, ln2)[layer], ag[layer]

                def sums(i, b):
                    eng.wait_ge(A.dv, i + 1)
                    to, cnt = ps[0:P, b, :], ps[0:P, 2 + b, 0:2]

                    def chunk_hi(h, c):
                        k = 5 * h + c
                        eng.matmul(to, AS[0][h][:, c, :], Y[0][0:P, k, :], start=(k == 0), stop=False)
                        ins = eng.matmul(to, AS[0][h][:, c, :], Y[1][0:P, k, :], start=False, stop=(k == NT - 1))
                        if layer == 0:
                            ins = eng.matmul(cnt, AS[0][h][:, c, :], ones_r[0:P, :], start=(k == 0), stop=(k == NT - 1))
                        return ins
                    for h in range(2):
                        eng.wait_ge(A.hi, 2 * i + h + 1)
                        chunk_hi(h, 0)
                        with eng.Fori(0, nlo):
                            eng.wait_ge(A.lo, 2 * i + h + 1)
                            for c in range(5):
                                eng.matmul(to, AS[1][h][:, c, :], Y[0][0:P, 5 * h + c, :], start=False, stop=False)
                                if layer == 0:
                                    eng.matmul(cnt, AS[1][h][:, c, :], ones_r[0:P, :], start=False, stop=False)
                        for c in range(1, 5):
                            ins = chunk_hi(h, c)
                        ins.then_inc(A.pe, 1)

                def finish(i, b):
                    if layer == 1:
                        eng.wait_ge(ysum, i + 1)
                        eng.matmul(ps[0:1, 4, :], ones[0:P, 0:1], TB[0:P, b, :], start=False, stop=False
                                   ).then_inc(r.sums, 1)
                    turn(L, b, i)

                sums(0, 0)
                with eng.Fori(0, NT // 2 - 1) as i2:
                    sums(2 * i2 + 1, 1)
                    finish(2 * i2, 0)
                    sums(2 * i2 + 2, 0)
                    finish(2 * i2 + 1, 1)
                sums(NT - 1, 1)
                finish(NT - 2, 0)
                finish(NT - 1, 1)

            def scores(K, hp, n):
                b, i = n // NT % 2, n % NT
                nxt = n // (2 * NT)
                if i == 0:
                    eng.wait_ge(A.cut, K.cuts0 + 14 * (hp + nxt) + 7 * b + 5)
                for c, (lo, w) in enumerate(CHUNKS):
                    if lo >= K.cols[i]:
                        continue
                    w = min(w, K.cols[i] - lo)
                    w += w % 2
                    before = min(c, K.banks[(n - 2) % NT] - 1)
                    eng.wait_ge(A.lo, K.bank(hp, n - 2, before))
                    to = flat(n % 2)[0:P, lo:lo + w]
                    eng.matmul(to, QSH[b][:, P * i:P * i + P], KS[b][:, lo:lo + w], start=True, stop=False)
                    ins = eng.matmul(to, QSL[b][:, P * i:P * i + P], KS[b][:, lo:lo + w], start=False, stop=True)
                ins.then_inc(A.scores, 1)

            def turn_probs(K, hp, n):
                for bank in range(K.banks[n]):
                    eng.wait_ge(A.exp, K.part(hp, n, min(bank, K.parts[n] - 1)))
                    for q in range(min(4, K.blocks[n] - 4 * bank)):
                        c = 4 * bank + q
                        ins = eng.transpose(ps[0:P, 3 * (n % 2) + bank, P * q:P * q + P],
                                            PB[0:P, n % 2, P * c:P * c + P], ident[0:P, 0:P])
                    ins.then_inc(A.tr, 1)

            def values(K, hp, g, half):
                b, gh = g // HG % 2, g % HG
                n = K.blocks[2 * g + 1]
                if half == 0:
                    eng.wait_ge(A.lo, K.bank(hp, 2 * g + 1, K.banks[2 * g + 1] - 1))
                    eng.wait_ge(A.post, K.group(hp, g - 1))
                    if gh == 0:
                        eng.wait_ge(A.cut, K.cuts0 + 14 * hp + 7 * b + 7)
                for c in range(n // 2 * half, n if half else n // 2):
                    s = 1 if c >= K.blocks[2 * g] else 0
                    for p in range(2):
                        rhs = PT[p][:, g % 2, c, s:2, :].rearrange("p s t -> p (s t)")
                        ins = eng.matmul(ps[:, 6, 126 * s:252], VS[b][:, c, :], rhs, start=(c == 0 and p == 0),
                                         stop=(c == n - 1 and p == 1))
                if half == 0:
                    return
                ins.then_inc(A.pv, 1)
                eng.wait_ge(A.diag, K.group(hp, g))
                for s in range(2):
                    ins = eng.matmul(ps[0:HD, 7, P * s:P * s + P], ones[0:P, :], diag[0:P, s, :], start=True, stop=True)
                ins.then_inc(A.bc, 1)

            def attend(K):
                scores(K, 0, 0)

                def body(hp, first=False, last=False):
                    for n in range(2 * NT):
                        if not (last and n == 2 * NT - 1):
                            scores(K, hp, n + 1)
                        turn_probs(K, hp, n)
                        if n >= 2 or not first:
                            values(K, hp, n // 2 - 1, n % 2)
                    if last:
                        for half in range(2):
                            values(K, hp, 2 * HG - 1, half)
                body(0, first=True)
                with eng.Fori(1, H // 2 - 1) as hp:
                    body(hp)
                body(H // 2 - 1, last=True)

            eng.wait_ge(const_ok, 6)
            eng.wait_ge(e.mm, 1)
            for bank, t in ((4, l_f), (5, k_f)):
                for j in range(EJ):
                    ins = eng.transpose(ps[0:P, bank, EQ * j:EQ * j + EQ], t[:, P * j:P * j + P], ident[0:EQ, 0:EQ])
            ins.then_inc(e.tr, 1)
            with eng.Fori(0, NT // 2) as i2:
                for b in range(2):
                    turn(ln0, b, 2 * i2 + b)
            eng.wait_ge(const_ok, 14)
            eng.wait_ge(e.win, 16)
            eng.reg_mov(pair, 0)
            for seg in range(SEG):
                adjacency(NW // 2 // SEG * seg, NW // 2 // SEG * (seg + 1))
                if seg == 0:
                    eng.wait_ge(w_split, 2 * (UNIT["g1l"] + 3) + 2)
                    eng.wait_ge(sp["x"].lo, KC)
                for i in range(NT // SEG * seg, NT // SEG * (seg + 1)):
                    product_tile(pj["g"], i, UNIT["g1l"], X0, pj["g"].v)
            eng.wait_ge(pj["g"].ps, NT)
            eng.sem_inc(w_used, 4)
            product_rows(pj["g"], UNIT["g1r"], X0, pj["g"].v, n0=NT)
            eng.wait_ge(e.many, 1)
            nlo = eng.value_load(many[0:1, 0:1], min_val=0, max_val=1)
            aggregate(0, nlo)
            product_rows(pj["g"], UNIT["g2l"], X0, pj["g"].v, n0=2 * NT, ready=sp["h"].lo)
            product_rows(pj["g"], UNIT["g2r"], X0, pj["g"].v, n0=3 * NT)
            eng.wait_ge(e.ev, 2)
            eng.matmul(ps[0:1, 4, :], ident[0:1, 1:2], brow[0:1, :], start=True, stop=False)
            aggregate(1, nlo)
            eng.matmul(ps[0:1, 4, :], ident[0:1, 1:2], brow[0:1, :], start=False, stop=True).then_inc(r.tr, 1)
            eng.wait_ge(r.row, 1)
            for k in range(KC):
                ins = eng.matmul(ps[:, 5, k:k + 1], prow[:, 128 * k:128 * k + 128], ones[0:1, 0:1], start=True, stop=True)
            ins.then_inc(r.tr, 1)
            eng.wait_ge(r.in_, 32)
            eng.wait_ge(r.col, 1)
            for k in range(KC):
                ins = eng.matmul(ps[:, 5, 8:9], w1r[:, 128 * k:128 * k + 128], rt[:, 1 + k:2 + k],
                                 start=(k == 0), stop=(k == KC - 1))
            ins.then_inc(r.h, 1)
            eng.wait_ge(r.he, 1)
            eng.matmul(ps[0:1, 5, 16:24], rt[:, 5:6], w2r, start=True, stop=True).then_inc(r.l, 1)

            product_cols(pj["qk"], UNIT["qs"], X0, pj["qk"].a, n0=0, k_ready=sp["s"].lo)
            product_cols(pj["qk"], UNIT["ks"], X0, pj["qk"].a, n0=4)
            product_rows(pj["v"], UNIT["vs"], X0, pj["v"].v, n0=0 * NT)
            attend(KS_)
            product_cols(pj["u"], UNIT["us"], X1, pj["u"].v, k_ready=sp["os"].lo)
            product_cols(pj["qk"], UNIT["qc"], X0, pj["qk"].a, n0=8, k_ready=pj["u"].t,
                         last=(pj["u"].v, 4))
            product_cols(pj["qk"], UNIT["qt"], X0, pj["qk"].a, n0=12, k_ready=sp["t"].lo)
            product_cols(pj["qk"], UNIT["kt"], X0, pj["qk"].a, n0=16)
            product_rows(pj["v"], UNIT["vt"], X0, pj["v"].v, n0=1 * NT)
            attend(KT_)
            product_cols(pj["u"], UNIT["ut"], X1, pj["u"].v, n0=4, k_ready=sp["ot"].lo)
            product_cols(pj["qk"], UNIT["kc"], X0, pj["qk"].a, n0=20, k_ready=pj["u"].t, k0=4,
                         last=(pj["u"].v, 8))
            product_rows(pj["v"], UNIT["vc"], X0, pj["v"].v, n0=2 * NT)
            attend(KC_)
            eng.wait_ge(w_split, 2 * (UNIT["uc"] + 3) + 2)
            eng.wait_ge(sp["oc"].lo, KC)
            for i in range(NT + 2):
                if i < NT:
                    product_tile(pj["uc"], i, UNIT["uc"], X1, pj["uc"].v)
                if i >= 2:
                    j = i - 2
                    eng.wait_ge(ln3.nrm, j + 1)
                    eng.wait_ge(ln3.ev, j + 1)
                    for k in range(KC):
                        ins = eng.transpose(ps[:, 4 + j % 2, P * k:P * k + P], TB[0:P, j % 2, 128 * k:128 * k + 128],
                                            ident[0:P, 0:P])
                    ins.then_inc(ln3.tr, 1)
            eng.wait_ge(pj["uc"].ps, NT)
            eng.sem_inc(w_used, 4)

            def mlp(q):
                u = 8 * q + UNIT["mlp"]
                product_cols(pj["m1"], u, X0, pj["m1"].a, n0=4 * q, k_ready=sp["m"].lo if isinstance(q, int) else None)
                eng.wait_ge(w_split, 2 * (u + 7) + 2)
                eng.wait_ge(pj["m1"].t, 4 * q + 4)
                for i in range(NT):
                    product_tile(pj["m2"], i, u, X1, pj["m2"].v, n0=NT * q)
                eng.wait_ge(pj["m2"].ps, NT * q + NT)
                eng.sem_inc(w_used, 4)
            mlp(0)
            with eng.Fori(1, NQ) as q:
                mlp(q)

        @block.scalar
        def _(eng):
            eng.wait_ge(const_ok, 5)

            def prime(sem_, n):
                eng.sem_inc(sem_, n)

            def deviation(L, b, n):
                eng.wait_ge(L.var, n + 1)
                eng.activation(sd[0:P, b, 0:1], mv[0:P, b, 1:2], ACT.Sqrt, bias=eps_t[0:P, :]).then_inc(L.std, 1)

            def cols_out(L, b, i, func=ACT.Copy):
                eng.wait_ge(L.tr, i + 3)
                eng.activation(ZT[:, :, ds(i * P, P)],
                               ps[:, 6 + b, 0:KC * P].rearrange("p (k t) -> p k t", k=KC), func).then_inc(L.ev, 1)

            def cut_hi(S, get, X, affine):
                for k in range(KC):
                    if affine:
                        eng.wait_ge(S.val, k + 1)
                    eng.activation(X[0][:, k, :], get(k), ACT.Copy).then_inc(S.hi, 1)

            def bias_cols(J, unit, dst_, bias, scale, n0=0):
                for m in range(4):
                    eng.wait_ge(w_used, unit + m + 1)
                    eng.activation(dst_[:, m, :], flat(m % 2)[:, 0:T], ACT.Identity, bias=bias[:, m:m + 1],
                                   scale=scale).then_inc(J.a, 1)

            def attend(K):
                eng.sem_inc(A.exp, K.total_parts)
                eng.sem_inc(A.hi, K.total)
                eng.sem_inc(A.bot, 2 * HG)

                def exponentials(hp, n):
                    eng.wait_ge(A.negmax, K.tile(hp, n))
                    eng.wait_ge(A.tr, K.bank(hp, n - 2, K.banks[(n - 2) % (2 * NT)] - 1))
                    w = K.cols[n % (2 * NT)]
                    for p, (lo, hi) in enumerate(((0, min(w, BANK)), (BANK, w))[:K.parts[n % (2 * NT)]]):
                        eng.activation(PB[0:P, n % 2, lo:hi], flat(n % 2)[0:P, lo:hi], ACT.Exp,
                                       bias=ngm[0:P, n % 2:n % 2 + 1], accum_out=rs[0:P, p, n % 4:n % 4 + 1]
                                       ).then_inc(A.exp, 1)

                def probs_hi(hp, n):
                    g = n // 2
                    eng.wait_ge(A.pv, K.group(hp, g - 2))
                    for bank in range(K.banks[n]):
                        nb = min(4, K.blocks[n] - 4 * bank)
                        eng.wait_ge(A.tr, K.bank(hp, n, bank))
                        eng.activation(PT[0][:, g % 2, 4 * bank:4 * bank + nb, n % 2, 0:P],
                                       ps[0:P, 3 * (n % 2) + bank, 0:P * nb].rearrange("p (c t) -> p c t", c=nb),
                                       ACT.Copy).then_inc(A.hi, 1)

                def bottom(hp, g):
                    eng.wait_ge(A.pv, K.group(hp, g))
                    eng.wait_ge(A.post, K.group(hp, g - 1))
                    eng.activation(comb, ps[64:128, 6, 0:252], ACT.Copy).then_inc(A.bot, 1)

                def body(hp, first=False, last=False):
                    for n in range(2 * NT):
                        probs_hi(hp, n)
                        if not (last and n == 2 * NT - 1):
                            exponentials(hp, n + 1)
                        if n % 2 == 1 and (n >= 3 or not first):
                            bottom(hp, n // 2 - 1)
                    if last:
                        bottom(hp, 2 * HG - 1)
                exponentials(0, 0)
                body(0, first=True)
                with eng.Fori(1, H // 2 - 1) as hp:
                    body(hp)
                body(H // 2 - 1, last=True)

            eng.wait_ge(e.tr, 1)
            for bank, t in ((4, loT), (5, keyT)):
                eng.activation(t[:, 0:EC].rearrange("p (q j) -> p j q", j=EJ),
                               ps[0:P, bank, 0:EC].rearrange("p (j q) -> p j q", j=EJ), ACT.Copy).then_inc(e.ev, 1)
            with eng.Fori(0, NT // 2) as i2:
                for b in range(2):
                    deviation(ln0, b, 2 * i2 + b)
                for b in range(2):
                    cols_out(ln0, b, 2 * i2 + b)
            eng.wait_ge(ln0.ev, NT + 2)
            cut_hi(sp["x"], lambda k: ZT[:, k, :], X0, False)
            def rows_hi(J, n0, first_i=0, end_i=NT):
                for i in range(first_i, end_i):
                    eng.wait_ge(J.ps, n0 + i + 1)
                    eng.activation(Y[0][0:P, i, :], ps[0:P, 6 + i % 2, :], ACT.Copy).then_inc(J.a, 1)

            def aggregate(layer):
                A, L = ag[layer], (ln1, ln2)[layer]

                def stage(i):
                    for h in range(2):
                        eng.wait_ge(A.pe, 2 * i + h + 1)
                        eng.activation(AS[0][h], AT[0:P, 5 * h:5 * h + 5, ds(i * P, P)], ACT.Copy).then_inc(A.hi, 1)

                def finish(i, b):
                    cols_out(L, b, i, ACT.Copy if layer else ACT.Relu)

                def deviations(i, b):
                    if layer:
                        deviation(L, b, 2 * i)
                        deviation(L, b, 2 * i + 1)

                stage(0)
                stage(1)
                deviations(0, 0)
                with eng.Fori(0, NT // 2 - 1) as i2:
                    stage(2 * i2 + 2)
                    finish(2 * i2, 0)
                    deviations(2 * i2 + 1, 1)
                    stage(2 * i2 + 3)
                    finish(2 * i2 + 1, 1)
                    deviations(2 * i2 + 2, 0)
                finish(NT - 2, 0)
                deviations(NT - 1, 1)
                finish(NT - 1, 1)

            for seg in range(SEG):
                with eng.Fori(NW // 2 // SEG * seg, NW // 2 // SEG * (seg + 1)) as w2:
                    for j in range(2):
                        w = 2 * w2 + j
                        eng.wait_ge(at_ready, w + 1)
                        eng.activation(AT[0:P, :, ds(w * WD, WD)],
                                       ps[0:P, j, 0:WK].rearrange("p (d h) -> p h d", h=NT), ACT.Copy
                                       ).then_inc(at_free, 1)
                rows_hi(pj["g"], 0, NT // SEG * seg, NT // SEG * (seg + 1))
            aggregate(0)
            eng.wait_ge(ln1.ev, NT + 2)
            cut_hi(sp["h"], lambda k: ZT[:, k, :], X0, False)
            rows_hi(pj["g"], 2 * NT)
            aggregate(1)
            eng.wait_ge(r.tr, 1)
            eng.wait_ge(x1_st, 16 * NT)
            eng.activation(prow, ps[0:1, 4, :], ACT.Copy, scale=1.0 / T).then_inc(r.row, 1)
            eng.wait_ge(r.tr, 2)
            eng.activation(rt[:, 1:5], ps[:, 5, 0:4], ACT.Copy).then_inc(r.col, 1)
            eng.wait_ge(small_in, 64)
            eng.wait_ge(r.h, 1)
            eng.activation(rt[:, 5:6], ps[:, 5, 8:9], ACT.Gelu, bias=rt[:, 0:1]).then_inc(r.he, 1)

            cut_hi(sp["s"], lambda k: PB[:, k % 2, :], X0, True)
            eng.wait_ge(biasq, 1)
            bias_cols(pj["qk"], UNIT["qs"], QK[:, 0], bcol_q, SCALE)
            bias_cols(pj["qk"], UNIT["ks"], QK[:, 1], bcol[:, 4:8], 1.0)
            attend(KS_)

            def cut_out(S, K):
                eng.wait_ge(A.post, K.group(H // 2 - 1, 2 * HG - 1))
                cut_hi(S, lambda k: ZT[:, k, :], X1, False)

            def out_hi(J, n0):
                for m in range(4):
                    eng.wait_ge(J.v, n0 + m + 1)
                    eng.activation(X0[0][:, m, :], PB[:, m % 2, :], ACT.Copy).then_inc(J.a, 1)
            cut_out(sp["os"], KS_)
            out_hi(pj["u"], 0)
            eng.wait_ge(biasq, 2)
            bias_cols(pj["qk"], UNIT["qc"], QK[:, 0], bcol_q, SCALE)
            cut_hi(sp["t"], lambda k: PB[:, k % 2, :], X0, True)
            eng.wait_ge(biasq, 3)
            eng.wait_ge(qc_st, 16 * 4)
            bias_cols(pj["qk"], UNIT["qt"], QK[:, 0], bcol_q, SCALE)
            bias_cols(pj["qk"], UNIT["kt"], QK[:, 1], bcol[:, 4:8], 1.0)
            attend(KT_)
            cut_out(sp["ot"], KT_)
            out_hi(pj["u"], 4)
            eng.wait_ge(bcol_in[3], 16)
            bias_cols(pj["qk"], UNIT["kc"], QK[:, 1], bcol[:, 4:8], 1.0)
            attend(KC_)
            cut_out(sp["oc"], KC_)
            for i in range(NT + 2):
                if i < NT:
                    eng.wait_ge(ln3.var, i + 1)
                    eng.activation(sd[0:P, i % 2, 0:1], mv[0:P, i % 2, 1:2], ACT.Sqrt, bias=eps_t[0:P, :]
                                   ).then_inc(ln3.std, 1)
                if i >= 2:
                    j = i - 2
                    eng.wait_ge(ln3.tr, j + 3)
                    eng.activation(ZT[:, :, P * j:P * j + P],
                                   ps[:, 4 + j % 2, 0:KC * P].rearrange("p (k t) -> p k t", k=KC), ACT.Copy
                                   ).then_inc(ln3.ev, 1)
            cut_hi(sp["m"], lambda k: PB[:, k % 2, :], X0, True)

            def mlp(q):
                for m in range(4):
                    eng.wait_ge(w_used, 8 * q + (UNIT["mlp"] + m + 1))
                    if not isinstance(q, int) or 4 * q + m >= 2:
                        eng.wait_ge(pj["m1"].t, 4 * q + m - 1)
                    b1 = b1col[:, m:m + 1] if isinstance(q, int) else b1col[:, ds(4 * q + m, 1)]
                    eng.activation(PB[:, m % 2, :], flat(m % 2)[:, 0:T], ACT.Gelu, bias=b1).then_inc(pj["m1"].a, 1)
            mlp(0)
            with eng.Fori(1, NQ) as q:
                mlp(q)

        @block.vector
        def _(eng):
            for s, n in ((ln0.tr, 2), (ln0.ev, 2), (ln1.tr, 2), (ln1.ev, 2), (ln2.tr, 2), (ln2.ev, 2), (ln3.tr, 2),
                         (ln3.ev, 2), (at_free, 2), (ag[0].pe, 2), (ag[0].dv, 2), (ag[1].pe, 2), (ag[1].dv, 2),
                         (oh_used, RING)):
                eng.sem_inc(s, n)

            link = Chain(eng, e.lk)
            eng.wait_ge(e.in_, 32)
            eng.tensor_copy(s_f, s_i).then_inc(e.lk, 1)
            eng.tensor_copy(d_f, d_i).then_inc(e.lk, 1)
            link.n = 2
            eng.wait_ge(e.lk, 2)
            link(eng.tensor_scalar(h_f, s_f, float(P), None, ALU.is_ge))
            for j in range(2, NT):
                link(eng.scalar_tensor_tensor(out=h_f, in0=s_f, scalar=float(P * j), in1=h_f, op0=ALU.is_ge, op1=ALU.add))
            link(eng.scalar_tensor_tensor(out=l_f, in0=h_f, scalar=-float(P), in1=s_f, op0=ALU.mult, op1=ALU.add))
            eng.scalar_tensor_tensor(out=k_f, in0=d_f, scalar=float(NT), in1=h_f, op0=ALU.mult, op1=ALU.add
                                     ).then_inc(e.mm, 1)
            d3 = d_f.rearrange("q (j p) -> q j p", j=EJ)
            link(eng.tensor_reduce(out=mm2[:, 0:3], in_=d3, op=ALU.min, axis=AX.X))
            eng.tensor_reduce(out=mm2[:, 3:6], in_=d3, op=ALU.max, axis=AX.X).then_inc(e.mm, 1)

            def stat(L, b, source, c):
                eng.sem_inc(held, 1)
                c(eng.bn_stats(stats[0:P, b, :], source))
                eng.sem_inc(held, 1)
                eng.bn_aggr(mv[0:P, b, :], stats[0:P, b, :]).then_inc(L.var, 1)

            with eng.Fori(0, NT // 2) as i2:
                c = Chain(eng, ln0.lk, 4 * i2)
                for b in range(2):
                    eng.wait_ge((ln0.src0, ln0.src1)[b], 16 * i2 + 16)
                    stat(ln0, b, TB[0:P, b, :], c)
                for b in range(2):
                    eng.wait_ge(ln0.std, 2 * i2 + b + 1)
                    c(eng.reciprocal(sd[0:P, b, 1:2], sd[0:P, b, 0:1]))
                    eng.tensor_scalar(TB[0:P, b, :], TB[0:P, b, :], mv[0:P, b, 0:1], sd[0:P, b, 1:2],
                                      ALU.subtract, ALU.mult).then_inc(ln0.nrm, 1)

            eng.wait_ge(const_ok, 14)
            eng.wait_ge(e.mmi, 16)
            link(eng.tensor_scalar(wcol[:, 1:2], wcol[:, 0:1], float(WD - 1), None, ALU.add))
            link(eng.tensor_scalar(msk, dbc[:, EC:2 * EC], wcol[:, 0:1], None, ALU.is_ge))
            link(eng.scalar_tensor_tensor(out=msk, in0=dbc[:, 0:EC], scalar=wcol[:, 1:2], in1=msk,
                                          op0=ALU.is_le, op1=ALU.mult))
            link(eng.scalar_tensor_tensor(out=dbc[:, 0:EC], in0=cid[:, 0:EC], scalar=1.0, in1=msk, op0=ALU.add, op1=ALU.mult))
            link(eng.tensor_reduce(out=wcol[:, 2:3], in_=dbc[:, 0:EC], op=ALU.max, axis=AX.X))
            link(eng.scalar_tensor_tensor(out=dbc[:, 0:EC], in0=msk, scalar=-1000.0, in1=cid[:, 0:EC], op0=ALU.mult, op1=ALU.add))
            link(eng.tensor_reduce(out=wcol[:, 4:5], in_=dbc[:, 0:EC], op=ALU.min, axis=AX.X))
            link(eng.tensor_scalar(wcol[:, 3:4], wcol[:, 2:3], 1.0, None, ALU.max))
            link(eng.tensor_scalar(wcol[:, 5:6], wcol[:, 3:4], -1.0, None, ALU.add))
            eng.tensor_scalar(wcol[:, 6:7].bitcast(I32), wcol[:, 4:5], 1000.0, wcol[:, 5:6], ALU.add, ALU.min
                              ).then_inc(e.w, 1)
            eng.tensor_copy(wcol[:, 7:8].bitcast(I32), wcol[:, 3:4]).then_inc(e.w, 1)

            def cut_lo(S, get, X):
                for k in range(KC):
                    eng.wait_ge(S.hi, k + 1)
                    eng.tensor_tensor(X[1][:, k, :], get(k), X[0][:, k, :].bitcast(F32), ALU.subtract).then_inc(S.lo, 1)

            def cut_affine(S, w, b, X, stored=False):
                for k in range(KC):
                    if k >= 2 and stored:
                        eng.wait_ge((S.st0, S.st1)[k % 2], 16)
                    if k >= 2:
                        eng.wait_ge(S.lo, k - 1)
                    eng.tensor_scalar(PB[:, k % 2, :], ZT[:, k, :], lncol[:, w, k:k + 1], lncol[:, b, k:k + 1],
                                      ALU.mult, ALU.add).then_inc(S.val, 1)
                    if k:
                        lo_affine(S, X, k - 1)
                lo_affine(S, X, KC - 1)

            def lo_affine(S, X, k):
                eng.wait_ge(S.hi, k + 1)
                eng.tensor_tensor(X[1][:, k, :], PB[:, k % 2, :], X[0][:, k, :].bitcast(F32), ALU.subtract
                                  ).then_inc(S.lo, 1)

            eng.wait_ge(ln0.ev, NT + 2)
            cut_lo(sp["x"], lambda k: ZT[:, k, :], X0)

            eng.wait_ge(e.win, 16)
            eng.wait_ge(e.ev, 2)
            def rows_lo(J, a0, first_i=0, end_i=NT):
                for i in range(first_i, end_i):
                    eng.wait_ge(J.a, a0 + i + 1)
                    eng.tensor_tensor(Y[1][0:P, i, :], ps[0:P, 6 + i % 2, :], Y[0][0:P, i, :].bitcast(F32), ALU.subtract
                                      ).then_inc(J.v, 1)

            def rows_bias(J, dst_, n0, row):
                eng.wait_ge(row_in, 16 * row)
                for i in range(NT):
                    eng.wait_ge(J.ps, n0 + i + 1)
                    eng.tensor_tensor(dst_[0:P, i, :], ps[0:P, 6 + i % 2, :], brow[0:P, :], ALU.add).then_inc(J.v, 1)
                eng.wait_ge(J.v, n0 + NT)
                eng.sem_inc(row_free, 1)

            def aggregate(layer, nlo):
                A, L = ag[layer], (ln1, ln2)[layer]

                def stage_lo(i):
                    with eng.Fori(0, nlo):
                        for h in range(2):
                            eng.wait_ge(A.hi, 2 * i + h + 1)
                            eng.tensor_tensor(AS[1][h], AT[0:P, 5 * h:5 * h + 5, ds(i * P, P)], AS[0][h].bitcast(F32),
                                              ALU.subtract).then_inc(A.lo, 1)

                def finish(i, b):
                    c = Chain(eng, L.lk, (8 if layer else 2) * i)
                    rc = rcnt[0:P, ds(i, 1), :].rearrange("p a c -> p (a c)")
                    rw = RW[0:P, ds(i, 1), :].rearrange("p a f -> p (a f)")
                    eng.wait_ge(A.pe, 2 * i + 4)
                    if layer == 0:
                        c(eng.tensor_scalar(cntm[0:P, b:b + 1], ps[0:P, 2 + b, 0:1], 1.0, None, ALU.max))
                        c(eng.reciprocal(rc, cntm[0:P, b:b + 1]))
                        eng.wait_ge(L.tr, i + 1)
                        eng.scalar_tensor_tensor(out=TB[0:P, b, :], in0=ps[0:P, b, :], scalar=rc, in1=rw,
                                                 op0=ALU.mult, op1=ALU.add).then_inc(L.nrm, 1)
                        eng.wait_ge(L.nrm, i + 1)
                        eng.sem_inc(A.dv, 1)
                        return
                    c(eng.scalar_tensor_tensor(out=rw, in0=ps[0:P, b, :], scalar=rc, in1=rw, op0=ALU.mult, op1=ALU.add))
                    eng.sem_inc(A.dv, 1)
                    eng.wait_ge((L.src0, L.src1)[b], (i - b) * 8 + 16)
                    c(eng.tensor_tensor(rw, rw, TB[0:P, b, :], ALU.add))
                    stat(L, b, rw, c)
                    eng.wait_ge(L.std, 2 * i + 1)
                    c(eng.reciprocal(sd[0:P, b, 1:2], sd[0:P, b, 0:1]))
                    m1 = mr1[0:P, ds(i, 1), :].rearrange("p a c -> p (a c)")
                    eng.tensor_copy(m1[:, 0:1], mv[0:P, b, 0:1]).then_inc(L.lk, 1)
                    eng.tensor_copy(m1[:, 1:2], sd[0:P, b, 1:2]).then_inc(L.lk, 1)
                    eng.tensor_scalar(TB[0:P, b, :], rw, mv[0:P, b, 0:1], sd[0:P, b, 1:2],
                                      ALU.subtract, ALU.mult).then_inc(ysum, 1)
                    c.n += 2
                    eng.wait_ge(ysum, i + 1)
                    stat(L, b, TB[0:P, b, :], c)
                    eng.wait_ge(L.std, 2 * i + 2)
                    c(eng.reciprocal(sd[0:P, b, 1:2], sd[0:P, b, 0:1]))
                    eng.wait_ge(L.tr, i + 2)
                    eng.tensor_scalar(TB[0:P, 2, :], TB[0:P, b, :], mv[0:P, b, 0:1], sd[0:P, b, 1:2],
                                      ALU.subtract, ALU.mult).then_inc(L.nrm, 1)

                stage_lo(0)
                with eng.Fori(0, NT // 2 - 1) as i2:
                    for b in range(2):
                        stage_lo(2 * i2 + b + 1)
                        finish(2 * i2 + b, b)
                stage_lo(NT - 1)
                finish(NT - 2, 0)
                finish(NT - 1, 1)

            eng.wait_ge(e.win, 16)
            link(eng.tensor_tensor(wide[:, 0:NW], win[:, :].rearrange("a (w c) -> a w c", c=2)[:, :, 1],
                                   win[:, :].rearrange("a (w c) -> a w c", c=2)[:, :, 0], ALU.subtract))
            link(eng.tensor_reduce(out=wide[:, NW:NW + 1], in_=wide[:, 0:NW], op=ALU.max, axis=AX.X))
            eng.tensor_scalar(many[:, :], wide[:, NW:NW + 1], float(4096 // (P * EG)), None, ALU.is_gt
                              ).then_inc(e.many, 1)

            eng.wait_ge(e.many, 1)
            nlo = eng.value_load(many[0:1, 0:1], min_val=0, max_val=1)

            pair = eng.alloc_register("pair")
            eng.reg_mov(pair, 0)
            for seg in range(SEG):
                with eng.Fori(NW // SEG * seg, NW // SEG * (seg + 1)) as w:
                    first = eng.value_load(win[0:1, ds(2 * w, 1)], min_val=0, max_val=EP // EG - 1)
                    end = eng.value_load(win[0:1, ds(2 * w + 1, 1)], min_val=1, max_val=EP // EG)
                    with eng.Fori(first, end) as c:
                        now = eng.snap(pair)
                        slot = eng.snap(now & (RING - 1))
                        eng.wait_ge(oh_used, now + 1)
                        eng.tensor_tensor(oh_lo[:, ds(slot, 1), :, :].rearrange("p a g c -> p (a g) c"),
                                          iota_b[:, 0:128].unsqueeze(1).to_broadcast([P, EG, 128]),
                                          loT[:, ds(c * EG, EG)].unsqueeze(2).to_broadcast([P, EG, 128]),
                                          ALU.is_equal).then_inc(oh_ready, 1)
                        eng.scalar_tensor_tensor(out=oh_key[:, ds(slot, 1), :, :].rearrange("p a g c -> p (a g) c"),
                                                 in0=iota_b[:, 0:WK].unsqueeze(1).to_broadcast([P, EG, WK]),
                                                 scalar=woff[:, ds(w, 1)],
                                                 in1=keyT[:, ds(c * EG, EG)].unsqueeze(2).to_broadcast([P, EG, WK]),
                                                 op0=ALU.add, op1=ALU.is_equal).then_inc(oh_ready, 1)
                        eng.reg_add(pair, pair, 1)
                if seg:
                    rows_lo(pj["g"], 0, NT // SEG * (seg - 1), NT // SEG * seg)
            rows_lo(pj["g"], 0, NT - NT // SEG, NT)
            rows_bias(pj["g"], RW, NT, 1)
            aggregate(0, nlo)
            eng.wait_ge(ln1.ev, NT + 2)
            cut_lo(sp["h"], lambda k: ZT[:, k, :], X0)
            rows_lo(pj["g"], NT)
            rows_bias(pj["g"], RW, 3 * NT, 2)
            aggregate(1, nlo)

            eng.wait_ge(r.l, 1)
            link = Chain(eng, r.lk)
            link(eng.tensor_tensor(rt[0:1, 24:32], ps[0:1, 5, 16:24], rt[0:1, 8:16], ALU.add))
            for j in range(2):
                lg = rt[0:1, 24 + 4 * j:28 + 4 * j]
                link(eng.tensor_reduce(out=rt[0:1, 32:33], in_=lg, op=ALU.max, axis=AX.X))
                link(eng.scalar_tensor_tensor(out=rt[0:1, 36:40], in0=lg, scalar=rt[0:1, 32:33], in1=rt[0:1, 16:20],
                                              op0=ALU.is_equal, op1=ALU.mult))
                link(eng.tensor_reduce(out=rt[0:1, 33:34], in_=rt[0:1, 36:40], op=ALU.max, axis=AX.X))
                eng.tensor_scalar(idx_i[0:1, j:j + 1], rt[0:1, 33:34], -1.0, 4.0, ALU.mult, ALU.add).then_inc(r.i, 1)

            def scaled_bias(n, came):
                eng.wait_ge(came, 16)
                eng.tensor_scalar(bcol_q[:], bcol[:, 0:4], SCALE, None, ALU.mult).then_inc(biasq, 1)

            def attend(K):
                eng.sem_inc(A.negmax, 2 * NT)
                eng.sem_inc(A.lo, K.total)
                eng.sem_inc(A.tr, K.total)
                eng.sem_inc(A.pv, 2 * HG)
                eng.sem_inc(A.diag, 2 * HG)
                eng.sem_inc(A.bc, 2 * HG)
                eng.sem_inc(A.post, 2 * HG)
                if K.causal:
                    eng.wait_ge(mask_ok, 2)

                def greatest(c, n):
                    eng.wait_ge(A.scores, K.tile(c.hp, n))
                    i = n % NT
                    if K.causal:
                        block_ = flat(n % 2)[0:P, P * i:P * i + P]
                        c(eng.tensor_tensor(block_, block_, mask, ALU.add))
                    eng.tensor_reduce(out=ngm[0:P, n % 2:n % 2 + 1], in_=flat(n % 2)[0:P, 0:K.cols[i]], op=ALU.max,
                                      axis=AX.X, negate=True).then_inc(A.negmax, 1)

                def probs_lo(hp, n):
                    g = n // 2
                    for bank in range(K.banks[n]):
                        nb = min(4, K.blocks[n] - 4 * bank)
                        blk = (slice(None), g % 2, slice(4 * bank, 4 * bank + nb), n % 2, slice(0, P))
                        eng.wait_ge(A.hi, K.bank(hp, n, bank))
                        eng.tensor_tensor(PT[1][blk],
                                          ps[0:P, 3 * (n % 2) + bank, 0:P * nb].rearrange("p (c t) -> p c t", c=nb),
                                          PT[0][blk].bitcast(F32), ALU.subtract).then_inc(A.lo, 1)

                def inverse(c, hp, g):
                    eng.wait_ge(A.exp, K.part(hp, 2 * g + 1, K.parts[2 * g + 1] - 1))
                    k = 2 * g % 4
                    if K.parts[2 * g + 1] == 2:
                        c(eng.tensor_tensor(rs[0:P, 0, k:k + 2], rs[0:P, 0, k:k + 2], rs[0:P, 1, k:k + 2], ALU.add))
                    c(eng.reciprocal(rr[0:P, :], rs[0:P, 0, k:k + 2]))
                    for s in range(2):
                        ins = eng.tensor_scalar(diag[0:P, s, :], ident[0:P, 0:P], rr[0:P, s:s + 1], None, ALU.mult)
                    ins.then_inc(A.diag, 1)

                def output(c, hp, g):
                    b, gh = g // HG % 2, g % HG
                    eng.wait_ge(A.bot, K.group(hp, g))
                    c(eng.tensor_tensor(comb, ps[0:HD, 6, 0:252], comb, ALU.add))
                    eng.wait_ge(A.bc, K.group(hp, g))
                    o = ZT[64 * b:64 * b + 64, ds(hp - (g < 0), 1), 2 * P * gh:2 * P * gh + 2 * P].rearrange("p a (s t) -> p (a s) t", s=2)
                    eng.tensor_tensor(o, ps[0:HD, 7, 0:2 * P].rearrange("p (s t) -> p s t", s=2),
                                      comb.rearrange("p (s t) -> p s t", s=2)[:, :, 0:P], ALU.mult).then_inc(A.post, 1)

                def body(hp, first=False, last=False):
                    c = Chain(eng, A.lk, K.links0 + int(K.causal) + K.links * hp - (0 if first else 3))
                    c.hp = hp
                    for n in range(2 * NT):
                        if not (last and n == 2 * NT - 1):
                            greatest(c, n + 1)
                        probs_lo(hp, n)
                        if n % 2 == 0 and (n >= 2 or not first):
                            inverse(c, hp, n // 2 - 1)
                        if n % 2 == 1 and (n >= 3 or not first):
                            output(c, hp, n // 2 - 1)
                    if last:
                        inverse(c, hp, 2 * HG - 1)
                        output(c, hp, 2 * HG - 1)
                c0 = Chain(eng, A.lk, K.links0)
                c0.hp = 0
                greatest(c0, 0)
                body(0, first=True)
                with eng.Fori(1, H // 2 - 1) as hp:
                    body(hp)
                body(H // 2 - 1, last=True)

            def clear_pads():
                for p in range(2):
                    for s in range(2):
                        ins = eng.memset(PT[p][:, :, :, s, P:P + 1].rearrange("p g c t -> p g (c t)").bitcast(F32), 0.0)
                        ins.then_inc(pad_ok, 1)

            def out_val(J, unit, n0, residual=False):
                for m in range(4):
                    eng.wait_ge(w_used, unit + m + 1)
                    if residual:
                        ins = eng.scalar_tensor_tensor(out=PB[:, m % 2, :], in0=flat(m % 2)[:, 0:T],
                                                       scalar=ocol[:, m:m + 1], in1=XR[:, m, :], op0=ALU.add, op1=ALU.add)
                    else:
                        ins = eng.tensor_scalar(PB[:, m % 2, :], flat(m % 2)[:, 0:T], ocol[:, m:m + 1], None, ALU.add)
                    ins.then_inc(J.v, 1)
                    eng.wait_ge(J.a, n0 + m + 1)
                    eng.tensor_tensor(X0[1][:, m, :], PB[:, m % 2, :], X0[0][:, m, :].bitcast(F32), ALU.subtract
                                      ).then_inc(J.t, 1)

            eng.wait_ge(small_in, 64)
            eng.wait_ge(r.h, 1)
            cut_affine(sp["s"], 0, 1, X0)
            scaled_bias(1, bcol_in[0])
            rows_bias(pj["v"], V, 0 * NT, 3)
            clear_pads()
            attend(KS_)
            cut_lo(sp["os"], lambda k: ZT[:, k, :], X1)
            eng.wait_ge(ocol_in[0], 16)
            out_val(pj["u"], UNIT["us"], 0)
            scaled_bias(2, bcol_in[1])
            eng.wait_ge(zt_in, 16)
            eng.wait_ge(pj["u"].t, 4)
            cut_affine(sp["t"], 2, 3, X0, stored=True)
            scaled_bias(3, bcol_in[2])
            rows_bias(pj["v"], V, 1 * NT, 4)
            clear_pads()
            attend(KT_)
            cut_lo(sp["ot"], lambda k: ZT[:, k, :], X1)
            eng.wait_ge(ocol_in[1], 16)
            eng.wait_ge(xr_in, 16)
            out_val(pj["u"], UNIT["ut"], 4, residual=True)
            rows_bias(pj["v"], V, 2 * NT, 5)
            clear_pads()
            attend(KC_)
            cut_lo(sp["oc"], lambda k: ZT[:, k, :], X1)
            eng.wait_ge(row_in, 16 * 6)
            J = pj["uc"]
            c = Chain(eng, ln3.lk)
            for i in range(NT):
                b = i % 2
                y = PB[0:P, b, 0:D]
                eng.wait_ge((ln3.src0, ln3.src1)[b], 16 * (i // 2 + 1))
                c(eng.tensor_scalar(y, TB[0:P, b, :], mr1[0:P, i, 0:1], mr1[0:P, i, 1:2], ALU.subtract, ALU.mult))
                c(eng.tensor_tensor(y, y, brow[0:P, :], ALU.add))
                eng.wait_ge(J.ps, i + 1)
                eng.tensor_tensor(y, ps[0:P, 6 + b, :], y, ALU.add).then_inc(J.v, 1)
                eng.wait_ge(J.v, i + 1)
                c(eng.tensor_tensor(ACC[0:P, i, :], y, TB[0:P, b, :], ALU.add))
                stat(ln3, b, y, c)
                eng.wait_ge(ln3.std, i + 1)
                c(eng.reciprocal(sd[0:P, b, 1:2], sd[0:P, b, 0:1]))
                eng.tensor_scalar(TB[0:P, b, :], y, mv[0:P, b, 0:1], sd[0:P, b, 1:2], ALU.subtract, ALU.mult
                                  ).then_inc(ln3.nrm, 1)
            eng.sem_inc(row_free, 1)
            eng.wait_ge(ln3.ev, NT + 2)
            cut_affine(sp["m"], 4, 5, X0)
            eng.wait_ge(row_in, 16 * 7)
            for i in range(NT):
                eng.tensor_tensor(ACC[0:P, i, :], ACC[0:P, i, :], brow[0:P, :], ALU.add).then_inc(pj["m2"].a, 1)
            eng.wait_ge(pj["m2"].a, NT)

            def mlp(q):
                J1, J2 = pj["m1"], pj["m2"]
                for m in range(4):
                    eng.wait_ge(J1.a, 4 * q + m + 1)
                    if m == 0 and not isinstance(q, int):
                        eng.wait_ge(J2.ps, NT * q)
                    eng.tensor_scalar(X1[0][:, m, :], PB[:, m % 2, :], 1.0, None, ALU.mult).then_inc(J1.v, 1)
                    eng.wait_ge(J1.v, 4 * q + m + 1)
                    eng.tensor_tensor(X1[1][:, m, :], PB[:, m % 2, :], X1[0][:, m, :].bitcast(F32), ALU.subtract
                                      ).then_inc(J1.t, 1)
                for i in range(NT):
                    eng.wait_ge(J2.ps, NT * q + i + 1)
                    ins = eng.tensor_tensor(ACC[0:P, i, :], ps[0:P, 6 + i % 2, :], ACC[0:P, i, :], ALU.add)
                    ins.then_inc(J2.v, 1)
            mlp(0)
            with eng.Fori(1, NQ - 1) as q:
                mlp(q)
            J1, J2 = pj["m1"], pj["m2"]
            q = NQ - 1
            eng.wait_ge(J2.ps, NT * q)
            for m in range(4):
                eng.wait_ge(J1.a, 4 * q + m + 1)
                eng.tensor_scalar(X1[0][:, m, :], PB[:, m % 2, :], 1.0, None, ALU.mult).then_inc(J1.v, 1)
                eng.wait_ge(J1.v, 4 * q + m + 1)
                eng.tensor_tensor(X1[1][:, m, :], PB[:, m % 2, :], X1[0][:, m, :].bitcast(F32), ALU.subtract
                                  ).then_inc(J1.t, 1)
            eng.wait_ge(J2.v, NT * q)
            for i in range(NT):
                eng.wait_ge(J2.ps, NT * q + i + 1)
                eng.tensor_tensor(ACC[0:P, i, :], ps[0:P, 6 + i % 2, :], ACC[0:P, i, :], ALU.add).then_inc(fin, 1)
                eng.wait_ge(fin, i + 1)
                eng.sem_inc(J2.v, 1)


def kernel(**inputs):
    import numpy as np
    import concourse.bacc as bacc
    from concourse.bass_utils import run_bass_kernel_spmd

    a = {k: np.asarray(v) for k, v in inputs.items()}
    f = {k[7:]: v for k, v in a.items() if k.startswith("L0_ffn_")}

    def by_rows(w):
        return w.T.reshape(-1, 128, w.shape[0]).reshape(-1, 128, 512)

    def by_blocks(w):
        return w.reshape(-1, 128, KC, 128).transpose(0, 3, 2, 1).reshape(-1, 128, 512)

    def by_cols(b):
        return b.reshape(-1, 128).T

    units = [by_rows(a[n]) for n in ("L0_gnn_W1_l", "L0_gnn_W1_r", "L0_gnn_W2_l", "L0_gnn_W2_r")]
    for n in range(NEXP):
        w = f["sp_in_w"][n]
        units += [by_blocks(w[0:D]), by_blocks(w[D:2 * D]), by_rows(w[2 * D:]), by_blocks(f["sp_out_w"][n])]
    for n in range(NEXP):
        units += [by_blocks(f["tq_w"][n]), by_blocks(f["tk_w"][n]), by_rows(f["tv_w"][n]), by_blocks(f["tp_w"][n])]
    w = f["cross_in_w"]
    units += [by_blocks(w[0:D]), by_blocks(w[D:2 * D]), by_rows(w[2 * D:]), by_rows(f["cross_out_w"])]
    units += [by_blocks(f["mlp_w1"]), by_rows(f["mlp_w2"])]
    qkv = [by_cols(f["sp_in_b"][n]) for n in range(NEXP)]
    qkv += [by_cols(np.concatenate([f["tq_b"][n], f["tk_b"][n], f["tv_b"][n]])) for n in range(NEXP)]
    qkv += [by_cols(f["cross_in_b"])]
    outs = [by_cols(f["sp_out_b"][n]) for n in range(NEXP)] + [by_cols(f["tp_b"][n]) for n in range(NEXP)]
    row_bias = [a["L0_gnn_b1"], a["L0_gnn_b2"]] + [f["sp_in_b"][n][2 * D:] for n in range(NEXP)]
    row_bias += [f["tv_b"][n] for n in range(NEXP)] + [f["cross_in_b"][2 * D:], f["cross_out_b"], f["mlp_b2"]]
    data = {
        "x": a["x"].reshape(NT, P, D),
        "src": a["src"],
        "dst": a["dst"],
        "weights": np.concatenate(units),
        "qkv_bias": np.stack(qkv),
        "out_bias": np.stack(outs),
        "row_bias": np.stack(row_bias),
        "ln_cols": np.stack([by_cols(f[n]) for n in ("norm_s_w", "norm_s_b", "norm_t_w", "norm_t_b",
                                                     "norm_mlp_w", "norm_mlp_b")], axis=1),
        "mlp_b1": by_cols(f["mlp_b1"]),
        "router_w1": f["router_w1"].T.reshape(KC, 128, 128).transpose(1, 0, 2).reshape(128, D),
        "router_w2": f["router_w2"].T,
        "router_b1": f["router_b1"].reshape(128, 1),
        "router_b2": f["router_b2"].reshape(1, 2 * NEXP),
    }
    nc = bacc.Bacc("TRN2", target_bir_lowering=False, num_devices=1)
    arrays, args = {}, []
    for name, v in data.items():
        v = np.ascontiguousarray(v)
        arrays[f"in_{name}"] = v
        args.append(nc.dram_tensor(f"in_{name}", v.shape, mybir.dt.from_np(v.dtype), kind="ExternalInput").ap())
    out = nc.dram_tensor("out_x", (NT, P, D), F32, kind="ExternalOutput").ap()
    gnn_ffn_program(nc, *args, out)
    got = run_bass_kernel_spmd(nc, [arrays], core_ids=[0])
    return got.results[0]["out_x"].reshape(T, D)
```

```python
from collections import namedtuple
from contextlib import ExitStack

import concourse.bass as bass
from concourse import mybir

F32 = mybir.dt.float32
F32R = mybir.dt.float32r
BF16 = mybir.dt.bfloat16
I32 = mybir.dt.int32
ALU = mybir.AluOpType
ACT = mybir.ActivationFunctionType
AX = mybir.AxisListType
ds = bass.ds

T, D, H, HD, NEXP = 1250, 512, 8, 64, 4
P = 125
NT = T // P
KC = D // 128
E = 41250
EC = E // P
EQ, EJ = 110, 3
WD = 25
NW = T // WD
WK = WD * NT
EPS = 1e-5
SCALE = float(HD) ** -0.5
BANK = 512
CHUNKS = [(0, 512), (512, 512), (1024, 226)]
EG = 4
EP = -(-EC // EG) * EG
EA = 2
RING = 2
X_LOADS = [(0, 2), (2, 5), (5, NT)]
SEG = 5
HG = NT // 2
NQ = 4

ORDER = ["g1l", "g1r", "g2l", "g2r", "qs", "ks", "vs", "us", "qc", "qt", "kt", "vt", "ut", "kc", "vc", "uc"]
UNIT = {n: 4 * i for i, n in enumerate(ORDER)}
UNIT["mlp"] = 4 * len(ORDER)
G0, S0 = 0, 16
T0 = S0 + 16 * NEXP
C0 = T0 + 16 * NEXP
M0 = C0 + 16
ROWB = dict(g1=0, g2=1, vs=2, vt=2 + NEXP, vc=2 + 2 * NEXP, uc=3 + 2 * NEXP, m2=4 + 2 * NEXP)


def Sems(make, prefix, names):
    names = names.split()
    return namedtuple(prefix, names)(*[make(f"{prefix}_{n}") for n in names])


class Chain:

    def __init__(self, eng, sem, base=0):
        self.eng, self.sem, self.base, self.n = eng, sem, base, 0

    def __call__(self, ins):
        self.n += 1
        ins.then_inc(self.sem, 1)
        self.eng.wait_ge(self.sem, self.base + self.n)


class Attn:

    def __init__(self, turn, causal):
        self.turn, self.causal = turn, causal
        self.blocks = [i + 1 if causal else NT for i in range(NT)] * 2
        self.banks = [(b + 3) // 4 for b in self.blocks]
        self.cols = [P * b for b in self.blocks]
        self.parts = [1 + (c > BANK) for c in self.cols]
        self.cum = [sum(self.banks[:n]) for n in range(2 * NT + 1)]
        self.cum_parts = [sum(self.parts[:n]) for n in range(2 * NT + 1)]
        self.total = self.cum[-1]
        self.total_parts = self.cum_parts[-1]
        full, half = 6 * NT, 2 * sum((i + 4) // 4 for i in range(NT))
        self.tiles0 = 2 * NT * (H // 2 + 1) * turn
        self.groups0 = 2 * HG * (H // 2 + 1) * turn
        self.banks0 = (H // 2 + 1) * (0, full, full + half)[turn]
        full, half = 4 * NT, 2 * sum(1 + (P * (i + 1) > BANK) for i in range(NT))
        self.parts0 = (H // 2 + 1) * (0, full, full + half)[turn]
        self.cuts0 = 7 * H * turn
        self.qin0 = 32 * H * turn
        full, half = 6 * HG, 4 * HG + 2 * sum(P * (2 * g + 1) > BANK for g in range(HG)) + 2 * NT
        self.links = half if causal else full
        self.links0 = H // 2 * (0, full, full + half)[turn]

    def tile(self, hp, n):
        return self.tiles0 + 2 * NT * (hp + 1) + n + 1

    def bank(self, hp, n, b):
        return self.banks0 + self.total * (hp + 1 + n // (2 * NT)) + self.cum[n % (2 * NT)] + b + 1

    def part(self, hp, n, p):
        return (self.parts0 + self.total_parts * (hp + 1 + n // (2 * NT)) + self.cum_parts[n % (2 * NT)] + p + 1)

    def group(self, hp, g):
        return self.groups0 + 2 * HG * (hp + 1) + g + 1


def gnn_ffn_program(nc, x, src, dst, weights, qkv_bias, out_bias, row_bias, ln_cols, mlp_b1,
                    router_w1, router_w2, router_b1, router_b2, out):
    with ExitStack() as ctx:
        def sb(name, shape, dt=F32):
            return ctx.enter_context(nc.sbuf_tensor(name, shape, dt))

        def sem(name):
            return ctx.enter_context(nc.semaphore(name))

        F = sb("F", [128, 22620])
        R = sb("R", [128, 22740], F32R)
        w_raw = sb("w_raw", [128, 2, 512])
        w_hi = sb("w_hi", [128, 4, 512], F32R)
        w_lo = sb("w_lo", [128, 4, 512], F32R)
        TB = sb("TB", [128, 3, 512])
        brow = sb("brow", [128, 512])
        ident = sb("ident", [128, 128])
        ones = sb("ones", [128, HD])
        ones_r = sb("ones_r", [128, 2], F32R)
        bcol = sb("bcol", [128, 12])
        bcol_q = sb("bcol_q", [128, 4])
        ocol = sb("ocol", [128, 4])
        lncol = sb("lncol", [128, 6, 4])
        b1col = sb("b1col", [128, 16])
        stats = sb("stats", [128, 2, 6])
        mv = sb("mv", [128, 2, 2])
        sd = sb("sd", [128, 2, 2])
        mr1 = sb("mr1", [128, NT, 2])
        rcnt = sb("rcnt", [128, NT, 1])
        cntm = sb("cntm", [128, 2])
        ngm = sb("ngm", [128, 2])
        rs = sb("rs", [128, 2, 4])
        rr = sb("rr", [128, 2])
        rt = sb("rt", [128, 48])
        eps_t = sb("eps_t", [128, 1])
        zero = sb("zero", [128, 1])
        idx_i = sb("idx_i", [1, 2], I32)
        win = sb("win", [1, NW], I32)
        wide = sb("wide", [1, NW + 1])
        many = sb("many", [1, 1], I32)
        ps = ctx.enter_context(nc.psum_tensor("ps", [128, 8, BANK], F32))

        def flat(a):
            return ps[:, 3 * a:3 * a + 3, :].rearrange("p a b -> p (a b)")

        def rows(a):
            return a.rearrange("p (i f) -> p i f", i=NT)

        def cols(a):
            return a.rearrange("p (k t) -> p k t", k=KC)

        AT = F[:, 0:12500].rearrange("p (h d) -> p h d", h=NT)
        RW = rows(F[:, 12500:17620])
        ZT = cols(F[:, 17620:22620])
        XA = rows(F[:, 0:5120])
        e_base = 12500

        def eview(off, n, parts=P):
            return F[0:parts, e_base + off:e_base + off + n]
        s_i = eview(0, 375, EQ).bitcast(I32)
        d_i = eview(375, 375, EQ).bitcast(I32)
        s_f = eview(750, 375, EQ)
        d_f = eview(1125, 375, EQ)
        h_f = eview(1500, 375, EQ)
        l_f = eview(0, 375, EQ)
        k_f = eview(375, 375, EQ)
        mm2 = eview(1875, 6, EQ)
        loT = eview(1882, EP)
        keyT = eview(2214, EP)
        wcol = eview(2546, 8, NW)
        woff = eview(2554, NW)
        iota_b = eview(2604, 128).bitcast(BF16)
        zero_b = eview(2732, 125).bitcast(BF16)
        oh_key = eview(2858, RING * EG * 125).bitcast(BF16).rearrange("p (r g c) -> p r g c", r=RING, g=EG)
        oh_lo = eview(3858, RING * EG * 64).bitcast(BF16).rearrange("p (r g c) -> p r g c", r=RING, g=EG)
        dbc = eview(2858, 2 * EC, NW)
        msk = eview(3518, EC, NW)
        cid = eview(4370, EP, NW)
        sq_lo = eview(4370, RING * EG * 64).bitcast(BF16).rearrange("p (r g c) -> p r g c", r=RING, g=EG)
        QK = F[:, 0:10000].rearrange("p (j m t) -> p j m t", j=2, m=KC)
        V = rows(F[:, 10000:15120])
        XR = cols(F[:, 10000:15000])
        PB = F[:, 15120:17620].rearrange("p (b t) -> p b t", b=2)
        ACC = rows(F[:, 0:5120])
        XL = rows(F[:, 4880:10000])
        YL = V
        w1r = F[:, 15120:15632]
        w2r = F[:, 15632:15640]
        prow = F[0:1, 15700:16212]
        diag = TB[:, 0, 0:250].rearrange("p (s t) -> p s t", s=2)
        comb = TB[0:HD, 1, 0:252]
        mask = TB[0:P, 0, 256:256 + P]

        X0 = (cols(R[:, 0:5000]), cols(R[:, 5000:10000]))
        X1 = (cols(R[:, 10000:15000]), cols(R[:, 15000:20000]))
        Y = (rows(R[:, 10000:15120]), rows(R[:, 15120:20240]))
        AS = [[R[0:P, 20240 + 1250 * p + 625 * h:20240 + 1250 * p + 625 * h + 625]
               .rearrange("p (c d) -> p c d", c=5) for h in range(2)] for p in range(2)]
        HB = 10080
        QSH = [R[:, HB:HB + 1250], R[:, HB + 1250:HB + 2500]]
        QSL = [R[:, HB + 2500:HB + 3750], R[:, HB + 3750:HB + 5000]]
        KS = [R[:, HB + 5000:HB + 6250], R[:, HB + 6250:HB + 7500]]
        VS = [R[0:P, HB + 7500 + 1280 * b:HB + 8780 + 1280 * b].rearrange("p (c n) -> p c n", c=NT) for b in range(2)]
        KT = R[:, HB + 10060:HB + 10060 + 1250]
        PT = [R[0:P, 5040 * p:5040 * p + 5040]
              .rearrange("p (g c s t) -> p g c s t", g=2, c=NT, s=2) for p in range(2)]

        mm_d = nc.dram_tensor("mm_d", [2, EC], F32, kind="Internal").ap()
        x1_d = nc.dram_tensor("x1_d", [NT, P, D], F32, kind="Internal").ap()
        zt_d = nc.dram_tensor("zt_d", [128, KC, T], F32, kind="Internal").ap()
        xt_d = nc.dram_tensor("xt_d", [128, KC, T], F32, kind="Internal").ap()
        qc_d = nc.dram_tensor("qc_d", [128, KC, T], F32, kind="Internal").ap()

        def groups_of(eng, w):
            both = eng.value_load(win[0:1, ds(w, 1)], min_val=1, max_val=128 * (EP // EG - 1) + EP // EG)
            why = "VectorE packs group numbers below EP / EG into both"
            first = nc.s_assert_within(eng.snap(both >> 7), 0, EP // EG - 1, skip_runtime_bounds_check_because=why)
            end = nc.s_assert_within(eng.snap(both & 127), 1, EP // EG, skip_runtime_bounds_check_because=why)
            return first, end

        const_ok, small_in, w_split, w_used = (sem(n) for n in ("const_ok", "small_in", "w_split", "w_used"))
        w_in = [sem("w_in0"), sem("w_in1")]
        ln_names = "src0 src1 var std nrm tr ev lk"
        ln0, ln2, ln3 = (Sems(sem, n, ln_names) for n in ("lnx", "lnz", "lnm"))
        y_norm, y_ready = sem("y_norm"), sem("y_ready")
        x_in = [sem(f"x_in{i}") for i in range(3)]
        ln1 = Sems(sem, "h", "nrm tr ev lk")
        sp = {n: Sems(sem, "cut_" + n, names) for n, names in
              dict(x="hi lo", h="hi lo", s="val hi lo", os="hi lo", t="val hi lo st0 st1", ot="hi lo", oc="hi lo",
                   m="hi lo").items()}
        pj = {n: Sems(sem, "prod_" + n, names) for n, names in
              dict(g="ps a v", qk="a", v="ps v", u="a v t", uc="ps v", m1="a v t", m2="ps a v").items()}
        A = Sems(sem, "att", "qin0 qin1 cut scores negmax exp tr hi lo pv diag bc bot post lk")
        KS_, KT_, KC_ = Attn(0, False), Attn(1, True), Attn(2, False)
        ag = [Sems(sem, f"agg{n}", "hi lo pe cnt dv") for n in range(2)]
        e = Sems(sem, "edge", "in_ lk tr mm mmd mmi w win ev many")
        key_ready, lo_sq, lo_ready, oh_used, at_ready, at_free = (
            sem(n) for n in ("key_ready", "lo_sq", "lo_ready", "oh_used", "at_ready", "at_free"))
        r = Sems(sem, "router", "in_ sums row tr col h he l i lk")
        bcol_in = [sem(f"bcol_in{i}") for i in range(4)]
        ocol_in = [sem(f"ocol_in{i}") for i in range(2)]
        row_in, row_free, xr_in, qc_st, qc_in, zt_in, x1_st, fin, out_st, biasq, pad_ok, mask_ok, ysum, zt_st, held = (
            sem(n) for n in ("row_in", "row_free", "xr_in", "qc_st", "qc_in", "zt_in", "x1_st", "fin", "out_st",
                             "biasq", "pad_ok", "mask_ok", "ysum", "zt_st", "held"))

        block = ctx.enter_context(nc.Block())

        @block.sync
        def _(eng):
            def load_units(unit, count, dram):
                for j in range(count):
                    if not isinstance(unit, int) or unit + j >= 2:
                        eng.wait_ge(w_split, 2 * (unit + j) - 2)
                    eng.dma_start(w_raw[:, j % 2, :], weights[ds(dram + j, 1), :, :].rearrange("a p c -> p (a c)")
                                  ).then_inc(w_in[j % 2], 16)

            def load_row(n, row):
                if n:
                    eng.wait_ge(row_free, n)
                eng.dma_start(brow[0:P, :], row_bias[ds(row, 1), :].to_broadcast([P, D])).then_inc(row_in, 16)

            def load_tiles(L, source):
                with eng.Fori(0, NT // 2) as i2:
                    for b in range(2):
                        eng.wait_ge(L.tr, 2 * i2 + b + 1)
                        eng.dma_start(TB[0:P, b, :], source[ds(2 * i2 + b, 1), :, :].rearrange("a p f -> p (a f)")
                                      ).then_inc((L.src0, L.src1)[b], 16)

            def load_heads(K):
                with eng.Fori(0, H // 2) as hp:
                    for b in range(2):
                        eng.wait_ge(A.scores, K.tile(hp, NT * (b - 1) - 1))
                        for half in range(2):
                            for j, t in ((0, QSL), (1, KS)):
                                eng.dma_start(t[b][64 * half:64 * half + 64, :].bitcast(F32),
                                              QK[64 * b:64 * b + 64, j, ds(hp, 1), :].rearrange("p a t -> p (a t)")
                                              ).then_inc((A.qin0, A.qin1)[b], 16)

            eng.dma_start(s_i, src.rearrange("(q r) -> q r", q=EQ)).then_inc(e.in_, 16)
            eng.dma_start(d_i, dst.rearrange("(q r) -> q r", q=EQ)).then_inc(e.in_, 16)
            for n, (lo, hi) in enumerate(X_LOADS):
                eng.dma_start(XA[0:P, lo:hi, :], x[lo:hi, :, :].rearrange("i p f -> p i f")).then_inc(x_in[n], 16)
            eng.dma_start(lncol[:], ln_cols).then_inc(small_in, 16)
            eng.dma_start(b1col[:], mlp_b1).then_inc(small_in, 16)
            eng.dma_start(rt[:, 0:1], router_b1).then_inc(small_in, 16)
            eng.dma_start(rt[0:1, 8:16], router_b2).then_inc(small_in, 16)
            eng.wait_ge(e.mm, 2)
            eng.dma_start(mm_d.rearrange("m (q j) -> q m j", j=EJ), mm2.rearrange("q (m j) -> q m j", m=2)
                          ).then_inc(e.mmd, 16)
            eng.wait_ge(e.mmd, 16)
            eng.dma_start(dbc, mm_d.rearrange("m c -> (m c)").unsqueeze(0).to_broadcast([NW, 2 * EC])
                          ).then_inc(e.mmi, 16)
            eng.wait_ge(e.w, 2)
            eng.dma_start(win[:, :].unsqueeze(2), wcol[:, 7:8].bitcast(I32)).then_inc(e.win, 16)
            eng.dma_start(wide[:, 0:NW].unsqueeze(2), wcol[:, 6:7]).then_inc(e.win, 16)
            load_row(0, ROWB["g1"])
            load_units(0, 16, G0)
            load_row(1, ROWB["g2"])
            load_tiles(ln2, x)
            with eng.Fori(0, NT) as i:
                eng.wait_ge(ysum, i + 1)
                eng.dma_start(x1_d[ds(i, 1), :, :].rearrange("a p f -> p (a f)"),
                              RW[0:P, ds(i, 1), :].rearrange("p a f -> p (a f)")).then_inc(x1_st, 16)
            eng.wait_ge(x1_st, 16 * NT)
            eng.dma_start(w1r, router_w1).then_inc(r.in_, 16)
            eng.dma_start(w2r, router_w2).then_inc(r.in_, 16)
            eng.wait_ge(r.i, 2)
            e_s = eng.value_load(idx_i[0:1, 0:1], min_val=0, max_val=NEXP - 1)
            load_units(UNIT["qs"], 2, e_s * 16 + S0)
            e_t = eng.value_load(idx_i[0:1, 1:2], min_val=0, max_val=NEXP - 1)
            eng.dma_start(bcol[:], qkv_bias[ds(e_s, 1), :, :].rearrange("a p c -> p (a c)")).then_inc(bcol_in[0], 16)
            eng.dma_start(ocol[:], out_bias[ds(e_s, 1), :, :].rearrange("a p c -> p (a c)")).then_inc(ocol_in[0], 16)
            load_row(2, e_s + ROWB["vs"])
            load_units(UNIT["qs"] + 2, 2, e_s * 16 + (S0 + 2))
            eng.dma_start(zt_d, ZT).then_inc(zt_st, 16)
            load_units(UNIT["ks"], 8, e_s * 16 + (S0 + 4))
            eng.wait_ge(pj["qk"].a, 8)
            eng.wait_ge(zt_st, 16)
            load_heads(KS_)
            load_units(UNIT["us"], 4, e_s * 16 + (S0 + 12))
            load_units(UNIT["qc"], 4, C0)
            eng.dma_start(bcol[:], qkv_bias[2 * NEXP, :, :]).then_inc(bcol_in[1], 16)
            load_row(3, e_t + ROWB["vt"])
            eng.wait_ge(sp["os"].lo, KC)
            eng.wait_ge(zt_st, 16)
            eng.dma_start(ZT, zt_d).then_inc(zt_in, 16)
            eng.wait_ge(pj["u"].v, 4)
            eng.dma_start(ocol[:], out_bias[ds(e_t + NEXP, 1), :, :].rearrange("a p c -> p (a c)")
                          ).then_inc(ocol_in[1], 16)
            load_units(UNIT["qt"], 4, e_t * 16 + T0)
            for m in range(4):
                eng.wait_ge(pj["qk"].a, 9 + m)
                eng.dma_start(qc_d[:, m, :], QK[:, 0, m, :]).then_inc(qc_st, 16)
            eng.dma_start(bcol[:], qkv_bias[ds(e_t + NEXP, 1), :, :].rearrange("a p c -> p (a c)")
                          ).then_inc(bcol_in[2], 16)
            for k in range(KC):
                eng.wait_ge(sp["t"].val, k + 1)
                eng.dma_start(xt_d[:, k, :], PB[:, k % 2, :]).then_inc((sp["t"].st0, sp["t"].st1)[k % 2], 16)
            load_units(UNIT["kt"], 8, e_t * 16 + (T0 + 4))
            eng.wait_ge(pj["qk"].a, 20)
            load_heads(KT_)
            load_units(UNIT["ut"], 4, e_t * 16 + (T0 + 12))
            eng.wait_ge(A.cut, 14 * H)
            eng.wait_ge(sp["t"].st0, 32)
            eng.wait_ge(sp["t"].st1, 32)
            eng.dma_start(XR, xt_d).then_inc(xr_in, 16)
            eng.dma_start(bcol[:], qkv_bias[2 * NEXP, :, :]).then_inc(bcol_in[3], 16)
            load_row(4, ROWB["vc"])
            eng.wait_ge(qc_st, 16 * 4)
            eng.dma_start(QK[:, 0, :, :], qc_d).then_inc(qc_in, 16)
            load_units(UNIT["kc"], 8, C0 + 4)
            eng.wait_ge(pj["qk"].a, 24)
            eng.wait_ge(qc_in, 16)
            load_heads(KC_)
            load_row(5, ROWB["uc"])
            eng.wait_ge(A.cut, 21 * H)
            eng.dma_start(XL[0:P], x1_d.rearrange("i p f -> p i f")).then_inc(ln3.src0, 16)
            load_units(UNIT["uc"], 4, C0 + 12)
            load_row(6, ROWB["m2"])
            with eng.Fori(0, NQ) as q:
                load_units(q * 8 + UNIT["mlp"], 4, q * 4 + M0)
                load_units(q * 8 + (UNIT["mlp"] + 4), 4, q * 4 + (M0 + 16))
            for i in range(NT):
                eng.wait_ge(fin, i + 1)
                eng.dma_start(out[i, :, :], ACC[0:P, i, :]).then_inc(out_st, 16)
            eng.wait_ge(out_st, 16 * NT)

        @block.gpsimd
        def _(eng):
            eng.memset(ident[:], 0.0).then_inc(const_ok, 1)
            eng.memset(ones[:], 1.0).then_inc(const_ok, 1)
            eng.memset(ones_r[:].bitcast(F32), 1.0).then_inc(const_ok, 1)
            eng.memset(eps_t[:], EPS).then_inc(const_ok, 1)
            eng.memset(zero[:], 0.0).then_inc(const_ok, 1)
            eng.wait_ge(const_ok, 1)
            eng.affine_select(out=ident[:], in_=ident[:], compare_op=ALU.not_equal, fill=1.0, base=0,
                              pattern=[[-1, 128]], channel_multiplier=1).then_inc(const_ok, 1)
            for t, step, count, per_partition in ((iota_b[:, 0:250], 1, 250, 0), (woff, WK, NW, 0), (cid, 1, EP // EG, 0),
                                                  (wcol[:, 0:1], 1, 1, WD), (rt[0:1, 16:20], -1, 4, 0)):
                eng.iota(t, pattern=[[step, count]] + ([[0, EG]] if t is cid else []), base=4 if step < 0 else 0, channel_multiplier=per_partition,
                         allow_small_or_imprecise_dtypes=True).then_inc(const_ok, 1)
            eng.memset(zero_b, 0.0).then_inc(const_ok, 1)
            eng.memset(loT[:, EC:EP], 0.0).then_inc(const_ok, 1)
            eng.memset(keyT[:, EC:EP], -1.0).then_inc(const_ok, 1)

            def hi_part(to, a):
                return eng.tensor_tensor(to, a, zero[0:to.shape[0], :].to_broadcast(list(to.shape)), ALU.add)

            def cut_unit(u, s):
                if isinstance(u, int):
                    eng.wait_ge(w_in[s % 2], 16 * (u // 2 + 1))
                    if u >= 4:
                        eng.wait_ge(w_used, u - 3)
                else:
                    eng.wait_ge(w_in[s % 2], (u - s % 2) * 8 + 16)
                    eng.sem_inc(held, 1)
                    eng.wait_ge(w_used, u - 3)
                    eng.sem_inc(held, 1)
                hi_part(w_hi[:, s, :], w_raw[:, s % 2, :]).then_inc(w_split, 1)
                eng.wait_ge(w_split, 2 * u + 1)
                eng.tensor_tensor(w_lo[:, s, :], w_raw[:, s % 2, :], w_hi[:, s, :].bitcast(F32), ALU.subtract
                                  ).then_inc(w_split, 1)

            def cut_units(unit, end):
                for u in range(unit, end):
                    cut_unit(u, u % 4)

            def cut_heads(K):
                eng.sem_inc(A.scores, 2 * NT)
                with eng.Fori(0, H // 2) as hp:
                    for b in range(2):
                        n0 = K.cuts0 + 14 * hp + 7 * b
                        eng.wait_ge((A.qin0, A.qin1)[b], K.qin0 + 64 * hp + 64)
                        eng.sem_inc(held, 1)
                        hi_part(QSH[b], QSL[b].bitcast(F32)).then_inc(A.cut, 1)
                        eng.wait_ge(A.cut, n0 + 1)
                        eng.sem_inc(held, 1)
                        eng.tensor_tensor(KT[64:128, :], KS[b][64:128, :].bitcast(F32),
                                          zero[64:128, :].to_broadcast([64, T]), ALU.add).then_inc(A.cut, 1)
                        eng.wait_ge(A.cut, n0 + 2)
                        eng.sem_inc(held, 1)
                        hi_part(KS[b][0:64, :], KS[b][0:64, :].bitcast(F32)).then_inc(A.cut, 1)
                        eng.wait_ge(A.cut, n0 + 3)
                        eng.tensor_tensor(QSL[b], QSL[b].bitcast(F32), QSH[b].bitcast(F32), ALU.subtract
                                          ).then_inc(A.cut, 1)
                        eng.wait_ge(A.cut, n0 + 4)
                        eng.tensor_tensor(KS[b][64:128, :], KS[b][64:128, :].bitcast(F32), KT[64:128, :].bitcast(F32),
                                          ALU.subtract).then_inc(A.cut, 1)
                        eng.wait_ge(A.cut, n0 + 5)
                        eng.wait_ge(A.pv, K.group(hp, HG * (b - 1) - 1))
                        eng.sem_inc(held, 1)
                        eng.wait_ge(pj["v"].v, NT * (K.turn + 1))
                        vh = V[0:P, :, ds(128 * hp + 64 * b, 64)]
                        eng.tensor_copy(VS[b][:, :, 0:64], vh).then_inc(A.cut, 1)
                        eng.wait_ge(A.cut, n0 + 6)
                        eng.sem_inc(held, 1)
                        eng.tensor_tensor(VS[b][:, :, 64:128], vh, VS[b][:, :, 0:64].bitcast(F32), ALU.subtract
                                          ).then_inc(A.cut, 1)

            cut_units(0, UNIT["us"])
            cut_heads(KS_)
            cut_units(UNIT["us"], UNIT["ut"])
            eng.memset(mask, 0.0).then_inc(mask_ok, 1)
            eng.wait_ge(mask_ok, 1)
            eng.affine_select(out=mask, in_=mask, compare_op=ALU.is_ge, fill=-1e30, base=0,
                              pattern=[[-1, P]], channel_multiplier=1).then_inc(mask_ok, 1)
            cut_heads(KT_)
            cut_units(UNIT["ut"], UNIT["uc"])
            cut_heads(KC_)
            cut_units(UNIT["uc"], UNIT["mlp"])
            eng.wait_ge(A.cut, 21 * H)
            eng.wait_ge(row_in, 16 * 6)
            eng.wait_ge(ln3.src0, 16)
            for i in range(NT):
                y = YL[0:P, i, :]
                eng.tensor_scalar(y, XL[0:P, i, :], mr1[0:P, i, 0:1], mr1[0:P, i, 1:2], ALU.subtract, ALU.mult
                                  ).then_inc(y_norm, 1)
                eng.wait_ge(y_norm, i + 1)
                eng.tensor_tensor(y, y, brow[0:P, :], ALU.add).then_inc(y_ready, 1)
            eng.wait_ge(y_ready, NT)
            eng.sem_inc(row_free, 1)
            for i in range(NT):
                tk = slice(P * i, P * i + P)
                eng.wait_ge(ln3.ev, i + 3)
                eng.tensor_tensor(X0[0][:, :, tk], ZT[:, :, tk], zero[:, :].unsqueeze(2).to_broadcast([128, KC, P]),
                                  ALU.add).then_inc(sp["m"].hi, 1)
            with eng.Fori(0, 2 * NQ) as q:
                for s in range(4):
                    cut_unit(q * 4 + (UNIT["mlp"] + s), s)

        @block.tensor
        def _(eng):
            def three(to, ah, al, bh, bl, first, last):
                eng.matmul(to, ah, bh, start=first, stop=False)
                eng.matmul(to, al, bh, start=False, stop=False)
                return eng.matmul(to, ah, bl, start=False, stop=last)

            def turn(L, b, i, source=None):
                eng.wait_ge(L.nrm, i + 1)
                eng.wait_ge(L.ev, i + 1)
                t = 2 if L is ln2 else b
                for k in range(KC):
                    a = TB[0:P, t, 128 * k:128 * k + 128] if source is None else source[:, 128 * k:128 * k + 128]
                    ins = eng.transpose(ps[:, 6 + b, P * k:P * k + P], a, ident[0:P, 0:P])
                ins.then_inc(L.tr, 1)

            def product_cols(J, unit, X, free, n0=0, k_ready=None, k0=0, last=None):
                for m in range(4):
                    eng.wait_ge(w_split, 2 * (unit + m) + 2)
                    if not isinstance(n0, int) or n0 + m >= 2:
                        eng.wait_ge(free, n0 + m - 1)
                    if last is not None and m < 2:
                        eng.wait_ge(last[0], last[1] - 1 + m)
                    for c, (lo, n) in enumerate(CHUNKS):
                        for k in range(KC):
                            if m == 0 and c == 0 and k_ready is not None:
                                eng.wait_ge(k_ready, k0 + k + 1)
                            wk = slice(128 * k, 128 * k + 128)
                            ins = three(flat(m % 2)[:, lo:lo + n], w_hi[:, m, wk], w_lo[:, m, wk],
                                        X[0][:, k, lo:lo + n], X[1][:, k, lo:lo + n], k == 0, k == KC - 1)
                    ins.then_inc(w_used, 1)

            def product_tile(J, i, unit, X, free, n0=0, ready=None, k0=0):
                if not isinstance(n0, int) or n0 + i >= 2:
                    eng.wait_ge(free, n0 + i - 1)
                tk = slice(P * i, P * i + P)
                for k in range(KC):
                    if i == 0:
                        eng.wait_ge(w_split, 2 * (unit + k) + 2)
                        if ready is not None:
                            eng.wait_ge(ready, k0 + k + 1)
                    ins = three(ps[0:P, 6 + i % 2, :], X[0][:, k, tk], X[1][:, k, tk],
                                w_hi[:, k, :], w_lo[:, k, :], k == 0, k == KC - 1)
                    if i == NT - 1 and k < KC - 1:
                        ins.then_inc(w_used, 1)
                ins.then_inc(J.ps, 1)
                if i == NT - 1:
                    eng.wait_ge(J.ps, n0 + NT)
                    eng.sem_inc(w_used, 1)

            def product_rows(J, unit, X, free, n0=0, ready=None):
                for i in range(NT):
                    product_tile(J, i, unit, X, free, n0, ready)

            pair = eng.alloc_register("pair")

            def adjacency(first_w2, end_w2):
                with eng.Fori(first_w2, end_w2) as w2:
                    for j in range(2):
                        w = 2 * w2 + j
                        acc = ps[:, j, 0:WK]
                        first, end = groups_of(eng, w)
                        eng.wait_ge(at_free, w + 1)
                        eng.matmul(acc, zero_b[:, 0:128], zero_b[:, 0:WK], start=True, stop=False)
                        with eng.Fori(first, end):
                            now = eng.snap(pair)
                            slot = eng.snap(now & (RING - 1))
                            eng.wait_ge(lo_ready, now + 1)
                            eng.wait_ge(key_ready, now + 1)
                            for g in range(EG):
                                ins = eng.matmul(acc, oh_lo[:, ds(slot, 1), g, :].rearrange("p a c -> p (a c)"),
                                                 oh_key[:, ds(slot, 1), g, :].rearrange("p a c -> p (a c)"),
                                                 start=False, stop=False)
                            ins.then_inc(oh_used, 1)
                            eng.reg_add(pair, pair, 1)
                        eng.matmul(acc, zero_b[:, 0:128], zero_b[:, 0:WK], start=False, stop=True).then_inc(at_ready, 1)

            def aggregate(layer, nlo):
                L, A = (ln1, ln2)[layer], ag[layer]

                def sums(i, b):
                    eng.wait_ge(A.dv, i + 1)
                    to, cnt = ps[0:P, b, :], ps[0:P, 2 + b, 0:2]

                    def chunk_hi(h, c):
                        k = 5 * h + c
                        eng.matmul(to, AS[0][h][:, c, :], Y[0][0:P, k, :], start=(k == 0), stop=False)
                        ins = eng.matmul(to, AS[0][h][:, c, :], Y[1][0:P, k, :], start=False, stop=(k == NT - 1))
                        if layer == 0:
                            ins = eng.matmul(cnt, AS[0][h][:, c, :], ones_r[0:P, :], start=(k == 0), stop=(k == NT - 1))
                        return ins
                    for h in range(2):
                        eng.wait_ge(A.hi, 2 * i + h + 1)
                        chunk_hi(h, 0)
                        with eng.If(nlo > 0):
                            eng.wait_ge(A.lo, 2 * i + h + 1)
                            for c in range(5):
                                eng.matmul(to, AS[1][h][:, c, :], Y[0][0:P, 5 * h + c, :], start=False, stop=False)
                                if layer == 0:
                                    eng.matmul(cnt, AS[1][h][:, c, :], ones_r[0:P, :], start=False, stop=False)
                        for c in range(1, 5):
                            ins = chunk_hi(h, c)
                        ins.then_inc(A.pe, 1)

                def finish(i, b):
                    if layer == 1:
                        eng.wait_ge(ysum, i + 1)
                        eng.matmul(ps[0:1, 4, :], ones[0:P, 0:1], TB[0:P, b, :], start=False, stop=False
                                   ).then_inc(r.sums, 1)
                    turn(L, b, i)

                sums(0, 0)
                with eng.Fori(0, NT // 2 - 1) as i2:
                    sums(2 * i2 + 1, 1)
                    finish(2 * i2, 0)
                    sums(2 * i2 + 2, 0)
                    finish(2 * i2 + 1, 1)
                sums(NT - 1, 1)
                finish(NT - 2, 0)
                finish(NT - 1, 1)

            def scores(K, hp, n):
                b, i = n // NT % 2, n % NT
                nxt = n // (2 * NT)
                if i == 0:
                    eng.wait_ge(A.cut, K.cuts0 + 14 * (hp + nxt) + 7 * b + 5)
                for c, (lo, w) in enumerate(CHUNKS):
                    if lo >= K.cols[i]:
                        continue
                    w = min(w, K.cols[i] - lo)
                    w += w % 2
                    before = min(c, K.banks[(n - 2) % NT] - 1)
                    eng.wait_ge(A.lo, K.bank(hp, n - 2, before))
                    to = flat(n % 2)[0:P, lo:lo + w]
                    eng.matmul(to, QSH[b][:, P * i:P * i + P], KS[b][:, lo:lo + w], start=True, stop=False)
                    ins = eng.matmul(to, QSL[b][:, P * i:P * i + P], KS[b][:, lo:lo + w], start=False, stop=True)
                ins.then_inc(A.scores, 1)

            def turn_probs(K, hp, n):
                for bank in range(K.banks[n]):
                    eng.wait_ge(A.exp, K.part(hp, n, min(bank, K.parts[n] - 1)))
                    for q in range(min(4, K.blocks[n] - 4 * bank)):
                        c = 4 * bank + q
                        ins = eng.transpose(ps[0:P, 3 * (n % 2) + bank, P * q:P * q + P],
                                            PB[0:P, n % 2, P * c:P * c + P], ident[0:P, 0:P])
                    ins.then_inc(A.tr, 1)

            def values(K, hp, g, half):
                b, gh = g // HG % 2, g % HG
                n = K.blocks[2 * g + 1]
                if half == 0:
                    eng.wait_ge(A.lo, K.bank(hp, 2 * g + 1, K.banks[2 * g + 1] - 1))
                    eng.wait_ge(A.post, K.group(hp, g - 1))
                    if gh == 0:
                        eng.wait_ge(A.cut, K.cuts0 + 14 * hp + 7 * b + 7)
                for c in range(n // 2 * half, n if half else n // 2):
                    s = 1 if c >= K.blocks[2 * g] else 0
                    for p in range(2):
                        rhs = PT[p][:, g % 2, c, s:2, :].rearrange("p s t -> p (s t)")
                        ins = eng.matmul(ps[:, 6, 126 * s:252], VS[b][:, c, :], rhs, start=(c == 0 and p == 0),
                                         stop=(c == n - 1 and p == 1))
                if half == 0:
                    return
                ins.then_inc(A.pv, 1)
                eng.wait_ge(A.diag, K.group(hp, g))
                for s in range(2):
                    ins = eng.matmul(ps[0:HD, 7, P * s:P * s + P], ones[0:P, :], diag[0:P, s, :], start=True, stop=True)
                ins.then_inc(A.bc, 1)

            def attend(K):
                scores(K, 0, 0)

                def body(hp, first=False, last=False):
                    for n in range(2 * NT):
                        if not (last and n == 2 * NT - 1):
                            scores(K, hp, n + 1)
                        turn_probs(K, hp, n)
                        if n >= 2 or not first:
                            values(K, hp, n // 2 - 1, n % 2)
                    if last:
                        for half in range(2):
                            values(K, hp, 2 * HG - 1, half)
                body(0, first=True)
                with eng.Fori(1, H // 2 - 1) as hp:
                    body(hp)
                body(H // 2 - 1, last=True)

            eng.wait_ge(const_ok, 6)
            eng.wait_ge(e.mm, 1)
            for bank, t in ((4, l_f), (5, k_f)):
                for j in range(EJ):
                    ins = eng.transpose(ps[0:P, bank, EQ * j:EQ * j + EQ], t[:, P * j:P * j + P], ident[0:EQ, 0:EQ])
            ins.then_inc(e.tr, 1)
            for i in range(NT):
                turn(ln0, i % 2, i, XA[0:P, i, :])
            eng.wait_ge(const_ok, 14)
            eng.wait_ge(e.win, 32)
            eng.reg_mov(pair, 0)
            for seg in range(SEG):
                adjacency(NW // 2 // SEG * seg, NW // 2 // SEG * (seg + 1))
                for i in range(NT // SEG * seg, NT // SEG * (seg + 1)):
                    product_tile(pj["g"], i, UNIT["g1l"], X0, pj["g"].v, ready=sp["x"].lo)
            product_rows(pj["g"], UNIT["g1r"], X0, pj["g"].v, n0=NT)
            eng.wait_ge(e.many, 1)
            nlo = eng.value_load(many[0:1, 0:1], min_val=0, max_val=1)
            aggregate(0, nlo)
            product_rows(pj["g"], UNIT["g2l"], X0, pj["g"].v, n0=2 * NT, ready=sp["h"].lo)
            product_rows(pj["g"], UNIT["g2r"], X0, pj["g"].v, n0=3 * NT)
            eng.wait_ge(e.ev, 2)
            eng.matmul(ps[0:1, 4, :], ident[0:1, 1:2], brow[0:1, :], start=True, stop=False)
            aggregate(1, nlo)
            eng.matmul(ps[0:1, 4, :], ident[0:1, 1:2], brow[0:1, :], start=False, stop=True).then_inc(r.tr, 1)
            eng.wait_ge(r.row, 1)
            for k in range(KC):
                ins = eng.matmul(ps[:, 5, k:k + 1], prow[:, 128 * k:128 * k + 128], ones[0:1, 0:1], start=True, stop=True)
            ins.then_inc(r.tr, 1)
            eng.wait_ge(r.in_, 32)
            eng.wait_ge(r.col, 1)
            for k in range(KC):
                ins = eng.matmul(ps[:, 5, 8:9], w1r[:, 128 * k:128 * k + 128], rt[:, 1 + k:2 + k],
                                 start=(k == 0), stop=(k == KC - 1))
            ins.then_inc(r.h, 1)
            eng.wait_ge(r.he, 1)
            eng.matmul(ps[0:1, 5, 16:24], rt[:, 5:6], w2r, start=True, stop=True).then_inc(r.l, 1)

            product_cols(pj["qk"], UNIT["qs"], X0, pj["qk"].a, n0=0, k_ready=sp["s"].lo)
            product_cols(pj["qk"], UNIT["ks"], X0, pj["qk"].a, n0=4)
            product_rows(pj["v"], UNIT["vs"], X0, pj["v"].v, n0=0 * NT)
            attend(KS_)
            product_cols(pj["u"], UNIT["us"], X1, pj["u"].v, k_ready=sp["os"].lo)
            product_cols(pj["qk"], UNIT["qc"], X0, pj["qk"].a, n0=8, k_ready=pj["u"].t,
                         last=(pj["u"].v, 4))
            product_cols(pj["qk"], UNIT["qt"], X0, pj["qk"].a, n0=12, k_ready=sp["t"].lo)
            product_cols(pj["qk"], UNIT["kt"], X0, pj["qk"].a, n0=16)
            product_rows(pj["v"], UNIT["vt"], X0, pj["v"].v, n0=1 * NT)
            attend(KT_)
            product_cols(pj["u"], UNIT["ut"], X1, pj["u"].v, n0=4, k_ready=sp["ot"].lo)
            product_cols(pj["qk"], UNIT["kc"], X0, pj["qk"].a, n0=20, k_ready=pj["u"].t, k0=4,
                         last=(pj["u"].v, 8))
            product_rows(pj["v"], UNIT["vc"], X0, pj["v"].v, n0=2 * NT)
            attend(KC_)
            for i in range(NT + 2):
                if i < NT:
                    product_tile(pj["uc"], i, UNIT["uc"], X1, pj["uc"].v, ready=sp["oc"].lo)
                if i >= 2:
                    j = i - 2
                    eng.wait_ge(ln3.nrm, j + 1)
                    eng.wait_ge(ln3.ev, j + 1)
                    for k in range(KC):
                        ins = eng.transpose(ps[:, 4 + j % 2, P * k:P * k + P], TB[0:P, j % 2, 128 * k:128 * k + 128],
                                            ident[0:P, 0:P])
                    ins.then_inc(ln3.tr, 1)

            def mlp(q):
                u = 8 * q + UNIT["mlp"]
                if isinstance(q, int):
                    eng.wait_ge(sp["m"].lo, NT)
                product_cols(pj["m1"], u, X0, pj["m1"].a, n0=4 * q)
                for i in range(NT):
                    product_tile(pj["m2"], i, u + 4, X1, pj["m2"].v, n0=NT * q, ready=pj["m1"].t, k0=4 * q)
            mlp(0)
            with eng.Fori(1, NQ) as q:
                mlp(q)

        @block.scalar
        def _(eng):
            eng.wait_ge(const_ok, 5)

            def deviation(L, b, n):
                eng.wait_ge(L.var, n + 1)
                eng.activation(sd[0:P, b, 0:1], mv[0:P, b, 1:2], ACT.Sqrt, bias=eps_t[0:P, :]).then_inc(L.std, 1)

            def cols_out(L, b, i, func=ACT.Copy):
                eng.wait_ge(L.tr, i + 3)
                eng.activation(ZT[:, :, ds(i * P, P)],
                               ps[:, 6 + b, 0:KC * P].rearrange("p (k t) -> p k t", k=KC), func).then_inc(L.ev, 1)

            def cut_hi(S, get, X, affine):
                for k in range(KC):
                    if affine:
                        eng.wait_ge(S.val, k + 1)
                    eng.activation(X[0][:, k, :], get(k), ACT.Copy).then_inc(S.hi, 1)

            def bias_cols(J, unit, dst_, bias, scale, n0=0):
                for m in range(4):
                    eng.wait_ge(w_used, unit + m + 1)
                    eng.activation(dst_[:, m, :], flat(m % 2)[:, 0:T], ACT.Identity, bias=bias[:, m:m + 1],
                                   scale=scale).then_inc(J.a, 1)

            def attend(K):
                eng.sem_inc(A.exp, K.total_parts)
                eng.sem_inc(A.hi, K.total)
                eng.sem_inc(A.bot, 2 * HG)

                def exponentials(hp, n, between=None):
                    eng.wait_ge(A.negmax, K.tile(hp, n))
                    eng.wait_ge(A.tr, K.bank(hp, n - 2, K.banks[(n - 2) % (2 * NT)] - 1))
                    w = K.cols[n % (2 * NT)]
                    for p, (lo, hi) in enumerate(((0, min(w, BANK)), (BANK, w))[:K.parts[n % (2 * NT)]]):
                        eng.activation(PB[0:P, n % 2, lo:hi], flat(n % 2)[0:P, lo:hi], ACT.Exp,
                                       bias=ngm[0:P, n % 2:n % 2 + 1], accum_out=rs[0:P, p, n % 4:n % 4 + 1]
                                       ).then_inc(A.exp, 1)
                        if p == 0 and between is not None:
                            bottom(hp, between)

                def probs_hi(hp, n):
                    g = n // 2
                    eng.wait_ge(A.pv, K.group(hp, g - 2))
                    for bank in range(K.banks[n]):
                        nb = min(4, K.blocks[n] - 4 * bank)
                        eng.wait_ge(A.tr, K.bank(hp, n, bank))
                        eng.activation(PT[0][:, g % 2, 4 * bank:4 * bank + nb, n % 2, 0:P],
                                       ps[0:P, 3 * (n % 2) + bank, 0:P * nb].rearrange("p (c t) -> p c t", c=nb),
                                       ACT.Copy).then_inc(A.hi, 1)

                def bottom(hp, g):
                    eng.wait_ge(A.pv, K.group(hp, g))
                    eng.wait_ge(A.post, K.group(hp, g - 1))
                    eng.activation(comb, ps[64:128, 6, 0:252], ACT.Copy).then_inc(A.bot, 1)

                def body(hp, first=False, last=False):
                    for n in range(2 * NT):
                        probs_hi(hp, n)
                        g = n // 2 - 1 if n % 2 == 1 and (n >= 3 or not first) else None
                        if not (last and n == 2 * NT - 1):
                            exponentials(hp, n + 1, g)
                        elif g is not None:
                            bottom(hp, g)
                    if last:
                        bottom(hp, 2 * HG - 1)
                exponentials(0, 0)
                body(0, first=True)
                with eng.Fori(1, H // 2 - 1) as hp:
                    body(hp)
                body(H // 2 - 1, last=True)

            eng.wait_ge(e.tr, 1)
            for bank, t in ((4, loT), (5, keyT)):
                eng.activation(t[:, 0:EC].rearrange("p (q j) -> p j q", j=EJ),
                               ps[0:P, bank, 0:EC].rearrange("p (j q) -> p j q", j=EJ), ACT.Copy).then_inc(e.ev, 1)
            for i in range(NT + 1):
                if i < NT:
                    deviation(ln0, i % 2, i)
                if i:
                    cols_out(ln0, (i - 1) % 2, i - 1)
            eng.wait_ge(ln0.ev, NT + 2)
            cut_hi(sp["x"], lambda k: ZT[:, k, :], X0, False)
            def rows_hi(J, n0, first_i=0, end_i=NT):
                for i in range(first_i, end_i):
                    eng.wait_ge(J.ps, n0 + i + 1)
                    eng.activation(Y[0][0:P, i, :], ps[0:P, 6 + i % 2, :], ACT.Copy).then_inc(J.a, 1)

            def aggregate(layer):
                A, L = ag[layer], (ln1, ln2)[layer]

                def stage(i):
                    for h in range(2):
                        eng.wait_ge(A.pe, 2 * i + h + 1)
                        eng.activation(AS[0][h], AT[0:P, 5 * h:5 * h + 5, ds(i * P, P)], ACT.Copy).then_inc(A.hi, 1)

                def finish(i, b):
                    cols_out(L, b, i, ACT.Copy if layer else ACT.Relu)

                def deviations(i, b):
                    if layer:
                        deviation(L, b, 2 * i)
                        deviation(L, b, 2 * i + 1)

                stage(0)
                stage(1)
                deviations(0, 0)
                with eng.Fori(0, NT // 2 - 1) as i2:
                    stage(2 * i2 + 2)
                    finish(2 * i2, 0)
                    deviations(2 * i2 + 1, 1)
                    stage(2 * i2 + 3)
                    finish(2 * i2 + 1, 1)
                    deviations(2 * i2 + 2, 0)
                finish(NT - 2, 0)
                deviations(NT - 1, 1)
                finish(NT - 1, 1)

            pair = eng.alloc_register("pair")
            eng.reg_mov(pair, 0)

            def one_hots(w):
                first, end = groups_of(eng, w)
                with eng.Fori(first, end) as c:
                    now = eng.snap(pair)
                    slot = eng.snap(now & (RING - 1))
                    eng.wait_ge(oh_used, now + 1)
                    for g in range(EA):
                        ins = eng.activation(sq_lo[:, ds(slot, 1), g, :].rearrange("p a c -> p (a c)"),
                                             iota_b[:, 0:128], ACT.Square, bias=loT[:, ds(c * EG + g, 1)])
                    ins.then_inc(lo_sq, 1)
                    eng.wait_ge(lo_sq, now + 1)
                    eng.activation(oh_lo[:, ds(slot, 1), 0:EA, :].rearrange("p a g c -> p (a g c)"),
                                   sq_lo[:, ds(slot, 1), 0:EA, :].rearrange("p a g c -> p (a g c)"), ACT.Relu,
                                   bias=ones[0:P, 0:1], scale=-1.0).then_inc(lo_ready, 1)
                    eng.reg_add(pair, pair, 1)

            def window_out(w, j):
                eng.wait_ge(at_ready, w + 1)
                eng.activation(AT[0:P, :, ds(w * WD, WD)],
                               ps[0:P, j, 0:WK].rearrange("p (d h) -> p h d", h=NT), ACT.Copy).then_inc(at_free, 1)

            eng.wait_ge(e.win, 32)
            one_hots(0)
            for seg in range(SEG):
                w0, pairs = NW // SEG * seg, NW // SEG // 2 - (seg == SEG - 1)
                with eng.Fori(0, pairs) as w2:
                    for j in range(2):
                        one_hots(2 * w2 + (w0 + j + 1))
                        window_out(2 * w2 + (w0 + j), j)
                if seg == SEG - 1:
                    one_hots(NW - 1)
                    window_out(NW - 2, 0)
                    window_out(NW - 1, 1)
                rows_hi(pj["g"], 0, NT // SEG * seg, NT // SEG * (seg + 1))
            aggregate(0)
            eng.wait_ge(ln1.ev, NT + 2)
            cut_hi(sp["h"], lambda k: ZT[:, k, :], X0, False)
            rows_hi(pj["g"], 2 * NT)
            aggregate(1)
            eng.wait_ge(r.tr, 1)
            eng.wait_ge(x1_st, 16 * NT)
            eng.activation(prow, ps[0:1, 4, :], ACT.Copy, scale=1.0 / T).then_inc(r.row, 1)
            eng.wait_ge(r.tr, 2)
            eng.activation(rt[:, 1:5], ps[:, 5, 0:4], ACT.Copy).then_inc(r.col, 1)
            eng.wait_ge(small_in, 64)
            eng.wait_ge(r.h, 1)
            eng.activation(rt[:, 5:6], ps[:, 5, 8:9], ACT.Gelu, bias=rt[:, 0:1]).then_inc(r.he, 1)

            cut_hi(sp["s"], lambda k: PB[:, k % 2, :], X0, True)
            eng.wait_ge(biasq, 1)
            bias_cols(pj["qk"], UNIT["qs"], QK[:, 0], bcol_q, SCALE)
            bias_cols(pj["qk"], UNIT["ks"], QK[:, 1], bcol[:, 4:8], 1.0)
            attend(KS_)

            def cut_out(S, K):
                eng.wait_ge(A.post, K.group(H // 2 - 1, 2 * HG - 1))
                cut_hi(S, lambda k: ZT[:, k, :], X1, False)

            def out_hi(J, n0):
                for m in range(4):
                    eng.wait_ge(J.v, n0 + m + 1)
                    eng.activation(X0[0][:, m, :], PB[:, m % 2, :], ACT.Copy).then_inc(J.a, 1)
            cut_out(sp["os"], KS_)
            out_hi(pj["u"], 0)
            eng.wait_ge(biasq, 2)
            bias_cols(pj["qk"], UNIT["qc"], QK[:, 0], bcol_q, SCALE)
            cut_hi(sp["t"], lambda k: PB[:, k % 2, :], X0, True)
            eng.wait_ge(biasq, 3)
            eng.wait_ge(qc_st, 16 * 4)
            bias_cols(pj["qk"], UNIT["qt"], QK[:, 0], bcol_q, SCALE)
            bias_cols(pj["qk"], UNIT["kt"], QK[:, 1], bcol[:, 4:8], 1.0)
            attend(KT_)
            cut_out(sp["ot"], KT_)
            out_hi(pj["u"], 4)
            eng.wait_ge(bcol_in[3], 16)
            bias_cols(pj["qk"], UNIT["kc"], QK[:, 1], bcol[:, 4:8], 1.0)
            attend(KC_)
            cut_out(sp["oc"], KC_)
            for i in range(NT + 2):
                if i < NT:
                    eng.wait_ge(ln3.var, i + 1)
                    eng.activation(sd[0:P, i % 2, 0:1], mv[0:P, i % 2, 1:2], ACT.Sqrt, bias=eps_t[0:P, :]
                                   ).then_inc(ln3.std, 1)
                if i >= 2:
                    j = i - 2
                    eng.wait_ge(ln3.tr, j + 3)
                    for k in range(KC):
                        ins = eng.activation(ZT[:, k, P * j:P * j + P], ps[:, 4 + j % 2, P * k:P * k + P],
                                             ACT.Identity, bias=lncol[:, 5, k:k + 1], scale=lncol[:, 4, k:k + 1])
                    ins.then_inc(ln3.ev, 1)

            def mlp(q):
                for m in range(4):
                    eng.wait_ge(w_used, 8 * q + (UNIT["mlp"] + m + 1))
                    if not isinstance(q, int) or 4 * q + m >= 2:
                        eng.wait_ge(pj["m1"].t, 4 * q + m - 1)
                    b1 = b1col[:, m:m + 1] if isinstance(q, int) else b1col[:, ds(4 * q + m, 1)]
                    eng.activation(PB[:, m % 2, :], flat(m % 2)[:, 0:T], ACT.Gelu, bias=b1).then_inc(pj["m1"].a, 1)
            mlp(0)
            with eng.Fori(1, NQ) as q:
                mlp(q)

        @block.vector
        def _(eng):
            for s, n in ((ln0.tr, 2), (ln0.ev, 2), (ln1.tr, 2), (ln1.ev, 2), (ln2.tr, 2), (ln2.ev, 2), (ln3.tr, 2),
                         (ln3.ev, 2), (at_free, 2), (ag[0].pe, 2), (ag[0].dv, 2), (ag[1].pe, 2), (ag[1].dv, 2),
                         (oh_used, RING)):
                eng.sem_inc(s, n)

            link = Chain(eng, e.lk)
            eng.wait_ge(e.in_, 32)
            eng.tensor_copy(s_f, s_i).then_inc(e.lk, 1)
            eng.tensor_copy(d_f, d_i).then_inc(e.lk, 1)
            link.n = 2
            eng.wait_ge(e.lk, 2)
            link(eng.tensor_scalar(h_f, s_f, float(P), None, ALU.is_ge))
            for j in range(2, NT):
                link(eng.scalar_tensor_tensor(out=h_f, in0=s_f, scalar=float(P * j), in1=h_f, op0=ALU.is_ge, op1=ALU.add))
            link(eng.scalar_tensor_tensor(out=l_f, in0=h_f, scalar=float(P), in1=s_f, op0=ALU.mult, op1=ALU.subtract))
            eng.scalar_tensor_tensor(out=k_f, in0=d_f, scalar=float(NT), in1=h_f, op0=ALU.mult, op1=ALU.add
                                     ).then_inc(e.mm, 1)
            d3 = d_f.rearrange("q (j p) -> q j p", j=EJ)
            link(eng.tensor_reduce(out=mm2[:, 0:3], in_=d3, op=ALU.min, axis=AX.X))
            eng.tensor_reduce(out=mm2[:, 3:6], in_=d3, op=ALU.max, axis=AX.X).then_inc(e.mm, 1)

            def stat(L, b, source, c):
                eng.sem_inc(held, 1)
                c(eng.bn_stats(stats[0:P, b, :], source))
                eng.sem_inc(held, 1)
                eng.bn_aggr(mv[0:P, b, :], stats[0:P, b, :]).then_inc(L.var, 1)

            c = Chain(eng, ln0.lk)
            for i in range(NT + 1):
                if i < NT:
                    for n, (lo, hi) in enumerate(X_LOADS):
                        if i == lo:
                            eng.wait_ge(x_in[n], 16)
                    stat(ln0, i % 2, XA[0:P, i, :], c)
                if i:
                    b = (i - 1) % 2
                    eng.wait_ge(ln0.std, i)
                    c(eng.reciprocal(sd[0:P, b, 1:2], sd[0:P, b, 0:1]))
                    eng.tensor_scalar(XA[0:P, i - 1, :], XA[0:P, i - 1, :], mv[0:P, b, 0:1], sd[0:P, b, 1:2],
                                      ALU.subtract, ALU.mult).then_inc(ln0.nrm, 1)

            eng.wait_ge(const_ok, 14)
            eng.wait_ge(e.mmi, 16)
            link(eng.tensor_scalar(wcol[:, 1:2], wcol[:, 0:1], float(WD - 1), None, ALU.add))
            link(eng.tensor_scalar(msk, dbc[:, EC:2 * EC], wcol[:, 0:1], None, ALU.is_ge))
            link(eng.scalar_tensor_tensor(out=msk, in0=dbc[:, 0:EC], scalar=wcol[:, 1:2], in1=msk,
                                          op0=ALU.is_le, op1=ALU.mult))
            link(eng.scalar_tensor_tensor(out=dbc[:, 0:EC], in0=cid[:, 0:EC], scalar=1.0, in1=msk, op0=ALU.add, op1=ALU.mult))
            link(eng.tensor_reduce(out=wcol[:, 2:3], in_=dbc[:, 0:EC], op=ALU.max, axis=AX.X))
            link(eng.scalar_tensor_tensor(out=dbc[:, 0:EC], in0=msk, scalar=-1000.0, in1=cid[:, 0:EC], op0=ALU.mult, op1=ALU.add))
            link(eng.tensor_reduce(out=wcol[:, 4:5], in_=dbc[:, 0:EC], op=ALU.min, axis=AX.X))
            link(eng.tensor_scalar(wcol[:, 3:4], wcol[:, 2:3], 1.0, None, ALU.max))
            link(eng.tensor_scalar(wcol[:, 5:6], wcol[:, 3:4], -1.0, None, ALU.add))
            link(eng.tensor_scalar(wcol[:, 1:2], wcol[:, 4:5], 1000.0, wcol[:, 5:6], ALU.add, ALU.min))
            eng.tensor_tensor(wcol[:, 6:7], wcol[:, 3:4], wcol[:, 1:2], ALU.subtract).then_inc(e.w, 1)
            eng.scalar_tensor_tensor(out=wcol[:, 7:8].bitcast(I32), in0=wcol[:, 1:2], scalar=128.0, in1=wcol[:, 3:4],
                                     op0=ALU.mult, op1=ALU.add).then_inc(e.w, 1)

            def cut_lo(S, get, X):
                for k in range(KC):
                    eng.wait_ge(S.hi, k + 1)
                    eng.tensor_tensor(X[1][:, k, :], get(k), X[0][:, k, :].bitcast(F32), ALU.subtract).then_inc(S.lo, 1)

            def cut_affine(S, w, b, X, stored=False):
                for k in range(KC):
                    if k >= 2 and stored:
                        eng.wait_ge((S.st0, S.st1)[k % 2], 16)
                    if k >= 2:
                        eng.wait_ge(S.lo, k - 1)
                    eng.tensor_scalar(PB[:, k % 2, :], ZT[:, k, :], lncol[:, w, k:k + 1], lncol[:, b, k:k + 1],
                                      ALU.mult, ALU.add).then_inc(S.val, 1)
                    if k:
                        lo_affine(S, X, k - 1)
                lo_affine(S, X, KC - 1)

            def lo_affine(S, X, k):
                eng.wait_ge(S.hi, k + 1)
                eng.tensor_tensor(X[1][:, k, :], PB[:, k % 2, :], X[0][:, k, :].bitcast(F32), ALU.subtract
                                  ).then_inc(S.lo, 1)

            eng.wait_ge(ln0.ev, NT + 2)
            cut_lo(sp["x"], lambda k: ZT[:, k, :], X0)

            eng.wait_ge(e.win, 32)
            eng.wait_ge(e.ev, 2)
            def rows_lo(J, a0, first_i=0, end_i=NT):
                for i in range(first_i, end_i):
                    eng.wait_ge(J.a, a0 + i + 1)
                    eng.tensor_tensor(Y[1][0:P, i, :], ps[0:P, 6 + i % 2, :], Y[0][0:P, i, :].bitcast(F32), ALU.subtract
                                      ).then_inc(J.v, 1)

            def rows_bias(J, dst_, n0, row):
                eng.wait_ge(row_in, 16 * row)
                for i in range(NT):
                    eng.wait_ge(J.ps, n0 + i + 1)
                    eng.tensor_tensor(dst_[0:P, i, :], ps[0:P, 6 + i % 2, :], brow[0:P, :], ALU.add).then_inc(J.v, 1)
                eng.wait_ge(J.v, n0 + NT)
                eng.sem_inc(row_free, 1)

            def aggregate(layer, nlo):
                A, L = ag[layer], (ln1, ln2)[layer]

                def stage_lo(i):
                    with eng.If(nlo > 0):
                        for h in range(2):
                            eng.wait_ge(A.hi, 2 * i + h + 1)
                            eng.tensor_tensor(AS[1][h], AT[0:P, 5 * h:5 * h + 5, ds(i * P, P)], AS[0][h].bitcast(F32),
                                              ALU.subtract).then_inc(A.lo, 1)

                def finish(i, b):
                    c = Chain(eng, L.lk, (8 if layer else 2) * i)
                    rc = rcnt[0:P, ds(i, 1), :].rearrange("p a c -> p (a c)")
                    rw = RW[0:P, ds(i, 1), :].rearrange("p a f -> p (a f)")
                    eng.wait_ge(A.pe, 2 * i + 4)
                    if layer == 0:
                        c(eng.tensor_scalar(cntm[0:P, b:b + 1], ps[0:P, 2 + b, 0:1], 1.0, None, ALU.max))
                        c(eng.reciprocal(rc, cntm[0:P, b:b + 1]))
                        eng.wait_ge(L.tr, i + 1)
                        eng.scalar_tensor_tensor(out=TB[0:P, b, :], in0=ps[0:P, b, :], scalar=rc, in1=rw,
                                                 op0=ALU.mult, op1=ALU.add).then_inc(L.nrm, 1)
                        eng.wait_ge(L.nrm, i + 1)
                        eng.sem_inc(A.dv, 1)
                        return
                    c(eng.scalar_tensor_tensor(out=rw, in0=ps[0:P, b, :], scalar=rc, in1=rw, op0=ALU.mult, op1=ALU.add))
                    eng.sem_inc(A.dv, 1)
                    eng.wait_ge((L.src0, L.src1)[b], (i - b) * 8 + 16)
                    c(eng.tensor_tensor(rw, rw, TB[0:P, b, :], ALU.add))
                    stat(L, b, rw, c)
                    eng.wait_ge(L.std, 2 * i + 1)
                    c(eng.reciprocal(sd[0:P, b, 1:2], sd[0:P, b, 0:1]))
                    m1 = mr1[0:P, ds(i, 1), :].rearrange("p a c -> p (a c)")
                    eng.tensor_copy(m1[:, 0:1], mv[0:P, b, 0:1]).then_inc(L.lk, 1)
                    eng.tensor_copy(m1[:, 1:2], sd[0:P, b, 1:2]).then_inc(L.lk, 1)
                    eng.tensor_scalar(TB[0:P, b, :], rw, mv[0:P, b, 0:1], sd[0:P, b, 1:2],
                                      ALU.subtract, ALU.mult).then_inc(ysum, 1)
                    c.n += 2
                    eng.wait_ge(ysum, i + 1)
                    stat(L, b, TB[0:P, b, :], c)
                    eng.wait_ge(L.std, 2 * i + 2)
                    c(eng.reciprocal(sd[0:P, b, 1:2], sd[0:P, b, 0:1]))
                    eng.wait_ge(L.tr, i + 2)
                    eng.tensor_scalar(TB[0:P, 2, :], TB[0:P, b, :], mv[0:P, b, 0:1], sd[0:P, b, 1:2],
                                      ALU.subtract, ALU.mult).then_inc(L.nrm, 1)

                stage_lo(0)
                with eng.Fori(0, NT // 2 - 1) as i2:
                    for b in range(2):
                        stage_lo(2 * i2 + b + 1)
                        finish(2 * i2 + b, b)
                stage_lo(NT - 1)
                finish(NT - 2, 0)
                finish(NT - 1, 1)

            eng.wait_ge(e.win, 32)
            link(eng.tensor_reduce(out=wide[:, NW:NW + 1], in_=wide[:, 0:NW], op=ALU.max, axis=AX.X))
            eng.tensor_scalar(many[:, :], wide[:, NW:NW + 1], float(4096 // (P * EG)), None, ALU.is_gt
                              ).then_inc(e.many, 1)

            eng.wait_ge(e.many, 1)
            nlo = eng.value_load(many[0:1, 0:1], min_val=0, max_val=1)

            pair = eng.alloc_register("pair")
            eng.reg_mov(pair, 0)
            for seg in range(SEG):
                with eng.Fori(NW // SEG * seg, NW // SEG * (seg + 1)) as w:
                    first, end = groups_of(eng, w)
                    with eng.Fori(first, end) as c:
                        now = eng.snap(pair)
                        slot = eng.snap(now & (RING - 1))
                        eng.wait_ge(oh_used, now + 1)
                        eng.scalar_tensor_tensor(out=oh_lo[:, ds(slot, 1), EA:EG, :].rearrange("p a g c -> p (a g) c"),
                                                 in0=iota_b[:, 0:128].unsqueeze(1).to_broadcast([P, EG - EA, 128]),
                                                 scalar=-1.0,
                                                 in1=loT[:, ds(c * EG + EA, EG - EA)].unsqueeze(2)
                                                 .to_broadcast([P, EG - EA, 128]),
                                                 op0=ALU.mult, op1=ALU.is_equal)
                        eng.scalar_tensor_tensor(out=oh_key[:, ds(slot, 1), :, :].rearrange("p a g c -> p (a g) c"),
                                                 in0=iota_b[:, 0:WK].unsqueeze(1).to_broadcast([P, EG, WK]),
                                                 scalar=woff[:, ds(w, 1)],
                                                 in1=keyT[:, ds(c * EG, EG)].unsqueeze(2).to_broadcast([P, EG, WK]),
                                                 op0=ALU.add, op1=ALU.is_equal).then_inc(key_ready, 1)
                        eng.reg_add(pair, pair, 1)
                if seg:
                    rows_lo(pj["g"], 0, NT // SEG * (seg - 1), NT // SEG * seg)
            rows_lo(pj["g"], 0, NT - NT // SEG, NT)
            rows_bias(pj["g"], RW, NT, 1)
            aggregate(0, nlo)
            eng.wait_ge(ln1.ev, NT + 2)
            cut_lo(sp["h"], lambda k: ZT[:, k, :], X0)
            rows_lo(pj["g"], NT)
            rows_bias(pj["g"], RW, 3 * NT, 2)
            aggregate(1, nlo)

            eng.wait_ge(r.l, 1)
            link = Chain(eng, r.lk)
            link(eng.tensor_tensor(rt[0:1, 24:32], ps[0:1, 5, 16:24], rt[0:1, 8:16], ALU.add))
            for j in range(2):
                lg = rt[0:1, 24 + 4 * j:28 + 4 * j]
                link(eng.tensor_reduce(out=rt[0:1, 32:33], in_=lg, op=ALU.max, axis=AX.X))
                link(eng.scalar_tensor_tensor(out=rt[0:1, 36:40], in0=lg, scalar=rt[0:1, 32:33], in1=rt[0:1, 16:20],
                                              op0=ALU.is_equal, op1=ALU.mult))
                link(eng.tensor_reduce(out=rt[0:1, 33:34], in_=rt[0:1, 36:40], op=ALU.max, axis=AX.X))
                eng.tensor_scalar(idx_i[0:1, j:j + 1], rt[0:1, 33:34], -1.0, 4.0, ALU.mult, ALU.add).then_inc(r.i, 1)

            def scaled_bias(n, came):
                eng.wait_ge(came, 16)
                eng.tensor_scalar(bcol_q[:], bcol[:, 0:4], SCALE, None, ALU.mult).then_inc(biasq, 1)

            def attend(K):
                eng.sem_inc(A.negmax, 2 * NT)
                eng.sem_inc(A.lo, K.total)
                eng.sem_inc(A.tr, K.total)
                eng.sem_inc(A.pv, 2 * HG)
                eng.sem_inc(A.diag, 2 * HG)
                eng.sem_inc(A.bc, 2 * HG)
                eng.sem_inc(A.post, 2 * HG)
                if K.causal:
                    eng.wait_ge(mask_ok, 2)

                def greatest(c, n):
                    eng.wait_ge(A.scores, K.tile(c.hp, n))
                    i = n % NT
                    if K.causal:
                        block_ = flat(n % 2)[0:P, P * i:P * i + P]
                        c(eng.tensor_tensor(block_, block_, mask, ALU.add))
                    eng.tensor_reduce(out=ngm[0:P, n % 2:n % 2 + 1], in_=flat(n % 2)[0:P, 0:K.cols[i]], op=ALU.max,
                                      axis=AX.X, negate=True).then_inc(A.negmax, 1)

                def probs_lo(hp, n):
                    g = n // 2
                    for bank in range(K.banks[n]):
                        nb = min(4, K.blocks[n] - 4 * bank)
                        blk = (slice(None), g % 2, slice(4 * bank, 4 * bank + nb), n % 2, slice(0, P))
                        eng.wait_ge(A.hi, K.bank(hp, n, bank))
                        eng.tensor_tensor(PT[1][blk],
                                          ps[0:P, 3 * (n % 2) + bank, 0:P * nb].rearrange("p (c t) -> p c t", c=nb),
                                          PT[0][blk].bitcast(F32), ALU.subtract).then_inc(A.lo, 1)

                def inverse(c, hp, g):
                    eng.wait_ge(A.exp, K.part(hp, 2 * g + 1, K.parts[2 * g + 1] - 1))
                    k = 2 * g % 4
                    if K.parts[2 * g + 1] == 2:
                        c(eng.tensor_tensor(rs[0:P, 0, k:k + 2], rs[0:P, 0, k:k + 2], rs[0:P, 1, k:k + 2], ALU.add))
                    c(eng.reciprocal(rr[0:P, :], rs[0:P, 0, k:k + 2]))
                    for s in range(2):
                        ins = eng.tensor_scalar(diag[0:P, s, :], ident[0:P, 0:P], rr[0:P, s:s + 1], None, ALU.mult)
                    ins.then_inc(A.diag, 1)

                def output(c, hp, g):
                    b, gh = g // HG % 2, g % HG
                    eng.wait_ge(A.bot, K.group(hp, g))
                    c(eng.tensor_tensor(comb, ps[0:HD, 6, 0:252], comb, ALU.add))
                    eng.wait_ge(A.bc, K.group(hp, g))
                    o = ZT[64 * b:64 * b + 64, ds(hp - (g < 0), 1), 2 * P * gh:2 * P * gh + 2 * P].rearrange("p a (s t) -> p (a s) t", s=2)
                    eng.tensor_tensor(o, ps[0:HD, 7, 0:2 * P].rearrange("p (s t) -> p s t", s=2),
                                      comb.rearrange("p (s t) -> p s t", s=2)[:, :, 0:P], ALU.mult).then_inc(A.post, 1)

                def body(hp, first=False, last=False):
                    c = Chain(eng, A.lk, K.links0 + int(K.causal) + K.links * hp - (0 if first else 3))
                    c.hp = hp
                    for n in range(2 * NT):
                        if not (last and n == 2 * NT - 1):
                            greatest(c, n + 1)
                        probs_lo(hp, n)
                        if n % 2 == 0 and (n >= 2 or not first):
                            inverse(c, hp, n // 2 - 1)
                        if n % 2 == 1 and (n >= 3 or not first):
                            output(c, hp, n // 2 - 1)
                    if last:
                        inverse(c, hp, 2 * HG - 1)
                        output(c, hp, 2 * HG - 1)
                c0 = Chain(eng, A.lk, K.links0)
                c0.hp = 0
                greatest(c0, 0)
                body(0, first=True)
                with eng.Fori(1, H // 2 - 1) as hp:
                    body(hp)
                body(H // 2 - 1, last=True)

            def clear_pads():
                for p in range(2):
                    for s in range(2):
                        ins = eng.memset(PT[p][:, :, :, s, P:P + 1].rearrange("p g c t -> p g (c t)").bitcast(F32), 0.0)
                        ins.then_inc(pad_ok, 1)

            def out_val(J, unit, n0, residual=False):
                for m in range(4):
                    eng.wait_ge(w_used, unit + m + 1)
                    if residual:
                        ins = eng.scalar_tensor_tensor(out=PB[:, m % 2, :], in0=flat(m % 2)[:, 0:T],
                                                       scalar=ocol[:, m:m + 1], in1=XR[:, m, :], op0=ALU.add, op1=ALU.add)
                    else:
                        ins = eng.tensor_scalar(PB[:, m % 2, :], flat(m % 2)[:, 0:T], ocol[:, m:m + 1], None, ALU.add)
                    ins.then_inc(J.v, 1)
                    eng.wait_ge(J.a, n0 + m + 1)
                    eng.tensor_tensor(X0[1][:, m, :], PB[:, m % 2, :], X0[0][:, m, :].bitcast(F32), ALU.subtract
                                      ).then_inc(J.t, 1)

            eng.wait_ge(small_in, 64)
            eng.wait_ge(r.h, 1)
            cut_affine(sp["s"], 0, 1, X0)
            scaled_bias(1, bcol_in[0])
            rows_bias(pj["v"], V, 0 * NT, 3)
            clear_pads()
            attend(KS_)
            cut_lo(sp["os"], lambda k: ZT[:, k, :], X1)
            eng.wait_ge(ocol_in[0], 16)
            out_val(pj["u"], UNIT["us"], 0)
            scaled_bias(2, bcol_in[1])
            eng.wait_ge(zt_in, 16)
            eng.wait_ge(pj["u"].t, 4)
            cut_affine(sp["t"], 2, 3, X0, stored=True)
            scaled_bias(3, bcol_in[2])
            rows_bias(pj["v"], V, 1 * NT, 4)
            clear_pads()
            attend(KT_)
            cut_lo(sp["ot"], lambda k: ZT[:, k, :], X1)
            eng.wait_ge(ocol_in[1], 16)
            eng.wait_ge(xr_in, 16)
            out_val(pj["u"], UNIT["ut"], 4, residual=True)
            rows_bias(pj["v"], V, 2 * NT, 5)
            clear_pads()
            attend(KC_)
            cut_lo(sp["oc"], lambda k: ZT[:, k, :], X1)
            J = pj["uc"]
            c = Chain(eng, ln3.lk)

            def attended(i):
                y = YL[0:P, i, :]
                eng.wait_ge(y_ready, i + 1)
                eng.wait_ge(J.ps, i + 1)
                eng.tensor_tensor(y, ps[0:P, 6 + i % 2, :], y, ALU.add).then_inc(J.v, 1)
                eng.wait_ge(J.v, i + 1)
                c(eng.tensor_tensor(ACC[0:P, i, :], y, XL[0:P, i, :], ALU.add))
                stat(ln3, i % 2, y, c)

            def normed(i):
                b = i % 2
                eng.wait_ge(ln3.std, i + 1)
                c(eng.reciprocal(sd[0:P, b, 1:2], sd[0:P, b, 0:1]))
                eng.wait_ge(ln3.tr, i + 1)
                eng.tensor_scalar(TB[0:P, b, :], YL[0:P, i, :], mv[0:P, b, 0:1], sd[0:P, b, 1:2],
                                  ALU.subtract, ALU.mult).then_inc(ln3.nrm, 1)

            def lo_tile(i):
                tk = slice(P * i, P * i + P)
                eng.wait_ge(sp["m"].hi, i + 1)
                eng.tensor_tensor(X0[1][:, :, tk], ZT[:, :, tk], X0[0][:, :, tk].bitcast(F32), ALU.subtract
                                  ).then_inc(sp["m"].lo, 1)
            for i in range(NT + 3):
                if i < NT:
                    attended(i)
                if 1 <= i <= NT:
                    normed(i - 1)
                if i >= 3:
                    lo_tile(i - 3)
            eng.wait_ge(row_in, 16 * 7)
            for i in range(NT):
                eng.tensor_tensor(ACC[0:P, i, :], ACC[0:P, i, :], brow[0:P, :], ALU.add).then_inc(pj["m2"].a, 1)
            eng.wait_ge(pj["m2"].a, NT)

            def mlp(q):
                J1, J2 = pj["m1"], pj["m2"]
                for m in range(4):
                    eng.wait_ge(J1.a, 4 * q + m + 1)
                    if m == 0 and not isinstance(q, int):
                        eng.wait_ge(J2.ps, NT * q)
                    eng.tensor_scalar(X1[0][:, m, :], PB[:, m % 2, :], 1.0, None, ALU.mult).then_inc(J1.v, 1)
                    eng.wait_ge(J1.v, 4 * q + m + 1)
                    eng.tensor_tensor(X1[1][:, m, :], PB[:, m % 2, :], X1[0][:, m, :].bitcast(F32), ALU.subtract
                                      ).then_inc(J1.t, 1)
                for i in range(NT):
                    eng.wait_ge(J2.ps, NT * q + i + 1)
                    ins = eng.tensor_tensor(ACC[0:P, i, :], ps[0:P, 6 + i % 2, :], ACC[0:P, i, :], ALU.add)
                    ins.then_inc(J2.v, 1)
            mlp(0)
            with eng.Fori(1, NQ - 1) as q:
                mlp(q)
            J1, J2 = pj["m1"], pj["m2"]
            q = NQ - 1
            eng.wait_ge(J2.ps, NT * q)
            for m in range(4):
                eng.wait_ge(J1.a, 4 * q + m + 1)
                eng.tensor_scalar(X1[0][:, m, :], PB[:, m % 2, :], 1.0, None, ALU.mult).then_inc(J1.v, 1)
                eng.wait_ge(J1.v, 4 * q + m + 1)
                eng.tensor_tensor(X1[1][:, m, :], PB[:, m % 2, :], X1[0][:, m, :].bitcast(F32), ALU.subtract
                                  ).then_inc(J1.t, 1)
            eng.wait_ge(J2.v, NT * q)
            for i in range(NT):
                eng.wait_ge(J2.ps, NT * q + i + 1)
                eng.tensor_tensor(ACC[0:P, i, :], ps[0:P, 6 + i % 2, :], ACC[0:P, i, :], ALU.add).then_inc(fin, 1)
                eng.wait_ge(fin, i + 1)
                eng.sem_inc(J2.v, 1)


def kernel(**inputs):
    import numpy as np
    import concourse.bacc as bacc
    from concourse.bass_utils import run_bass_kernel_spmd

    a = {k: np.asarray(v) for k, v in inputs.items()}
    f = {k[7:]: v for k, v in a.items() if k.startswith("L0_ffn_")}

    def by_rows(w):
        return w.T.reshape(-1, 128, w.shape[0]).reshape(-1, 128, 512)

    def by_blocks(w):
        return w.reshape(-1, 128, KC, 128).transpose(0, 3, 2, 1).reshape(-1, 128, 512)

    def by_cols(b):
        return b.reshape(-1, 128).T

    units = [by_rows(a[n]) for n in ("L0_gnn_W1_l", "L0_gnn_W1_r", "L0_gnn_W2_l", "L0_gnn_W2_r")]
    for n in range(NEXP):
        w = f["sp_in_w"][n]
        units += [by_blocks(w[0:D]), by_blocks(w[D:2 * D]), by_rows(w[2 * D:]), by_blocks(f["sp_out_w"][n])]
    for n in range(NEXP):
        units += [by_blocks(f["tq_w"][n]), by_blocks(f["tk_w"][n]), by_rows(f["tv_w"][n]), by_blocks(f["tp_w"][n])]
    w = f["cross_in_w"]
    units += [by_blocks(w[0:D]), by_blocks(w[D:2 * D]), by_rows(w[2 * D:]), by_rows(f["cross_out_w"])]
    units += [by_blocks(f["mlp_w1"]), by_rows(f["mlp_w2"])]
    qkv = [by_cols(f["sp_in_b"][n]) for n in range(NEXP)]
    qkv += [by_cols(np.concatenate([f["tq_b"][n], f["tk_b"][n], f["tv_b"][n]])) for n in range(NEXP)]
    qkv += [by_cols(f["cross_in_b"])]
    outs = [by_cols(f["sp_out_b"][n]) for n in range(NEXP)] + [by_cols(f["tp_b"][n]) for n in range(NEXP)]
    row_bias = [a["L0_gnn_b1"], a["L0_gnn_b2"]] + [f["sp_in_b"][n][2 * D:] for n in range(NEXP)]
    row_bias += [f["tv_b"][n] for n in range(NEXP)] + [f["cross_in_b"][2 * D:], f["cross_out_b"], f["mlp_b2"]]
    data = {
        "x": a["x"].reshape(NT, P, D),
        "src": a["src"],
        "dst": a["dst"],
        "weights": np.concatenate(units),
        "qkv_bias": np.stack(qkv),
        "out_bias": np.stack(outs),
        "row_bias": np.stack(row_bias),
        "ln_cols": np.stack([by_cols(f[n]) for n in ("norm_s_w", "norm_s_b", "norm_t_w", "norm_t_b",
                                                     "norm_mlp_w", "norm_mlp_b")], axis=1),
        "mlp_b1": by_cols(f["mlp_b1"]),
        "router_w1": f["router_w1"].T.reshape(KC, 128, 128).transpose(1, 0, 2).reshape(128, D),
        "router_w2": f["router_w2"].T,
        "router_b1": f["router_b1"].reshape(128, 1),
        "router_b2": f["router_b2"].reshape(1, 2 * NEXP),
    }
    nc = bacc.Bacc("TRN2", target_bir_lowering=False, num_devices=1)
    arrays, args = {}, []
    for name, v in data.items():
        v = np.ascontiguousarray(v)
        arrays[f"in_{name}"] = v
        args.append(nc.dram_tensor(f"in_{name}", v.shape, mybir.dt.from_np(v.dtype), kind="ExternalInput").ap())
    out = nc.dram_tensor("out_x", (NT, P, D), F32, kind="ExternalOutput").ap()
    gnn_ffn_program(nc, *args, out)
    got = run_bass_kernel_spmd(nc, [arrays], core_ids=[0])
    return got.results[0]["out_x"].reshape(T, D)
```
